# Optimizing a Trainium2 kernel written in Bass

```python
import numpy as np
import jax
import jax.numpy as jnp

def _softmax(x, axis=-1):
    return jax.nn.softmax(x, axis=axis)

def _gelu(x):
    return jax.nn.gelu(x, approximate=True)

def _silu(x):
    return jax.nn.silu(x)

def _sigmoid(x):
    return jax.nn.sigmoid(x)

def _layernorm(x, axis=-1, eps=1e-05):
    m = jnp.mean(x, axis=axis, keepdims=True)
    v = jnp.var(x, axis=axis, keepdims=True)
    return (x - m) / jnp.sqrt(v + eps)

def _scatter_add(tgt, idx, src, axis=0):
    return tgt.at[idx].add(src)

def _segment_sum(src, seg, n):
    return jax.ops.segment_sum(src, seg, n)
kernel_name = 'mk_hybrid_d1_jaxref_r8_0cd0e3'

def setup_inputs(seed: int=0):
    np.random.seed(seed)
    _w = jnp.asarray

    def _L0_attn_a_setup():
        import jax, jax.numpy as jnp
        import numpy as np
        D_MODEL = 128
        N_LAYERS = 2
        N_HEADS = 16
        HEAD_DIM = D_MODEL // N_HEADS
        D_FFN = 4 * D_MODEL
        B, L = (4, 128)

        def layer_norm(x, g, b, eps=1e-05):
            mu = jnp.mean(x, axis=-1, keepdims=True)
            var = jnp.var(x, axis=-1, keepdims=True)
            return (x - mu) * jax.lax.rsqrt(var + eps) * g + b

        def make_decay(length):
            gamma = 1.0 - 2.0 ** (-5.0 - jnp.arange(N_HEADS, dtype=jnp.float32))
            n = jnp.arange(length, dtype=jnp.float32)[:, None]
            m = jnp.arange(length, dtype=jnp.float32)[None, :]
            diff = n - m
            pow_ = gamma[:, None, None] ** diff[None]
            return jnp.where(diff[None] >= 0, pow_, 0.0)

        def _forward(x, proj_w, proj_b, reto_w, reto_b, ln1_g, ln1_b, ln2_g, ln2_b, ffn1_w, ffn1_b, ffn2_w, ffn2_b, lnf_g, lnf_b):
            Bx, Lx, _ = x.shape
            D = make_decay(Lx)
            for i in range(N_LAYERS):
                ln_x = layer_norm(x, ln1_g[i], ln1_b[i])
                p = ln_x @ proj_w[i] + proj_b[i]
                q, k, v, xo = jnp.split(p, 4, axis=-1)
                q = q.reshape(Bx, Lx, N_HEADS, HEAD_DIM).transpose(0, 2, 1, 3)
                k = k.reshape(Bx, Lx, N_HEADS, HEAD_DIM).transpose(0, 2, 1, 3)
                v = v.reshape(Bx, Lx, N_HEADS, HEAD_DIM).transpose(0, 2, 1, 3)
                scores = jnp.einsum('bhld,bhmd->bhlm', q, k) * D[None]
                ret = jnp.einsum('bhlm,bhmd->bhld', scores, v)
                ret = ret.transpose(0, 2, 1, 3).reshape(Bx, Lx, D_MODEL)
                ret = ret * jax.nn.silu(xo)
                ret = ret @ reto_w[i] + reto_b[i]
                x = x + ret
                h = layer_norm(x, ln2_g[i], ln2_b[i])
                h = jax.nn.gelu(h @ ffn1_w[i] + ffn1_b[i], approximate=False) @ ffn2_w[i] + ffn2_b[i]
                x = x + h
            return layer_norm(x, lnf_g, lnf_b)
        key = jax.random.key(seed)
        ks = jax.random.split(key, 16)
        s = 0.02
        inp = {'x': jax.random.normal(ks[0], (B, L, D_MODEL), jnp.float32), 'proj_w': jax.random.normal(ks[1], (N_LAYERS, D_MODEL, 4 * D_MODEL), jnp.float32) * s, 'proj_b': jnp.zeros((N_LAYERS, 4 * D_MODEL), jnp.float32), 'reto_w': jax.random.normal(ks[2], (N_LAYERS, D_MODEL, D_MODEL), jnp.float32) * s, 'reto_b': jnp.zeros((N_LAYERS, D_MODEL), jnp.float32), 'ln1_g': jnp.ones((N_LAYERS, D_MODEL), jnp.float32), 'ln1_b': jnp.zeros((N_LAYERS, D_MODEL), jnp.float32), 'ln2_g': jnp.ones((N_LAYERS, D_MODEL), jnp.float32), 'ln2_b': jnp.zeros((N_LAYERS, D_MODEL), jnp.float32), 'ffn1_w': jax.random.normal(ks[3], (N_LAYERS, D_MODEL, D_FFN), jnp.float32) * s, 'ffn1_b': jnp.zeros((N_LAYERS, D_FFN), jnp.float32), 'ffn2_w': jax.random.normal(ks[4], (N_LAYERS, D_FFN, D_MODEL), jnp.float32) * s, 'ffn2_b': jnp.zeros((N_LAYERS, D_MODEL), jnp.float32), 'lnf_g': jnp.ones((D_MODEL,), jnp.float32), 'lnf_b': jnp.zeros((D_MODEL,), jnp.float32)}
        return inp
    _L0_attn_a_in = _L0_attn_a_setup()

    def _L0_attn_b_setup():
        import jax, jax.numpy as jnp
        import numpy as np
        N_EMBD = 128
        N_HEAD = 16
        HEAD_SIZE = N_EMBD // N_HEAD
        B, T = (4, 256)
        key = jax.random.key(seed)
        ks = jax.random.split(key, 6)
        s = 1.0 / np.sqrt(N_EMBD)
        x = jax.random.normal(ks[0], (B, T, N_EMBD), dtype=jnp.float32)
        Wq = jax.random.uniform(ks[1], (N_HEAD, N_EMBD, HEAD_SIZE), minval=-s, maxval=s, dtype=jnp.float32)
        Wk = jax.random.uniform(ks[2], (N_HEAD, N_EMBD, HEAD_SIZE), minval=-s, maxval=s, dtype=jnp.float32)
        Wv = jax.random.uniform(ks[3], (N_HEAD, N_EMBD, HEAD_SIZE), minval=-s, maxval=s, dtype=jnp.float32)
        Wo = jax.random.uniform(ks[4], (N_EMBD, N_EMBD), minval=-s, maxval=s, dtype=jnp.float32)
        bo = jax.random.uniform(ks[5], (N_EMBD,), minval=-s, maxval=s, dtype=jnp.float32)
        return {'x': x, 'Wq': Wq, 'Wk': Wk, 'Wv': Wv, 'Wo': Wo, 'bo': bo}
    _L0_attn_b_in = _L0_attn_b_setup()

    def _L0_ffn_setup():
        import jax, jax.numpy as jnp
        import numpy as np
        TOP_K = 2
        key = jax.random.key(seed)
        ks = jax.random.split(key, 5)
        B, T, D, F, E = (4, 256, 128, 512, 8)
        s = 0.02
        return {'x': jax.random.normal(ks[0], (B, T, D), jnp.float32), 'gate_w': jax.random.normal(ks[1], (D, E), jnp.float32) * s, 'w1': jax.random.normal(ks[2], (E, D, F), jnp.float32) * s, 'w3': jax.random.normal(ks[3], (E, D, F), jnp.float32) * s, 'w2': jax.random.normal(ks[4], (E, F, D), jnp.float32) * s}
    _L0_ffn_in = _L0_ffn_setup()
    _d = {'L0_attn_a_x': _L0_attn_a_in['x'], 'L0_attn_a_proj_w': _L0_attn_a_in['proj_w'], 'L0_attn_a_proj_b': _L0_attn_a_in['proj_b'], 'L0_attn_a_reto_w': _L0_attn_a_in['reto_w'], 'L0_attn_a_reto_b': _L0_attn_a_in['reto_b'], 'L0_attn_a_ln1_g': _L0_attn_a_in['ln1_g'], 'L0_attn_a_ln1_b': _L0_attn_a_in['ln1_b'], 'L0_attn_a_ln2_g': _L0_attn_a_in['ln2_g'], 'L0_attn_a_ln2_b': _L0_attn_a_in['ln2_b'], 'L0_attn_a_ffn1_w': _L0_attn_a_in['ffn1_w'], 'L0_attn_a_ffn1_b': _L0_attn_a_in['ffn1_b'], 'L0_attn_a_ffn2_w': _L0_attn_a_in['ffn2_w'], 'L0_attn_a_ffn2_b': _L0_attn_a_in['ffn2_b'], 'L0_attn_a_lnf_g': _L0_attn_a_in['lnf_g'], 'L0_attn_a_lnf_b': _L0_attn_a_in['lnf_b'], 'L0_attn_b_Wq': _L0_attn_b_in['Wq'], 'L0_attn_b_Wk': _L0_attn_b_in['Wk'], 'L0_attn_b_Wv': _L0_attn_b_in['Wv'], 'L0_attn_b_Wo': _L0_attn_b_in['Wo'], 'L0_attn_b_bo': _L0_attn_b_in['bo'], 'L0_ffn_gate_w': _L0_ffn_in['gate_w'], 'L0_ffn_w1': _L0_ffn_in['w1'], 'L0_ffn_w3': _L0_ffn_in['w3'], 'L0_ffn_w2': _L0_ffn_in['w2']}
    _x0 = _d['L0_attn_a_x']
    _d['L0_attn_a_x'] = jax.random.normal(jax.random.fold_in(jax.random.key(seed), 1), (4, 512, 128), dtype=_x0.dtype)
    del _x0
    return _d

def reference(L0_attn_a_x, L0_attn_a_proj_w, L0_attn_a_proj_b, L0_attn_a_reto_w, L0_attn_a_reto_b, L0_attn_a_ln1_g, L0_attn_a_ln1_b, L0_attn_a_ln2_g, L0_attn_a_ln2_b, L0_attn_a_ffn1_w, L0_attn_a_ffn1_b, L0_attn_a_ffn2_w, L0_attn_a_ffn2_b, L0_attn_a_lnf_g, L0_attn_a_lnf_b, L0_attn_b_Wq, L0_attn_b_Wk, L0_attn_b_Wv, L0_attn_b_Wo, L0_attn_b_bo, L0_ffn_gate_w, L0_ffn_w1, L0_ffn_w3, L0_ffn_w2):

    def _L0_attn_a_ref(x, proj_w, proj_b, reto_w, reto_b, ln1_g, ln1_b, ln2_g, ln2_b, ffn1_w, ffn1_b, ffn2_w, ffn2_b, lnf_g, lnf_b):
        import jax, jax.numpy as jnp
        import numpy as np
        D_MODEL = 128
        N_LAYERS = 2
        N_HEADS = 16
        HEAD_DIM = D_MODEL // N_HEADS
        D_FFN = 4 * D_MODEL
        B, L = (4, 128)

        def layer_norm(x, g, b, eps=1e-05):
            mu = jnp.mean(x, axis=-1, keepdims=True)
            var = jnp.var(x, axis=-1, keepdims=True)
            return (x - mu) * jax.lax.rsqrt(var + eps) * g + b

        def make_decay(length):
            gamma = 1.0 - 2.0 ** (-5.0 - jnp.arange(N_HEADS, dtype=jnp.float32))
            n = jnp.arange(length, dtype=jnp.float32)[:, None]
            m = jnp.arange(length, dtype=jnp.float32)[None, :]
            diff = n - m
            pow_ = gamma[:, None, None] ** diff[None]
            return jnp.where(diff[None] >= 0, pow_, 0.0)

        def _forward(x, proj_w, proj_b, reto_w, reto_b, ln1_g, ln1_b, ln2_g, ln2_b, ffn1_w, ffn1_b, ffn2_w, ffn2_b, lnf_g, lnf_b):
            Bx, Lx, _ = x.shape
            D = make_decay(Lx)
            for i in range(N_LAYERS):
                ln_x = layer_norm(x, ln1_g[i], ln1_b[i])
                p = ln_x @ proj_w[i] + proj_b[i]
                q, k, v, xo = jnp.split(p, 4, axis=-1)
                q = q.reshape(Bx, Lx, N_HEADS, HEAD_DIM).transpose(0, 2, 1, 3)
                k = k.reshape(Bx, Lx, N_HEADS, HEAD_DIM).transpose(0, 2, 1, 3)
                v = v.reshape(Bx, Lx, N_HEADS, HEAD_DIM).transpose(0, 2, 1, 3)
                scores = jnp.einsum('bhld,bhmd->bhlm', q, k) * D[None]
                ret = jnp.einsum('bhlm,bhmd->bhld', scores, v)
                ret = ret.transpose(0, 2, 1, 3).reshape(Bx, Lx, D_MODEL)
                ret = ret * jax.nn.silu(xo)
                ret = ret @ reto_w[i] + reto_b[i]
                x = x + ret
                h = layer_norm(x, ln2_g[i], ln2_b[i])
                h = jax.nn.gelu(h @ ffn1_w[i] + ffn1_b[i], approximate=False) @ ffn2_w[i] + ffn2_b[i]
                x = x + h
            return layer_norm(x, lnf_g, lnf_b)
        return _forward(x, proj_w, proj_b, reto_w, reto_b, ln1_g, ln1_b, ln2_g, ln2_b, ffn1_w, ffn1_b, ffn2_w, ffn2_b, lnf_g, lnf_b)

    def _L0_attn_b_ref(x, Wq, Wk, Wv, Wo, bo):
        import jax, jax.numpy as jnp
        import numpy as np
        N_EMBD = 128
        N_HEAD = 16
        HEAD_SIZE = N_EMBD // N_HEAD
        B, T = (4, 256)
        q = jnp.einsum('btd,hdk->bhtk', x, Wq)
        k = jnp.einsum('btd,hdk->bhtk', x, Wk)
        v = jnp.einsum('btd,hdk->bhtk', x, Wv)
        scale = 1.0 / jnp.sqrt(jnp.asarray(HEAD_SIZE, dtype=x.dtype))
        scores = jnp.einsum('bhqk,bhsk->bhqs', q, k) * scale
        Tn = x.shape[1]
        causal = jnp.tril(jnp.ones((Tn, Tn), dtype=bool))
        scores = jnp.where(causal, scores, jnp.asarray(-jnp.inf, dtype=scores.dtype))
        weights = jax.nn.softmax(scores, axis=-1)
        out = jnp.einsum('bhqs,bhsk->bhqk', weights, v)
        out = out.transpose(0, 2, 1, 3).reshape(x.shape[0], Tn, N_EMBD)
        out = out @ Wo.T + bo
        return out

    def _L0_ffn_ref(x, gate_w, w1, w3, w2):
        import jax, jax.numpy as jnp
        import numpy as np
        TOP_K = 2
        logits = jnp.einsum('btd,de->bte', x, gate_w)
        probs = jax.nn.softmax(logits, axis=-1)
        expert_weights, expert_indices = jax.lax.top_k(probs, TOP_K)
        expert_weights = expert_weights / expert_weights.sum(-1, keepdims=True)
        E = w1.shape[0]
        out = jnp.zeros_like(x)
        for i in range(E):
            wi = jnp.where(expert_indices == i, expert_weights, 0.0).sum(-1)
            h = jax.nn.silu(jnp.einsum('btd,df->btf', x, w1[i])) * jnp.einsum('btd,df->btf', x, w3[i])
            out = out + jnp.einsum('btf,fd->btd', h, w2[i]) * wi[..., None]
        return out
    x = L0_attn_a_x
    x = x + _L0_attn_a_ref(_layernorm(x, axis=-1), L0_attn_a_proj_w, L0_attn_a_proj_b, L0_attn_a_reto_w, L0_attn_a_reto_b, L0_attn_a_ln1_g, L0_attn_a_ln1_b, L0_attn_a_ln2_g, L0_attn_a_ln2_b, L0_attn_a_ffn1_w, L0_attn_a_ffn1_b, L0_attn_a_ffn2_w, L0_attn_a_ffn2_b, L0_attn_a_lnf_g, L0_attn_a_lnf_b)
    x = x + _L0_ffn_ref(_layernorm(x, axis=-1), L0_ffn_gate_w, L0_ffn_w1, L0_ffn_w3, L0_ffn_w2)
    x = x + _L0_attn_b_ref(_layernorm(x, axis=-1), L0_attn_b_Wq, L0_attn_b_Wk, L0_attn_b_Wv, L0_attn_b_Wo, L0_attn_b_bo)
    x = x + _L0_ffn_ref(_layernorm(x, axis=-1), L0_ffn_gate_w, L0_ffn_w1, L0_ffn_w3, L0_ffn_w2)
    return x

_drawn_inputs = setup_inputs


def setup_inputs(seed=0):
    import zlib

    import numpy as np

    out = dict(_drawn_inputs(seed))
    spreads = {'L0_attn_a_proj_b': (0.0, 0.1),
     'L0_attn_a_reto_b': (0.0, 0.1),
     'L0_attn_a_ln1_g': (1.0, 0.6),
     'L0_attn_a_ln1_b': (0.0, 0.57),
     'L0_attn_a_ln2_g': (1.0, 0.6),
     'L0_attn_a_ln2_b': (0.0, 0.8),
     'L0_attn_a_ffn1_b': (0.0, 0.482),
     'L0_attn_a_ffn2_b': (0.0, 0.1),
     'L0_attn_a_lnf_g': (1.0, 0.2),
     'L0_attn_a_lnf_b': (0.0, 0.1)}
    factors = {'L0_attn_b_Wq': 7.901,
     'L0_attn_b_Wk': 7.793,
     'L0_ffn_gate_w': 8.0,
     'L0_ffn_w1': 7.069,
     'L0_ffn_w3': 7.038,
     'L0_ffn_w2': 7.029}
    for name, (base, spread) in spreads.items():
        noise = np.random.default_rng([zlib.crc32(name.encode()), seed]).standard_normal(out[name].shape)
        drawn = base * np.exp(spread * noise) if base else spread * noise
        out[name] = jnp.asarray(drawn.astype(out[name].dtype))
    for name, factor in factors.items():
        out[name] = (out[name] * factor).astype(out[name].dtype)
    return out
```

```python
from contextlib import ExitStack

import numpy as np
import concourse.bass as bass
from concourse import mybir

ALU = mybir.AluOpType
ACT = mybir.ActivationFunctionType
F32 = mybir.dt.float32
F32R = mybir.dt.float32r
BF16 = mybir.dt.bfloat16
AX_X = mybir.AxisListType.X

P = 128
D = 128
NT = 16
SEQ = 4
TPS = NT // SEQ
L = TPS * P
LAYERS = 2
H = 16
HD = D // H
F = 4 * D
FB = F // P
E = 8
EPS = 1e-5
BIG = 1e30
SCALE = float(HD) ** -0.5
HG = 4
NG = H // HG
KR = 3 * HD
KM = KR + 2
VW = HD + 1

C_ID = 0
C_GQ = C_ID + P
C_GK = C_GQ + P
C_BLK = C_GK + P
C_MQ = C_BLK + P
C_MK = C_MQ + P
C_HM = C_MK + P
C_G128 = C_HM + HG
C_LQ = C_G128 + 1
C_LK = C_LQ + 1
C_ONE2 = C_LK + 1
C_ONES = C_ONE2 + 1
C_TRI = C_ONES + P
C_EPS = C_TRI + E * E
C_END = C_EPS + 1


def constants():
    gamma = (1.0 - 2.0 ** (-5.0 - np.arange(H, dtype=np.float64)))
    gch = np.repeat(gamma, HD)
    i = np.arange(P)
    c = np.zeros((P, C_END), np.float32)
    c[:, C_ID:C_ID + P] = np.eye(P)
    c[:, C_GQ:C_GQ + P] = gch[:, None] ** (i[None, :] + 1)
    c[:, C_GK:C_GK + P] = gch[None, :] ** (P - 1 - i[:, None])
    c[:, C_BLK:C_BLK + P] = (i[:, None] // HD) == (i[None, :] // HD)
    c[:, C_MQ:C_MQ + P] = np.where(i[None, :] > i[:, None], -BIG, 0.0)
    c[:, C_MK:C_MK + P] = np.where(i[:, None] > i[None, :], -BIG, 0.0)
    for j in range(HG):
        c[:, C_HM + j] = (i // HD) % HG == j
    c[:, C_G128] = gch ** P
    r = i % 32
    c[:, C_LQ] = ((r >= HD) & (r < 2 * HD)) | (r == KR + 1)
    c[:, C_LK] = (r >= 2 * HD) & (r < 3 * HD)
    c[:, C_ONE2] = (r == KR) | (r == KR + 1)
    c[:, C_ONES:C_ONES + P] = 1.0
    e = np.arange(E)
    c[:, C_TRI:C_TRI + E * E] = (e[None, :] < e[:, None]).reshape(1, -1)
    c[:, C_EPS] = EPS
    diff = i[None, :] - i[:, None]
    decay = np.where(diff[:, None, :] >= 0, gamma[None, :, None] ** np.maximum(diff, 0)[:, None, :], 0.0)
    return c, decay.astype(np.float32).reshape(P, H * P)


def mixer_kernel(nc, a_x, a_const, a_decay, a_proj_w, a_proj_bc, a_proj_b, a_reto_w, a_reto_b, a_lng, a_lnb,
                 a_lnf, a_ffn1_w, a_ffn1_b, a_ffn2_w, a_ffn2_b, a_wqkv, a_wo, a_bo,
                 a_gate_w, a_w1, a_w3, a_w2, a_out):
    with ExitStack() as ctx:
        def sb(name, shape, dt=F32):
            return ctx.enter_context(nc.sbuf_tensor(name, shape, dt))

        def ps(name, shape):
            return ctx.enter_context(nc.psum_tensor(name, shape, F32))

        def sem(name):
            return ctx.enter_context(nc.semaphore(name))

        const = sb("const", [P, C_END])
        decay = sb("decay", [P, H, P])
        proj_w = sb("proj_w", [P, LAYERS, 4 * D])
        proj_bc = sb("proj_bc", [P, LAYERS, 4])
        kvx_b = sb("kvx_b", [P, LAYERS, 3 * D])
        reto_w = sb("reto_w", [P, LAYERS, D])
        reto_b = sb("reto_b", [1, LAYERS, D])
        lng = sb("lng", [P, 2 * LAYERS])
        lnb = sb("lnb", [P, 2 * LAYERS])
        lnf = sb("lnf", [P, 2, D])
        ffn1_w = sb("ffn1_w", [P, LAYERS, F])
        ffn1_b = sb("ffn1_b", [P, LAYERS, FB])
        ffn2_w = sb("ffn2_w", [P, LAYERS, FB, D])
        ffn2_b = sb("ffn2_b", [1, LAYERS, D])
        wqkv = sb("wqkv", [P, 3, D])
        wo = sb("wo", [P, D])
        bo = sb("bo", [1, D])
        gate_w = sb("gate_w", [P, E])
        w1 = sb("w1", [P, E, F])
        w3 = sb("w3", [P, E, F])
        w2 = sb("w2", [P, E, FB, D])

        X = sb("X", [P, NT, D])
        R = sb("R", [P, NT, D])
        xn = sb("xn", [P, NT, D])
        xT = sb("xT", [P, NT * P])
        st6 = sb("st6", [P, NT, 6])
        mv = sb("mv", [P, NT, 2])
        std = sb("std", [P, NT])
        rstd = sb("rstd", [P, NT])
        hT = sb("hT", [P, 2, FB, L])
        qT = sb("qT", [P, 2, L])
        silu_a = qT
        qgT = sb("qgT", [P, 2, L])
        kTm = sb("kTm", [P, 2, HG, L])
        kbm = sb("kbm", [P, LAYERS, HG])
        kvx = sb("kvx", [P, 2, 3 * D])
        kg = sb("kg", [P, 2, D])
        pm = sb("pm", [P, 2, 2, 8, P])
        sx = sb("sx", [P, 2, D])
        rg = sb("rg", [P, 2, D])
        rgT = sb("rgT", [P, 2, D])
        dst = sb("dst", [P, D])
        state = sb("state", [P, 2, D])
        lg = sb("lg", [P, NT, E])
        lgm = sb("lgm", [P, NT])
        lgd = sb("lgd", [P, NT, E])
        lge = sb("lge", [P, NT, E])
        cgt = sb("cgt", [P, 4, E, E])
        cge = sb("cge", [P, 4, E, E])
        rank = sb("rank", [P, NT, E])
        wsum = sb("wsum", [P, NT])
        wrec = sb("wrec", [P, NT])
        wi = sb("wi", [P, NT, E])
        wq_pad = sb("wq_pad", [P, NG, P])
        wk_pad = sb("wk_pad", [P, NG, P])
        idb = sb("idb", [P, P], BF16)
        mqb = sb("mqb", [P, P], BF16)
        mkb = sb("mkb", [P, P], BF16)
        rq = sb("rq", [P, L], F32R)
        rk = sb("rk", [P, L], F32R)
        ks = sb("ks", [P, 2, L], F32R)
        qs = sb("qs", [P, 2, L], F32R)
        qm = sb("qm", [P, 2, L], F32R)
        rmax = sb("rmax", [P, 2, TPS, HG])
        nmp = qgT[:, 0, :].rearrange("p (t n) -> p t n", t=TPS)
        va = kTm[:, :, :, :].rearrange("p a j n -> p (a j n)")[:, 0:2 * TPS * H * VW].rearrange(
            "p (a t h c) -> p a t h c", a=2, t=TPS, h=H)
        pt = pm[:, 0, :, :, :].rearrange("p u (k j) n -> p u k (j n)", k=2)
        rden = sb("rden", [P, 2, TPS * HG])
        aoT = rgT

        PA = ps("PA", [P, 2, 512])
        PB = ps("PB", [P, 2, 512])
        PC = ps("PC", [P, 2, 512])
        P6 = ps("P6", [P, 512])
        P7 = ps("P7", [P, 512])

        ident = const[:, C_ID:C_ID + P]
        ones_row = const[0:1, C_ONES:C_ONES + P]

        in_x = sem("in_x")
        in_const = sem("in_const")
        in_ret = sem("in_ret")
        in_moe = sem("in_moe")
        in_att = sem("in_att")
        out_done = sem("out_done")
        v_chain = sem("v_chain")
        ln_var = sem("ln_var")
        ln_std = sem("ln_std")
        xn_ready = sem("xn_ready")
        tp_ready = sem("tp_ready")
        xT_ready = sem("xT_ready")
        kbm_ready = sem("kbm_ready")
        qk_ps = sem("qk_ps")
        qk_sb = sem("qk_sb")
        qg_sb = sem("qg_sb")
        kvx_ps = sem("kvx_ps")
        kvx_sb = sem("kvx_sb")
        kg_sb = sem("kg_sb")
        sc_ps = sem("sc_ps")
        pm_sb = sem("pm_sb")
        silu_sb = sem("silu_sb")
        pv_ps = sem("pv_ps")
        rg_sb = sem("rg_sb")
        state_sb = sem("state_sb")
        rt_ps = sem("rt_ps")
        rt_sb = sem("rt_sb")
        ro_ps = sem("ro_ps")
        ro_up = sem("ro_up")
        f1_ps = sem("f1_ps")
        f1_sb = sem("f1_sb")
        f2_ps = sem("f2_ps")
        f2_up = sem("f2_up")
        lg_ps = sem("lg_ps")
        lg_d = sem("lg_d")
        lg_e = sem("lg_e")
        m1_ps = sem("m1_ps")
        m1_si = sem("m1_si")
        m1_sb = sem("m1_sb")
        m2_ps = sem("m2_ps")
        m2_up = sem("m2_up")
        pad_ready = sem("pad_ready")
        v_ps = sem("v_ps")
        v_sb = sem("v_sb")
        k_ps = sem("k_ps")
        k_rd = sem("k_rd")
        k_sb = sem("k_sb")
        q_ps = sem("q_ps")
        q_rd = sem("q_rd")
        q_sb = sem("q_sb")
        mx_ps = sem("mx_ps")
        mx_sb = sem("mx_sb")
        nm_sb = sem("nm_sb")
        ex_ps = sem("ex_ps")
        ex_sb = sem("ex_sb")
        av_ps = sem("av_ps")
        av_sb = sem("av_sb")
        ao_ps = sem("ao_ps")
        ao_sb = sem("ao_sb")
        wo_ps = sem("wo_ps")
        wo_up = sem("wo_up")

        in_const_n, in_ret_n, in_att_n, in_moe_n = 2 * 16, 12 * 16, 3 * 16, 4 * 16

        block = ctx.enter_context(nc.Block())

        LN0, LNF, LNM1, LNC, LNM2 = 0, 2 * LAYERS + 1, 2 * LAYERS + 2, 2 * LAYERS + 3, 2 * LAYERS + 4
        turned = {n: k for k, n in enumerate([n for n in range(9) if n not in (LN0, LNF)])}

        @block.sync
        def _(sp):
            x_t = a_x.rearrange("(t p) d -> p t d", p=P)
            for s in range(SEQ):
                sp.dma_start(X[:, TPS * s:TPS * s + TPS, :], x_t[:, TPS * s:TPS * s + TPS, :]).then_inc(in_x, 16)
            sp.dma_start(const[:, :], a_const).then_inc(in_const, 16)
            sp.dma_start(decay[:, :, :], a_decay.rearrange("p (h n) -> p h n", h=H)).then_inc(in_const, 16)
            sp.dma_start(proj_w[:, :, :], a_proj_w.rearrange("l d n -> d l n")).then_inc(in_ret, 16)
            sp.dma_start(proj_bc[:, :, :], a_proj_bc.rearrange("p (l c) -> p l c", l=LAYERS)).then_inc(in_ret, 16)
            sp.dma_start(kvx_b[:, :, :], a_proj_b[:, D:4 * D].partition_broadcast(P)).then_inc(in_ret, 16)
            sp.dma_start(reto_w[:, :, :], a_reto_w.rearrange("l d n -> d l n")).then_inc(in_ret, 16)
            sp.dma_start(reto_b[:, :, :], a_reto_b.rearrange("(a l) n -> a l n", a=1)).then_inc(in_ret, 16)
            sp.dma_start(lng[:, :], a_lng).then_inc(in_ret, 16)
            sp.dma_start(lnb[:, :], a_lnb).then_inc(in_ret, 16)
            sp.dma_start(lnf[:, :, :], a_lnf.partition_broadcast(P)).then_inc(in_ret, 16)
            sp.dma_start(ffn1_w[:, :, :], a_ffn1_w.rearrange("l d n -> d l n")).then_inc(in_ret, 16)
            sp.dma_start(ffn1_b[:, :, :], a_ffn1_b.rearrange("p (l f) -> p l f", l=LAYERS)).then_inc(in_ret, 16)
            sp.dma_start(ffn2_w[:, :, :, :], a_ffn2_w.rearrange("l (f p) n -> p l f n", p=P)).then_inc(in_ret, 16)
            sp.dma_start(ffn2_b[:, :, :], a_ffn2_b.rearrange("(a l) n -> a l n", a=1)).then_inc(in_ret, 16)
            sp.dma_start(gate_w[:, :], a_gate_w).then_inc(in_moe, 16)
            sp.dma_start(w1[:, :, :], a_w1.rearrange("e d f -> d e f")).then_inc(in_moe, 16)
            sp.dma_start(w3[:, :, :], a_w3.rearrange("e d f -> d e f")).then_inc(in_moe, 16)
            sp.dma_start(w2[:, :, :, :], a_w2.rearrange("e (f p) d -> p e f d", p=P)).then_inc(in_moe, 16)
            sp.dma_start(wqkv[:, :, :], a_wqkv.rearrange("c d n -> d c n")).then_inc(in_att, 16)
            sp.dma_start(wo[:, :], a_wo).then_inc(in_att, 16)
            sp.dma_start(bo[:, :], a_bo.rearrange("(a n) -> a n", a=1)).then_inc(in_att, 16)
            o_t = a_out.rearrange("(t p) d -> p t d", p=P)
            for s in range(SEQ):
                sp.wait_ge(m2_up, SEQ * E + (s + 1) * E)
                sp.dma_start(o_t[:, TPS * s:TPS * s + TPS, :], X[:, TPS * s:TPS * s + TPS, :]).then_inc(out_done, 16)
            sp.wait_ge(out_done, 16 * SEQ)

        @block.vector
        def _(dve):
            chain = [0]

            def link(ins):
                chain[0] += 1
                ins.then_inc(v_chain, 1)
                dve.wait_ge(v_chain, chain[0])

            def bc(ap, shape, axis):
                return ap.unsqueeze(axis).to_broadcast(shape)

            def norm_tiles(n, src, out):
                for t in range(NT):
                    ins = nc.vector.bn_stats(st6[:, t, :], src[:, t, :])
                link(ins)
                for t in range(NT):
                    ins = nc.vector.bn_aggr(mv[:, t, :], st6[:, t, :])
                ins.then_inc(ln_var, 1)
                dve.wait_ge(ln_std, n + 1)
                link(nc.vector.reciprocal(rstd[:, :], std[:, :]))
                for t in range(NT):
                    ins = nc.vector.tensor_scalar(out[:, t, :], src[:, t, :], mv[:, t, 0:1], rstd[:, t:t + 1],
                                                  ALU.subtract, ALU.mult)
                    if n in turned:
                        ins.then_inc(xn_ready, 1)
                if n not in turned:
                    link(ins)

            def retention(layer):
                def project_out(t):
                    g = layer * NT + t
                    dve.wait_ge(kvx_ps, g + 1)
                    if g >= 2:
                        dve.wait_ge(pv_ps, g - 1)
                    nc.vector.tensor_tensor(kvx[:, g % 2, :], P6[:, 0:3 * D], kvx_b[:, layer, :],
                                            ALU.add).then_inc(kvx_sb, 1)
                    dve.wait_ge(kvx_sb, g + 1)
                    nc.vector.tensor_tensor(kg[:, g % 2, :], kvx[:, g % 2, 0:D], const[:, C_GK:C_GK + P],
                                            ALU.mult).then_inc(kg_sb, 1)

                def decay_q(s):
                    g = layer * SEQ + s
                    dve.wait_ge(qk_sb, g + 1)
                    nc.vector.tensor_tensor(
                        qgT[:, g % 2, :].rearrange("p (t n) -> p t n", t=TPS),
                        qT[:, g % 2, :].rearrange("p (t n) -> p t n", t=TPS),
                        bc(const[:, C_GQ:C_GQ + P], [P, TPS, P], 1), ALU.mult).then_inc(qg_sb, 1)

                def decay_scores(t, u):
                    g = layer * NT + t
                    dve.wait_ge(sc_ps, 2 * g + u + 1)
                    src = PA if u == 0 else PB
                    nc.vector.tensor_tensor(pm[:, g % 2, u, :, :],
                                            src[:, :, :].rearrange("p b (j n) -> p (b j) n", n=P),
                                            decay[:, 8 * u:8 * u + 8, :], ALU.mult).then_inc(pm_sb, 1)

                def gate(t):
                    g = layer * NT + t
                    dve.wait_ge(pv_ps, g + 1)
                    dve.wait_ge(silu_sb, g + 1)
                    if g >= 2:
                        dve.wait_ge(rt_ps, g - 1)
                    nc.vector.tensor_tensor(rg[:, g % 2, :], P7[:, 0:D], sx[:, g % 2, :],
                                            ALU.mult).then_inc(rg_sb, 1)
                    if t % TPS < TPS - 1:
                        link(nc.vector.tensor_tensor(dst[:, :], P7[:, D:2 * D], const[:, C_BLK:C_BLK + P], ALU.mult))
                        if t % TPS == 0:
                            ins = nc.vector.tensor_copy(state[:, g % 2, :], dst[:, :])
                        else:
                            ins = nc.vector.scalar_tensor_tensor(
                                out=state[:, g % 2, :], in0=state[:, (g - 1) % 2, :],
                                scalar=const[:, C_G128:C_G128 + 1], in1=dst[:, :], op0=ALU.mult, op1=ALU.add)
                        ins.then_inc(state_sb, 1)
                        dve.wait_ge(state_sb, layer * SEQ * (TPS - 1) + t // TPS * (TPS - 1) + t % TPS + 1)

                def add_out(t):
                    g = layer * NT + t
                    dve.wait_ge(ro_ps, g + 1)
                    nc.vector.tensor_tensor(R[:, t, :], P7[:, 0:D], R[:, t, :], ALU.add).then_inc(ro_up, 1)

                for s in range(NT + 3):
                    if s < NT:
                        project_out(s)
                        if s % TPS == 0:
                            decay_q(s // TPS)
                        decay_scores(s, 0)
                    if s >= 3:
                        add_out(s - 3)
                    if s < NT:
                        decay_scores(s, 1)
                    if 1 <= s < NT + 1:
                        gate(s - 1)

            def feed_forward(layer):
                for t in range(NT):
                    g = layer * NT + t
                    dve.wait_ge(f2_ps, g + 1)
                    src = P6 if g % 2 == 0 else P7
                    nc.vector.tensor_tensor(R[:, t, :], src[:, 0:D], R[:, t, :], ALU.add).then_inc(f2_up, 1)

            def experts(m):
                dve.wait_ge(lg_ps, m + 1)
                link(nc.vector.tensor_copy(lg[:, :, :], P6[:, 0:NT * E].rearrange("p (t e) -> p t e", e=E)))
                link(nc.vector.tensor_reduce(lgm[:, :], lg[:, :, :], AX_X, ALU.max))
                nc.vector.tensor_tensor(lgd[:, :, :], lg[:, :, :], bc(lgm[:, :], [P, NT, E], 2),
                                        ALU.subtract).then_inc(lg_d, 1)
                for c in range(NT // 4):
                    rows = [nc.vector.tensor_tensor(
                        o[:, k, :, :],
                        bc(lg[:, 4 * c + k, :], [P, E, E], 1),
                        bc(lg[:, 4 * c + k, :], [P, E, E], 2), op)
                        for k in range(4) for o, op in ((cgt, ALU.is_gt), (cge, ALU.is_ge))]
                    link(rows[-1])
                    tri = const[:, C_TRI:C_TRI + E * E]
                    link(nc.vector.tensor_tensor(cge[:, :, :, :].rearrange("p k a b -> p k (a b)"),
                                                 cge[:, :, :, :].rearrange("p k a b -> p k (a b)"),
                                                 bc(tri, [P, 4, E * E], 1), ALU.mult))
                    link(nc.vector.tensor_tensor(cgt[:, :, :, :], cgt[:, :, :, :], cge[:, :, :, :], ALU.max))
                    link(nc.vector.tensor_reduce(rank[:, 4 * c:4 * c + 4, :], cgt[:, :, :, :], AX_X, ALU.add))
                dve.wait_ge(lg_e, m + 1)
                link(nc.vector.scalar_tensor_tensor(out=wi[:, :, :], in0=rank[:, :, :], scalar=2.0,
                                                    in1=lge[:, :, :], op0=ALU.is_lt, op1=ALU.mult))
                link(nc.vector.tensor_reduce(wsum[:, :], wi[:, :, :], AX_X, ALU.add))
                link(nc.vector.reciprocal(wrec[:, :], wsum[:, :]))
                link(nc.vector.tensor_tensor(wi[:, :, :], wi[:, :, :], bc(wrec[:, :], [P, NT, E], 2), ALU.mult))

                def add_expert(s, e):
                    g = (m * SEQ + s) * E + e
                    dve.wait_ge(m2_ps, g + 1)
                    if g >= 1:
                        dve.wait_ge(m2_up, g)
                    src = PC[:, g % 2, :]
                    for k in range(TPS):
                        t = TPS * s + k
                        ins = nc.vector.scalar_tensor_tensor(
                            out=X[:, t, :], in0=src[:, k * D:(k + 1) * D], scalar=wi[:, t, e:e + 1],
                            in1=X[:, t, :], op0=ALU.mult, op1=ALU.add)
                    ins.then_inc(m2_up, 1)

                prev = None
                for s in range(SEQ):
                    for e in range(E):
                        for f in range(FB):
                            g = ((m * SEQ + s) * E + e) * FB + f
                            dve.wait_ge(m1_si, g + 1)
                            if f == 0 and (m * SEQ + s) * E + e >= 2:
                                dve.wait_ge(m2_ps, (m * SEQ + s) * E + e - 1)
                            nc.vector.tensor_tensor(hT[:, (g // FB) % 2, f, :], silu_a[:, g % 2, :],
                                                    PB[:, g % 2, :], ALU.mult).then_inc(m1_sb, 1)
                            if f == 1 and prev is not None:
                                add_expert(*prev)
                        prev = (s, e)
                add_expert(*prev)

            def pad_weights():
                dve.wait_ge(in_att, in_att_n)
                nc.vector.memset(wk_pad[:, :, :], 0.0)
                link(nc.vector.memset(wq_pad[:, :, :], 0.0))
                for c, pad, low in ((0, wq_pad, 1), (1, wk_pad, 2)):
                    v = pad[:, :, :].rearrange("p a (g r) -> p a g r", g=HG)
                    src = wqkv[:, c, :].rearrange("p (a g k) -> p a g k", a=NG, g=HG)
                    for r in range(3):
                        for a in range(NG):
                            nc.vector.tensor_scalar(v[:, a, :, HD * r:HD * r + HD], src[:, a, :, :],
                                                    -1.0 if r == low else 1.0, None, ALU.mult)
                nc.vector.memset(nmp[:, :, :], 0.0)
                nc.vector.memset(va[:, :, :, :, :], 1.0)
                nc.vector.tensor_copy(idb[:, :], ident)
                nc.vector.tensor_copy(mqb[:, :], const[:, C_MQ:C_MQ + P])
                link(nc.vector.tensor_copy(mkb[:, :], const[:, C_MK:C_MK + P]))
                nc.vector.tensor_copy(dst[:, 0:1], const[:, C_HM:C_HM + 1]).then_inc(pad_ready, 1)

            def attention():
                def split(out, low, rounded, src):
                    return nc.vector.scalar_tensor_tensor(
                        out=out, in0=src, scalar=low, in1=rounded[:, :].bitcast(F32),
                        op0=ALU.mult, op1=ALU.subtract, reverse1=True)

                def stacks(n):
                    s, a = divmod(n, NG)
                    if a == 0:
                        dve.wait_ge(v_ps, s + 1)
                        if s >= 2:
                            dve.wait_ge(av_ps, 8 * (s - 1) * NG)
                        nc.vector.tensor_copy(
                            va[:, s % 2, :, :, 0:HD].rearrange("p t h k -> p (t h) k"),
                            P6[:, :].rearrange("p (x k) -> p x k", k=HD)).then_inc(v_sb, 1)
                    dve.wait_ge(k_rd, n + 1)
                    if n >= 2:
                        dve.wait_ge(ex_ps, 8 * (n - 1))
                    split(ks[:, n % 2, :], const[:, C_LK:C_LK + 1], rk, P6[:, :]).then_inc(k_sb, 1)
                    dve.wait_ge(q_rd, 2 * n + 1)
                    split(qs[:, n % 2, :], const[:, C_LQ:C_LQ + 1], rq, P6[:, :]).then_inc(q_sb, 1)

                def row_max(n, v):
                    i, pair = divmod(v, 2)
                    g = 8 * n + v
                    dve.wait_ge(mx_ps, g + 1)
                    w = (i + 1) * P
                    ins = nc.vector.tensor_reduce(rmax[:, n % 2, i, 2 * pair:2 * pair + 2], PA[:, :, 0:w],
                                                  AX_X, ALU.max)
                    ins.then_inc(mx_sb, 1)

                def minus_max(n):
                    dve.wait_ge(mx_sb, 8 * n + 8)
                    if n >= 1:
                        dve.wait_ge(q_ps, 2 * n)
                    v = nmp[:, :, :].rearrange("p t (g r) -> p t g r", g=HG)
                    nc.vector.tensor_scalar(v[:, :, :, KR:KR + 1].rearrange("p t g r -> p t (g r)"),
                                            rmax[:, n % 2, :, :], -1.0, None, ALU.mult)
                    nc.vector.tensor_copy(v[:, :, :, KR + 1:KR + 2].rearrange("p t g r -> p t (g r)"),
                                          rmax[:, n % 2, :, :]).then_inc(nm_sb, 1)

                def shifted(n):
                    dve.wait_ge(q_rd, 2 * n + 2)
                    if n >= 2:
                        dve.wait_ge(ex_ps, 8 * (n - 1))
                    split(qm[:, n % 2, :], const[:, C_LQ:C_LQ + 1], rq, P6[:, :]).then_inc(q_sb, 1)

                def weigh(n):
                    s, a = divmod(n, NG)
                    dve.wait_ge(av_ps, 8 * (n + 1))
                    o = P7[:, 0:TPS * HG * VW].rearrange("p (x c) -> p x c", c=VW)
                    link(nc.vector.reciprocal(rden[:, n % 2, :], o[:, :, HD]))
                    out = xn[:, TPS * s:TPS * s + TPS, HG * HD * a:HG * HD * (a + 1)]
                    for k in range(TPS):
                        ins = nc.vector.tensor_tensor(
                            out[:, k, :].rearrange("p (g c) -> p g c", c=HD),
                            o[:, k * HG:(k + 1) * HG, 0:HD],
                            bc(rden[:, n % 2, k * HG:(k + 1) * HG], [P, HG, HD], 2), ALU.mult)
                    ins.then_inc(av_sb, 1)

                items = SEQ * NG
                for n in range(items + 1):
                    if n < items:
                        stacks(n)
                        for v in range(8):
                            row_max(n, v)
                        minus_max(n)
                    if n >= 1:
                        weigh(n - 1)
                    if n < items:
                        shifted(n)
                for t in range(NT):
                    dve.wait_ge(wo_ps, t + 1)
                    nc.vector.tensor_tensor(X[:, t, :], PA[:, t % 2, 0:D], X[:, t, :], ALU.add).then_inc(wo_up, 1)
                dve.wait_ge(wo_up, NT)

            dve.wait_ge(in_const, in_const_n)
            dve.wait_ge(in_ret, in_ret_n)
            for layer in range(LAYERS):
                for j in range(HG):
                    ins = nc.vector.tensor_tensor(kbm[:, layer, j:j + 1], proj_bc[:, layer, 1:2],
                                                  const[:, C_HM + j:C_HM + j + 1], ALU.mult)
            ins.then_inc(kbm_ready, 1)
            dve.wait_ge(in_x, 16 * SEQ)
            norm_tiles(LN0, X, R)
            for layer in range(LAYERS):
                norm_tiles(1 + 2 * layer, R, xn)
                retention(layer)
                dve.wait_ge(ro_up, (layer + 1) * NT)
                norm_tiles(2 + 2 * layer, R, xn)
                feed_forward(layer)
                dve.wait_ge(f2_up, (layer + 1) * NT)
            norm_tiles(LNF, R, xn)
            link(nc.vector.tensor_tensor(xn[:, :, :], xn[:, :, :], bc(lnf[:, 0, :], [P, NT, D], 1), ALU.mult))
            link(nc.vector.tensor_tensor(xn[:, :, :], xn[:, :, :], bc(lnf[:, 1, :], [P, NT, D], 1), ALU.add))
            link(nc.vector.tensor_tensor(X[:, :, :], X[:, :, :], xn[:, :, :], ALU.add))
            norm_tiles(LNM1, X, xn)
            experts(0)
            dve.wait_ge(m2_up, SEQ * E)
            pad_weights()
            norm_tiles(LNC, X, xn)
            attention()
            norm_tiles(LNM2, X, xn)
            experts(1)

        @block.scalar
        def _(act):
            def norm_std(n):
                act.wait_ge(ln_var, n + 1)
                nc.scalar.activation(std[:, :], mv[:, :, 1], ACT.Sqrt,
                                     bias=const[:, C_EPS:C_EPS + 1]).then_inc(ln_std, 1)

            def turn(n, gain=None, shift=None):
                norm_std(n)
                for s in range(SEQ):
                    g = turned[n] * SEQ + s
                    act.wait_ge(tp_ready, g + 1)
                    dst_, src = xT[:, s * L:(s + 1) * L], PC[:, g % 2, :]
                    if gain is None:
                        ins = nc.scalar.activation(dst_, src, ACT.Copy)
                    else:
                        ins = nc.scalar.activation(dst_, src, ACT.Identity, bias=shift, scale=gain)
                    ins.then_inc(xT_ready, 1)

            def retention(layer):
                def qk_out(s):
                    g = layer * SEQ + s
                    act.wait_ge(qk_ps, g + 1)
                    if g >= 2:
                        act.wait_ge(qg_sb, g - 1)
                    nc.scalar.activation(qT[:, g % 2, :], PC[:, 0, :], ACT.Identity, bias=proj_bc[:, layer, 0:1])
                    for j in range(HG):
                        ins = nc.scalar.activation(kTm[:, g % 2, j, :], PC[:, 1, :], ACT.Identity,
                                                   bias=kbm[:, layer, j:j + 1], scale=const[:, C_HM + j:C_HM + j + 1])
                    ins.then_inc(qk_sb, 1)

                def silu(t):
                    g = layer * NT + t
                    act.wait_ge(kvx_sb, g + 1)
                    if g >= 2:
                        act.wait_ge(rg_sb, g - 1)
                    nc.scalar.activation(sx[:, g % 2, :], kvx[:, g % 2, 2 * D:3 * D], ACT.Silu).then_inc(silu_sb, 1)

                def turn_gated(t):
                    g = layer * NT + t
                    act.wait_ge(rt_ps, g + 1)
                    if g >= 2:
                        act.wait_ge(ro_ps, g - 1)
                    nc.scalar.activation(rgT[:, g % 2, :], P6[:, 0:D], ACT.Copy).then_inc(rt_sb, 1)

                if layer == 0:
                    act.wait_ge(kbm_ready, 1)
                qk_out(0)
                for s in range(NT + 2):
                    if s < NT:
                        silu(s)
                    if s % TPS == 2 and s // TPS + 1 < SEQ:
                        qk_out(s // TPS + 1)
                    if s >= 2:
                        turn_gated(s - 2)

            def feed_forward(layer):
                for s in range(SEQ):
                    for f in range(FB):
                        g = (layer * SEQ + s) * FB + f
                        act.wait_ge(f1_ps, g + 1)
                        if f == 0 and layer * SEQ + s >= 2:
                            act.wait_ge(f2_ps, (layer * SEQ + s - 1) * TPS)
                        src = (PA, PB)[f // 2][:, f % 2, :]
                        nc.scalar.activation(hT[:, (layer * SEQ + s) % 2, f, :], src, ACT.Gelu,
                                             bias=ffn1_b[:, layer, f:f + 1]).then_inc(f1_sb, 1)

            def experts(m):
                act.wait_ge(lg_d, m + 1)
                nc.scalar.activation(lge[:, :, :], lgd[:, :, :], ACT.Exp).then_inc(lg_e, 1)
                for k in range(SEQ * E * FB):
                    g = m * SEQ * E * FB + k
                    act.wait_ge(m1_ps, g + 1)
                    if g >= 2:
                        act.wait_ge(m1_sb, g - 1)
                    nc.scalar.activation(silu_a[:, g % 2, :], PA[:, g % 2, :], ACT.Silu).then_inc(m1_si, 1)

            def attention():
                items = SEQ * NG

                def stacks(n):
                    act.wait_ge(k_ps, n + 1)
                    if n >= 1:
                        act.wait_ge(k_sb, n)
                    nc.scalar.activation(rk[:, :], P6[:, :], ACT.Identity,
                                         bias=const[:, C_ONE2:C_ONE2 + 1]).then_inc(k_rd, 1)
                    round_q(2 * n)

                def round_q(m):
                    act.wait_ge(q_ps, m + 1)
                    if m >= 1:
                        act.wait_ge(q_sb, m)
                    nc.scalar.activation(rq[:, :], P6[:, :], ACT.Copy).then_inc(q_rd, 1)

                def exps(n, v):
                    g = 8 * n + v
                    j = v // 2
                    act.wait_ge(ex_ps, g + 1)
                    if g >= 2:
                        act.wait_ge(av_ps, g - 1)
                    w = (TPS - j) * P
                    src = (PB, PC)[g % 2]
                    nc.scalar.activation(pt[:, g % 2, :, 0:w], src[:, :, 0:w], ACT.Exp,
                                         scale=SCALE).then_inc(ex_sb, 1)

                for n in range(items + 1):
                    if n < items:
                        stacks(n)
                    if n >= 1:
                        for v in range(8):
                            exps(n - 1, v)
                    if n < items:
                        round_q(2 * n + 1)
                for t in range(NT):
                    act.wait_ge(ao_ps, t + 1)
                    if t >= 2:
                        act.wait_ge(wo_ps, t - 1)
                    nc.scalar.activation(aoT[:, t % 2, :], (P6, P7)[t % 2][:, 0:P],
                                         ACT.Copy).then_inc(ao_sb, 1)

            act.wait_ge(in_const, in_const_n)
            act.wait_ge(in_ret, in_ret_n)
            norm_std(LN0)
            for layer in range(LAYERS):
                turn(1 + 2 * layer, lng[:, 2 * layer:2 * layer + 1], lnb[:, 2 * layer:2 * layer + 1])
                retention(layer)
                turn(2 + 2 * layer, lng[:, 2 * layer + 1:2 * layer + 2], lnb[:, 2 * layer + 1:2 * layer + 2])
                feed_forward(layer)
            norm_std(LNF)
            turn(LNM1)
            experts(0)
            turn(LNC)
            attention()
            turn(LNM2)
            experts(1)

        @block.tensor
        def _(pe):
            mm = nc.tensor.matmul

            def turn(n):
                for t in range(NT):
                    g = turned[n] * NT + t
                    s = g // TPS
                    if t % TPS == 0 and s >= 2:
                        pe.wait_ge(xT_ready, s - 1)
                    pe.wait_ge(xn_ready, g + 1)
                    ins = nc.tensor.transpose(PC[:, s % 2, (t % TPS) * P:(t % TPS + 1) * P], xn[:, t, :], ident)
                    if t % TPS == TPS - 1:
                        ins.then_inc(tp_ready, 1)

            def retention(layer):
                xr = turned[1 + 2 * layer] * SEQ

                def qk(s):
                    g = layer * SEQ + s
                    pe.wait_ge(xT_ready, xr + (SEQ if s == 0 else s + 1))
                    if s >= 1:
                        pe.wait_ge(qk_sb, g)
                    mm(PC[:, 0, :], proj_w[:, layer, 0:D], xT[:, s * L:(s + 1) * L], start=True, stop=True)
                    mm(PC[:, 1, :], proj_w[:, layer, D:2 * D], xT[:, s * L:(s + 1) * L], start=True,
                       stop=True).then_inc(qk_ps, 1)

                def kvx_mm(t):
                    g = layer * NT + t
                    if g >= 1:
                        pe.wait_ge(kvx_sb, g)
                    if t >= 3:
                        pe.wait_ge(rt_sb, g - 2)
                    mm(P6[:, 0:3 * D], xT[:, t * P:(t + 1) * P], proj_w[:, layer, D:4 * D], start=True,
                       stop=True).then_inc(kvx_ps, 1)

                def scores(t, u):
                    g = layer * NT + t
                    b = layer * SEQ + t // TPS
                    pe.wait_ge(qk_sb, b + 1)
                    if g >= 1:
                        pe.wait_ge(pm_sb, 2 * (g - 1) + u + 1)
                    c = slice((t % TPS) * P, (t % TPS + 1) * P)
                    for j in range(HG):
                        for k in range(2):
                            r = slice(32 * (2 * u + k), 32 * (2 * u + k) + 32)
                            ins = mm((PA, PB)[u][:, k, j * P:(j + 1) * P], kTm[r, b % 2, j, c], qT[r, b % 2, c],
                                     start=True, stop=True)
                    ins.then_inc(sc_ps, 1)

                def seen_by(layer, t):
                    return (layer * SEQ + t // TPS) * (TPS - 1) + t % TPS

                def retain(t):
                    g = layer * NT + t
                    if t >= 2:
                        pe.wait_ge(ro_up, g - 1)
                    b = layer * SEQ + t // TPS
                    pe.wait_ge(pm_sb, 2 * g + 2)
                    pe.wait_ge(kg_sb, g + 1)
                    if g >= 1:
                        pe.wait_ge(rg_sb, g)
                    first = t % TPS == 0
                    seen = seen_by(layer, t)
                    if seen:
                        pe.wait_ge(state_sb, seen)
                    if not first:
                        pe.wait_ge(qg_sb, b + 1)
                        mm(P7[:, 0:D], qgT[:, b % 2, (t % TPS) * P:(t % TPS + 1) * P], state[:, (g - 1) % 2, :],
                           start=True, stop=False, skip_group_check=True)
                    for h in range(H):
                        u, k = divmod(h, 8)
                        ins = mm(P7[:, HD * h:HD * h + HD], pm[:, g % 2, u, k, :],
                                 kvx[:, g % 2, D + HD * h:D + HD * h + HD], start=first, stop=first or h == H - 1,
                                 skip_group_check=True)
                    if t % TPS < TPS - 1:
                        ins = mm(P7[:, D:2 * D], kg[:, g % 2, :], kvx[:, g % 2, D:2 * D], start=True, stop=True)
                    ins.then_inc(pv_ps, 1)

                def turn_gated(t):
                    g = layer * NT + t
                    pe.wait_ge(rg_sb, g + 1)
                    pe.wait_ge(kvx_sb, layer * NT + min(t + 3, NT))
                    nc.tensor.transpose(P6[:, 0:D], rg[:, g % 2, :], ident).then_inc(rt_ps, 1)

                def reto(t):
                    g = layer * NT + t
                    pe.wait_ge(rt_sb, g + 1)
                    done = min(t + 2, NT)
                    pe.wait_ge(rg_sb, layer * NT + done)
                    pe.wait_ge(state_sb, seen_by(layer, done))
                    if g >= 1:
                        pe.wait_ge(ro_up, g)
                    mm(P7[:, 0:D], rgT[:, g % 2, :], reto_w[:, layer, :], start=True, stop=False)
                    mm(P7[:, 0:D], ones_row, reto_b[:, layer, :], start=False, stop=True).then_inc(ro_ps, 1)

                qk(0)
                for s in range(NT + 3):
                    if s < NT:
                        kvx_mm(s)
                        scores(s, 0)
                    if s >= 3:
                        reto(s - 3)
                    if s < NT:
                        scores(s, 1)
                    if 2 <= s < NT + 2:
                        turn_gated(s - 2)
                    if 1 <= s < NT + 1:
                        retain(s - 1)
                    if s % TPS == 2 and s // TPS + 1 < SEQ:
                        qk(s // TPS + 1)

            def feed_forward(layer):
                xr = turned[2 + 2 * layer] * SEQ

                def up(s):
                    pe.wait_ge(xT_ready, xr + s + 1)
                    for f in range(FB):
                        g = (layer * SEQ + s) * FB + f
                        if g >= 4:
                            pe.wait_ge(f1_sb, g - 3)
                        mm((PA, PB)[f // 2][:, f % 2, :], ffn1_w[:, layer, f * P:(f + 1) * P],
                           xT[:, s * L:(s + 1) * L], start=True, stop=True).then_inc(f1_ps, 1)

                def down(s):
                    b = layer * SEQ + s
                    pe.wait_ge(f1_sb, (b + 1) * FB)
                    for k in range(TPS):
                        g = b * TPS + k
                        if g >= 2:
                            pe.wait_ge(f2_up, g - 1)
                        dst_ = (P6 if g % 2 == 0 else P7)[:, 0:D]
                        for f in range(FB):
                            mm(dst_, hT[:, b % 2, f, k * P:(k + 1) * P], ffn2_w[:, layer, f, :], start=f == 0,
                               stop=False)
                        mm(dst_, ones_row, ffn2_b[:, layer, :], start=False, stop=True).then_inc(f2_ps, 1)

                up(0)
                for s in range(SEQ):
                    if s + 1 < SEQ:
                        up(s + 1)
                    down(s)

            def experts(m):
                xr = turned[(LNM1, LNM2)[m]] * SEQ
                pe.wait_ge(xT_ready, xr + SEQ)
                for t in range(NT):
                    ins = mm(P6[:, t * E:(t + 1) * E], xT[:, t * P:(t + 1) * P], gate_w[:, :], start=True, stop=True)
                ins.then_inc(lg_ps, 1)

                def down(s, e):
                    b = (m * SEQ + s) * E + e
                    pe.wait_ge(m1_sb, (b + 1) * FB)
                    if b >= 2:
                        pe.wait_ge(m2_up, b - 1)
                    for k in range(TPS):
                        for f in range(FB):
                            ins = mm(PC[:, b % 2, k * D:(k + 1) * D], hT[:, b % 2, f, k * P:(k + 1) * P],
                                     w2[:, e, f, :], start=f == 0, stop=f == FB - 1)
                    ins.then_inc(m2_ps, 1)

                prev = None
                for s in range(SEQ):
                    for e in range(E):
                        for f in range(FB):
                            g = ((m * SEQ + s) * E + e) * FB + f
                            if g >= 2:
                                pe.wait_ge(m1_sb, g - 1)
                            mm(PA[:, g % 2, :], w1[:, e, f * P:(f + 1) * P], xT[:, s * L:(s + 1) * L],
                               start=True, stop=True)
                            mm(PB[:, g % 2, :], w3[:, e, f * P:(f + 1) * P], xT[:, s * L:(s + 1) * L],
                               start=True, stop=True).then_inc(m1_ps, 1)
                        if prev is not None:
                            down(*prev)
                        prev = (s, e)
                down(*prev)

            def attention():
                xr = turned[LNC] * SEQ
                items = SEQ * NG

                def seq(s):
                    return xT[:, s * L:(s + 1) * L]

                def stacks(n):
                    s, a = divmod(n, NG)
                    if a == 0:
                        for k in range(TPS):
                            ins = mm(P6[:, k * P:(k + 1) * P], xT[:, (s * TPS + k) * P:(s * TPS + k + 1) * P],
                                     wqkv[:, 2, :], start=True, stop=True)
                        ins.then_inc(v_ps, 1)
                        pe.wait_ge(v_sb, s + 1)
                    mm(P6[:, :], wk_pad[:, a, :], seq(s), start=True, stop=True).then_inc(k_ps, 1)
                    pe.wait_ge(k_sb, n + 1)
                    mm(P6[:, :], wq_pad[:, a, :], seq(s), start=True, stop=False,
                       skip_group_check=True).then_inc(q_ps, 1)

                def shifted_q(n):
                    pe.wait_ge(nm_sb, n + 1)
                    pe.wait_ge(q_sb, 2 * n + 1)
                    for k in range(TPS):
                        ins = mm(P6[:, k * P:(k + 1) * P], nmp[:, k, :], ident, start=False, stop=True,
                                 skip_group_check=True)
                    ins.then_inc(q_ps, 1)
                    pe.wait_ge(q_sb, 2 * n + 2)

                def max_scores(n, v):
                    i, pair = divmod(v, 2)
                    g = 8 * n + v
                    pe.wait_ge(q_sb, 2 * n + 1)
                    if g >= 1:
                        pe.wait_ge(mx_sb, g)
                    w = (i + 1) * P
                    for k in range(2):
                        mm(PA[:, k, i * P:w], idb[:, :], mqb[:, :], start=True, stop=False, skip_group_check=True)
                    for k in range(2):
                        r = 32 * (2 * pair + k)
                        ins = mm(PA[:, k, 0:w], qs[r:r + KR, n % 2, i * P:w], ks[r:r + KR, n % 2, 0:w],
                                 start=False, stop=True, skip_group_check=True)
                    ins.then_inc(mx_ps, 1)

                def exp_scores(n, v):
                    j, pair = divmod(v, 2)
                    g = 8 * n + v
                    if g >= 2:
                        pe.wait_ge(ex_sb, g - 1)
                    elif g == 1:
                        pe.wait_ge(xT_ready, xr + SEQ)
                    w = (TPS - j) * P
                    dst_ = (PB, PC)[g % 2]
                    for k in range(2):
                        mm(dst_[:, k, 0:P], idb[:, :], mkb[:, :], start=True, stop=False, skip_group_check=True)
                    for k in range(2):
                        r = 32 * (2 * pair + k)
                        ins = mm(dst_[:, k, 0:w], ks[r:r + KM, n % 2, j * P:(j + 1) * P],
                                 qm[r:r + KM, n % 2, j * P:L], start=False, stop=True, skip_group_check=True)
                    ins.then_inc(ex_ps, 1)

                def weighted(n, v):
                    s, a = divmod(n, NG)
                    j, pair = divmod(v, 2)
                    g = 8 * n + v
                    pe.wait_ge(ex_sb, g + 1)
                    if v == 0 and n >= 1:
                        pe.wait_ge(av_sb, n)
                    for k in range(2):
                        gh = 2 * pair + k
                        for i in range(j, TPS):
                            o = (i * HG + gh) * VW
                            ins = mm(P7[:, o:o + VW], pt[:, g % 2, k, (i - j) * P:(i - j + 1) * P],
                                     va[:, s % 2, j, HG * a + gh, :], start=(v == 0 and k == 0 and i == 0),
                                     stop=j == i, skip_group_check=True)
                    ins.then_inc(av_ps, 1)

                pe.wait_ge(pad_ready, 1)
                pe.wait_ge(xT_ready, xr + SEQ)
                for n in range(items + 1):
                    if n < items:
                        stacks(n)
                    for v in range(8):
                        if n < items:
                            max_scores(n, v)
                        if n >= 1:
                            exp_scores(n - 1, v)
                            if v >= 1:
                                weighted(n - 1, v - 1)
                    if n >= 1:
                        weighted(n - 1, 7)
                    if n < items:
                        shifted_q(n)
                for t in range(NT + 1):
                    if t < NT:
                        if t % TPS == 0:
                            pe.wait_ge(av_sb, max((t // TPS + 1) * NG, items))
                        if t >= 2:
                            pe.wait_ge(ao_sb, t - 1)
                        nc.tensor.transpose((P6, P7)[t % 2][:, 0:P], xn[:, t, :], ident).then_inc(ao_ps, 1)
                    if t >= 1:
                        k = t - 1
                        pe.wait_ge(ao_sb, k + 1)
                        if k >= 2:
                            pe.wait_ge(wo_up, k - 1)
                        mm(PA[:, k % 2, 0:D], aoT[:, k % 2, :], wo[:, :], start=True, stop=False)
                        mm(PA[:, k % 2, 0:D], ones_row, bo[:, :], start=False, stop=True).then_inc(wo_ps, 1)

            pe.wait_ge(in_const, in_const_n)
            pe.wait_ge(in_ret, in_ret_n)
            for layer in range(LAYERS):
                turn(1 + 2 * layer)
                retention(layer)
                turn(2 + 2 * layer)
                feed_forward(layer)
            pe.wait_ge(in_moe, in_moe_n)
            turn(LNM1)
            experts(0)
            pe.wait_ge(in_att, in_att_n)
            turn(LNC)
            attention()
            turn(LNM2)
            experts(1)


def kernel(**inputs):
    import concourse.bacc as bacc
    from concourse.bass_utils import run_bass_kernel_spmd

    a = {k: np.asarray(v) for k, v in inputs.items()}
    const, decay = constants()
    ln = lambda s: np.ascontiguousarray(np.stack(
        [a[f"L0_attn_a_ln{1 + j}_{s}"][layer] for layer in range(LAYERS) for j in range(2)], axis=1))
    heads = lambda w: w.transpose(1, 0, 2).reshape(D, D)
    arrays = {
        "x": a["L0_attn_a_x"].reshape(NT * P, D),
        "const": const,
        "decay": decay,
        "proj_w": a["L0_attn_a_proj_w"],
        "proj_bc": a["L0_attn_a_proj_b"].reshape(LAYERS * 4, D).T,
        "proj_b": a["L0_attn_a_proj_b"],
        "reto_w": a["L0_attn_a_reto_w"],
        "reto_b": a["L0_attn_a_reto_b"],
        "lng": ln("g"),
        "lnb": ln("b"),
        "lnf": np.stack([a["L0_attn_a_lnf_g"], a["L0_attn_a_lnf_b"]]),
        "ffn1_w": a["L0_attn_a_ffn1_w"],
        "ffn1_b": a["L0_attn_a_ffn1_b"].reshape(LAYERS * FB, P).T,
        "ffn2_w": a["L0_attn_a_ffn2_w"],
        "ffn2_b": a["L0_attn_a_ffn2_b"],
        "wqkv": np.stack([heads(a[f"L0_attn_b_W{c}"]) for c in "qkv"]),
        "wo": a["L0_attn_b_Wo"].T,
        "bo": a["L0_attn_b_bo"],
        "gate_w": a["L0_ffn_gate_w"],
        "w1": a["L0_ffn_w1"],
        "w3": a["L0_ffn_w3"],
        "w2": a["L0_ffn_w2"],
    }
    nc = bacc.Bacc("TRN2", target_bir_lowering=False, num_devices=1)
    feeds, args = {}, []
    for name, v in arrays.items():
        v = np.ascontiguousarray(v)
        feeds[f"in_{name}"] = v
        args.append(nc.dram_tensor(f"in_{name}", v.shape, mybir.dt.from_np(v.dtype), kind="ExternalInput").ap())
    out = nc.dram_tensor("out", (NT * P, D), F32, kind="ExternalOutput").ap()
    mixer_kernel(nc, *args, out)
    r = run_bass_kernel_spmd(nc, [feeds], core_ids=[0])
    return r.results[0]["out"].reshape(SEQ, L, D)
```

```python
from contextlib import ExitStack

import numpy as np
import concourse.bass as bass
from concourse import mybir

ALU = mybir.AluOpType
ACT = mybir.ActivationFunctionType
F32 = mybir.dt.float32
F32R = mybir.dt.float32r
BF16 = mybir.dt.bfloat16
I32 = mybir.dt.int32
AX_X = mybir.AxisListType.X

P = 128
D = 128
NT = 16
SEQ = 4
TPS = NT // SEQ
L = TPS * P
LAYERS = 2
H = 16
HD = D // H
F = 4 * D
FB = F // P
E = 8
EPS = 1e-5
BIG = 1e30
SCALE = float(HD) ** -0.5
HG = 4
NG = H // HG
NP3 = 3
KQ = NP3 * NP3 * HD
KS = 96
QKM = HD * H


C_ID = 0
C_GQ = C_ID + P
C_GK = C_GQ + P
C_BLK = C_GK + P
C_MQ = C_BLK + P
C_MK = C_MQ + P
C_G128 = C_MK + P
C_ONES = C_G128 + 1
C_TRI = C_ONES + P
C_END = C_TRI + E * E


def constants():
    gamma = (1.0 - 2.0 ** (-5.0 - np.arange(H, dtype=np.float64)))
    gch = np.tile(gamma, HD)
    i = np.arange(P)
    c = np.zeros((P, C_END), np.float32)
    c[:, C_ID:C_ID + P] = np.eye(P)
    c[:, C_GQ:C_GQ + P] = gch[:, None] ** (i[None, :] + 1)
    c[:, C_GK:C_GK + P] = gch[None, :] ** (P - 1 - i[:, None])
    c[:, C_BLK:C_BLK + P] = (i[:, None] % H) == (i[None, :] // HD)
    c[:, C_MQ:C_MQ + P] = np.where(i[None, :] > i[:, None], -BIG, 0.0)
    c[:, C_MK:C_MK + P] = np.where(i[:, None] > i[None, :], -BIG, 0.0)
    c[:, C_G128] = gch ** P
    c[:, C_ONES:C_ONES + P] = 1.0
    e = np.arange(E)
    c[:, C_TRI:C_TRI + E * E] = (e[None, :] < e[:, None]).reshape(1, -1)
    diff = i[None, :] - i[:, None]
    decay = np.where(diff[:, None, :] >= 0, gamma[None, :, None] ** np.maximum(diff, 0)[:, None, :], 0.0)
    return c, decay.astype(np.float32).reshape(P, H * P)


LN0, LNF, LNM1, LNC, LNM2 = 0, 2 * LAYERS + 1, 2 * LAYERS + 2, 2 * LAYERS + 3, 2 * LAYERS + 4
TURNED = [n for n in range(9) if n not in (LN0, LNF)]
NV = SEQ * H // 2


def front_key(what, c):
    if what == "turn":
        return ("turn", 1 + 2 * (c // SEQ) if c < LAYERS * SEQ else LNC, c % SEQ)
    return (what, c) if what in "qk" else (what, c % SEQ)


def turn_no(n, s):
    return TURNED.index(n) * SEQ + s


def ring_plan():
    def front(layer, s):
        return [("turn", 1 + 2 * layer, s), ("q", layer * SEQ + s), ("k", layer * SEQ + s)]

    def route(m, s):
        return [("turn", (LNM1, LNM2)[m], s), ("router", m, s)]

    def att(s):
        return [("turn", LNC, s), ("q", LAYERS * SEQ + s), ("k", LAYERS * SEQ + s), ("v", s)]

    plan = front(0, 0)
    for layer in range(LAYERS):
        for s in range(SEQ):
            plan += [("xo", layer, s)] + (front(layer, s + 1) if s + 1 < SEQ else [("turn", 2 + 2 * layer, 0)])
        for s in range(SEQ):
            if s + 1 < SEQ:
                plan += [("turn", 2 + 2 * layer, s + 1)]
            else:
                plan += front(layer + 1, 0) if layer + 1 < LAYERS else route(0, 0)
    for s in range(1, SEQ):
        plan += route(0, s)
    plan += att(0) + att(1)
    for s in range(SEQ):
        plan += route(1, s)
    return {key: k for k, key in enumerate(plan)}


def pair_plan():
    plan = [("max", 0, v) for v in range(NV)] + [("mx", 0, 0)]

    def tail(s):
        return [("tr", s, 0), ("ao", s, 0), ("wo", s, 0)]

    for s in range(SEQ):
        for v in range(NV):
            plan += slot_uses(s, v)
    plan += tail(SEQ - 1)
    return {key: k for k, key in enumerate(plan)}


def slot_uses(s, v):
    out = []
    if s + 1 < SEQ and v < NV // 2:
        out += [("max", s + 1, 2 * v), ("max", s + 1, 2 * v + 1)]
    if s >= 1:
        out += {2: [("tr", s - 1, 0)], 5: [("ao", s - 1, 0)], 7: [("wo", s - 1, 0)]}.get(v, [])
    if s + 1 < SEQ and v == NV // 2 + 2:
        out += [("mx", s + 1, 0)]
    if s + 2 < SEQ and 0 <= v - (NV // 2 + 4) < 4:
        out += [(("turn", "q", "k", "v")[v - (NV // 2 + 4)], s + 2, 0)]
    return out


RING = ring_plan()
PAIR = pair_plan()


def max_unit(v):
    return TPS - 1 - v // (H // 2), v % (H // 2)


def exp_unit(v):
    return v // (H // 2), v % (H // 2)


def mixer_kernel(nc, a_x, a_const, a_decay, a_proj_w, a_proj_bc, a_kv_b, a_reto_w, a_reto_b, a_lng, a_lnb,
                 a_lnf, a_ffn1_w, a_ffn1_b, a_ffn2_w, a_ffn2_b, a_wqkv, a_wo, a_bo,
                 a_gate_w, a_w1, a_w3, a_w2, a_out):
    with ExitStack() as ctx:
        def sb(name, shape, dt=F32):
            return ctx.enter_context(nc.sbuf_tensor(name, shape, dt))

        def ps(name, shape):
            return ctx.enter_context(nc.psum_tensor(name, shape, F32))

        def sem(name):
            return ctx.enter_context(nc.semaphore(name))

        const = sb("const", [P, C_END])
        decay = sb("decay", [P, H, P])
        proj_w = sb("proj_w", [P, LAYERS, 4 * D])
        proj_bc = sb("proj_bc", [P, LAYERS, 4])
        kv_b = sb("kv_b", [P, LAYERS, 2 * D])
        reto_w = sb("reto_w", [P, LAYERS, D])
        reto_b = sb("reto_b", [1, LAYERS, D])
        lng = sb("lng", [P, 2 * LAYERS])
        lnb = sb("lnb", [P, 2 * LAYERS])
        lnf = sb("lnf", [P, 2, D])
        ffn_w = sb("ffn_w", [P, LAYERS, 2, F])
        ffn1_w = ffn_w[:, :, 0, :]
        ffn2_w = ffn_w[:, :, 1, :].rearrange("p l (f n) -> p l f n", f=FB)
        ffn1_b = sb("ffn1_b", [P, LAYERS, FB])
        ffn2_b = sb("ffn2_b", [1, LAYERS, D])
        wqkv = ffn_w[:, 1, 0, 0:3 * D].rearrange("p (c n) -> p c n", c=3)
        wo = ffn_w[:, 1, 0, 3 * D:4 * D]
        bo = sb("bo", [1, D])
        gate_w = sb("gate_w", [P, E])
        w13 = (ffn_w[:, 0, :, :], proj_w[:, :, :])
        w2 = tuple(w.rearrange("p (f n) -> p f n", f=FB)
                   for w in (ffn_w[:, 1, 1, :], kv_b[:, :, :].rearrange("p l n -> p (l n)")))
        w13h = sb("w13h", [P, 2, 2, F], F32R)
        w13l = sb("w13l", [P, 2, 2, F], F32R)

        X = sb("X", [P, NT, D])
        R = sb("R", [P, NT, D])
        xn = sb("xn", [P, NT, D])
        xT = sb("xT", [P, 2, L])
        xh = sb("xh", [P, NT * P], F32R)
        xl = sb("xl", [P, NT * P], F32R)
        st6 = sb("st6", [P, TPS, 6])
        mv = sb("mv", [P, TPS, 2])
        rs = sb("rs", [P, 3, TPS])
        pm = sb("pm", [P, 4, 8 * P])
        pt = pm[:, :, :].rearrange("p b (k n) -> p b k n", k=2)
        hT = pm[:, :, :].rearrange("p (a g) (f n) -> p a (g f) n", a=2, f=2)
        VA = 9 * HD * HG
        va = sb("va", [P, TPS, NG, VA])
        work = va[:, :, :, :].rearrange("p j a x -> p (j a x)")
        sxT = work[:, 0:2 * L].rearrange("p (a n) -> p a n", a=2)
        qgT = work[:, 2 * L:4 * L].rearrange("p (a n) -> p a n", a=2)
        vp = work[:, 4 * L:4 * L + 2 * NG * 40 * HG].rearrange("p (b a x) -> p b a x", b=2, a=NG)
        qkf = sb("qkf", [P, 2, L])
        qkt_ret = work[:, 7 * L:9 * L].rearrange("p (a n) -> p a n", a=2)
        qkt_att = R[:, 0:2 * TPS, :].rearrange("p (a i) n -> p a (i n)", a=2)
        qkp = sb("qkp", [P, NP3, 2, L], BF16)
        qst = sb("qst", [KS, 2, H * L], BF16)
        kst = sb("kst", [KS, 2, H * L], BF16)
        vs = sb("vs", [P, 2, TPS * D])
        kvb = vs[:, 0, :].rearrange("p (a n) -> p a n", a=2)
        kg = vs[:, 1, 0:2 * D].rearrange("p (a n) -> p a n", a=2)
        rgT = vs[:, 1, 2 * D:4 * D].rearrange("p (a n) -> p a n", a=2)
        dst = sb("dst", [P, D])
        state = sb("state", [P, 2, D])
        late = decay[:, :, :].rearrange("p h n -> p (h n)")
        silu_a = late[:, 2 * L:4 * L].rearrange("p (a n) -> p a n", a=2)
        aor = late[:, 0:2 * L].rearrange("p (b n) -> p b n", b=2)
        aoT = late[:, 2 * L:3 * L]
        mxT = late[0:NP3 * H, 3 * L:3 * L + L // 2].bitcast(BF16)
        mxf = late[:, 3 * L + L // 2:3 * L + L // 2 + TPS * NP3 * H].rearrange("p (i w) -> p i w", i=TPS)
        lg = sb("lg", [P, TPS, E])
        lgm = sb("lgm", [P, TPS])
        lgd = sb("lgd", [P, TPS, E])
        lge = sb("lge", [P, TPS, E])
        cgt = late[:, 0:TPS * E * E].rearrange("p (k a b) -> p k a b", k=TPS, a=E)
        cge = late[:, TPS * E * E:2 * TPS * E * E].rearrange("p (k a b) -> p k a b", k=TPS, a=E)
        rank = sb("rank", [P, TPS, E])
        wsum = sb("wsum", [P, TPS])
        wi = sb("wi", [P, NT, E])
        idb = sb("idb", [P, P], BF16)
        mqb = sb("mqb", [P, P], BF16)
        mkb = sb("mkb", [P, P], BF16)
        rmax = sb("rmax", [P, TPS, H])
        mxr = sb("mxr", [P, TPS, H])
        mxb = sb("mxb", [P, TPS, NP3, H], BF16)
        rden = sb("rden", [P, 2 * TPS * 2, HG])

        parts_dram = nc.dram_tensor("parts_dram", (2, 5, 2, P, L), BF16, kind="Internal").ap()
        max_dram = nc.dram_tensor("max_dram", (2, NP3 * H, L), BF16, kind="Internal").ap()

        PA = ps("PA", [P, 2, 512])
        PB = ps("PB", [P, 2, 512])
        PC = ps("PC", [P, 2, 512])
        P6 = ps("P6", [P, 512])
        P7 = ps("P7", [P, 512])
        ring_bank = (P6, P7)

        ident = const[:, C_ID:C_ID + P]
        ones_row = const[0:1, C_ONES:C_ONES + P]

        in_x = [sem(f"in_x{s}") for s in range(SEQ)]
        in_const = sem("in_const")
        in_decay = sem("in_decay")
        in_ret = sem("in_ret")
        in_att = sem("in_att")
        in_w13 = (sem("in_w13a"), sem("in_w13b"))
        in_w2 = (sem("in_w2a"), sem("in_w2b"))
        out_done = sem("out_done")
        filled = sem("filled")
        k_ones = sem("k_ones")
        parts_out = sem("parts_out")
        st_in = (sem("st_ina"), sem("st_inb"))
        max_out = sem("max_out")
        max_in = sem("max_in")
        v_chain = sem("v_chain")
        xn_ready = sem("xn_ready")
        ring_ps = sem("ring_ps")
        ring_sb = sem("ring_sb")
        pair_ps = sem("pair_ps")
        pair_sb = sem("pair_sb")
        xl_ready = sem("xl_ready")
        qt_sb = sem("qt_sb")
        q2_sb = sem("q2_sb")
        q3_sb = sem("q3_sb")
        qg_sb = sem("qg_sb")
        kv_ps = sem("kv_ps")
        kv_sb = sem("kv_sb")
        vp_sb = sem("vp_sb")
        kg_sb = sem("kg_sb")
        sc_ps = sem("sc_ps")
        pm_sb = sem("pm_sb")
        re_ps = sem("re_ps")
        rg_sb = sem("rg_sb")
        state_sb = sem("state_sb")
        ro_ps = sem("ro_ps")
        ro_up = sem("ro_up")
        f1_ps = sem("f1_ps")
        f1_sb = sem("f1_sb")
        f2_ps = sem("f2_ps")
        f2_up = sem("f2_up")
        lg_d = sem("lg_d")
        routed = sem("routed")
        va_zero = sem("va_zero")
        lg_e = sem("lg_e")
        w_hi = sem("w_hi")
        w_lo = sem("w_lo")
        m1_ps = sem("m1_ps")
        m1_si = sem("m1_si")
        m1_sb = sem("m1_sb")
        m2_ps = sem("m2_ps")
        m2_up = sem("m2_up")
        att_const = sem("att_const")
        va_sb = sem("va_sb")
        mx_sb = sem("mx_sb")
        ex_ps = sem("ex_ps")
        ex_sb = sem("ex_sb")
        av_ps = sem("av_ps")
        ao_raw = sem("ao_raw")

        in_ret_n, in_att_n = 15 * 16, 2 * 16

        block = ctx.enter_context(nc.Block())
        A = LAYERS * SEQ

        def wait_ring(eng, *key):
            eng.wait_ge(ring_sb, RING[key] + 1)

        def wait_front(eng, what, c):
            if c >= A + 2:
                eng.wait_ge(pair_sb, PAIR[(what, c - A, 0)] + 1)
            else:
                wait_ring(eng, *front_key(what, c))

        @block.sync
        def _(sp):
            x_t = a_x.rearrange("(t p) d -> p t d", p=P)
            for s in range(SEQ):
                sp.dma_start(X[:, TPS * s:TPS * s + TPS, :], x_t[:, TPS * s:TPS * s + TPS, :]).then_inc(in_x[s], 16)
                if s == 0:
                    sp.dma_start(const[:, :], a_const).then_inc(in_const, 16)
            sp.dma_start(lng[:, :], a_lng).then_inc(in_ret, 16)
            sp.dma_start(lnb[:, :], a_lnb).then_inc(in_ret, 16)
            sp.dma_start(proj_bc[:, :, :], a_proj_bc.rearrange("p (l c) -> p l c", l=LAYERS)).then_inc(in_ret, 16)
            sp.dma_start(proj_w[:, :, :], a_proj_w.rearrange("l d n -> d l n")).then_inc(in_ret, 16)
            sp.dma_start(kv_b[:, :, :], a_kv_b.partition_broadcast(P)).then_inc(in_ret, 16)
            sp.dma_start(reto_w[:, :, :], a_reto_w.rearrange("l d n -> d l n")).then_inc(in_ret, 16)
            sp.dma_start(reto_b[:, :, :], a_reto_b.rearrange("(a l) n -> a l n", a=1)).then_inc(in_ret, 16)
            sp.dma_start(lnf[:, :, :], a_lnf.partition_broadcast(P)).then_inc(in_ret, 16)
            sp.dma_start(ffn1_w, a_ffn1_w.rearrange("l d n -> d l n")).then_inc(in_ret, 16)
            sp.dma_start(ffn1_b[:, :, :], a_ffn1_b.rearrange("p (l f) -> p l f", l=LAYERS)).then_inc(in_ret, 16)
            for layer in range(LAYERS):
                sp.dma_start(ffn2_w[:, layer, :, :],
                             a_ffn2_w[layer].rearrange("(f p) n -> p f n", p=P)).then_inc(in_ret, 16)
            sp.dma_start(ffn2_b[:, :, :], a_ffn2_b.rearrange("(a l) n -> a l n", a=1)).then_inc(in_ret, 16)
            sp.dma_start(gate_w[:, :], a_gate_w).then_inc(in_ret, 16)
            sp.dma_start(bo[:, :], a_bo.rearrange("(a n) -> a n", a=1)).then_inc(in_ret, 16)
            sp.dma_start(decay[:, :, :], a_decay.rearrange("p (h n) -> p h n", h=H)).then_inc(in_decay, 16)
            sp.wait_ge(filled, 2)
            ones = pm[0:NP3, :, :].rearrange("p b n -> p (b n)").bitcast(BF16)
            for b in range(2):
                sp.dma_start(kst[KQ:KQ + NP3, b, :], ones).then_inc(k_ones, 16)

            def stacks(c):
                b = c % 2
                sp.wait_ge(q3_sb, c + 1)
                if c >= 2:
                    sp.wait_ge(st_in[b], 7 * 16 * (c // 2))
                sp.dma_start(parts_dram[b, 0:NP3].rearrange("i q p n -> p (i q) n"),
                             qkp[:, :, :, :].rearrange("p i q n -> p (i q) n")).then_inc(parts_out, 16)
                sp.dma_start(parts_dram[b, NP3:5, 1].rearrange("i p n -> p i n"),
                             qkp[:, 0:2, 1, :]).then_inc(parts_out, 16)
                sp.wait_ge(parts_out, 32 * (c + 1))
                if 2 <= c < LAYERS * SEQ + 2:
                    sp.wait_ge(sc_ps, 2 * TPS * (c - 1))
                if c >= LAYERS * SEQ + 2:
                    sp.wait_ge(ex_ps, NV * (c - 1 - LAYERS * SEQ))
                for u in range(NP3):
                    r = slice(NP3 * HD * u, NP3 * HD * (u + 1))
                    q = parts_dram[b, 0:NP3, 0].rearrange("i (k h) n -> i k (h n)", h=H)
                    k = parts_dram[b, u:u + NP3, 1].rearrange("i (k h) n -> i k (h n)", h=H)
                    sp.dma_start(qst[r, b, :], q).then_inc(st_in[b], 16)
                    sp.dma_start(kst[r, b, :], k).then_inc(st_in[b], 16)
                sp.dma_start(qst[KQ:KQ + NP3, b, :], qst[KQ + 8:KQ + 8 + NP3, b, :]).then_inc(st_in[b], 16)

            def expert_w13(m, e):
                n = m * E + e
                if n >= 2:
                    sp.wait_ge(w_lo, n - 1)
                    sp.wait_ge(w_hi, n - 1)
                sp.dma_start(w13[n % 2][:, 0, :], a_w1[e]).then_inc(in_w13[n % 2], 16)
                sp.dma_start(w13[n % 2][:, 1, :], a_w3[e]).then_inc(in_w13[n % 2], 16)

            def expert_w2(m, e):
                n = m * E + e
                if n >= 2:
                    sp.wait_ge(m2_ps, SEQ * (n - 1))
                sp.dma_start(w2[n % 2], a_w2[e].rearrange("(f p) d -> p f d", p=P)).then_inc(in_w2[n % 2], 16)

            def maxima(s):
                b = s % 2
                sp.wait_ge(pair_sb, PAIR[("mx", s, 0)] + 1)
                if s >= 2:
                    sp.wait_ge(max_in, 16 * (s - 1))
                sp.dma_start(max_dram[b], mxT).then_inc(max_out, 16)
                sp.wait_ge(max_out, 16 * (s + 1))
                sp.dma_start(qst[KQ:KQ + NP3, b, :], max_dram[b].rearrange("(i h) n -> i (h n)", h=H)
                             ).then_inc(max_in, 16)

            for c in range(LAYERS * SEQ):
                stacks(c)
                if c == SEQ:
                    sp.wait_ge(f2_ps, NT)
                    expert_w13(0, 0)
            sp.wait_ge(kv_ps, LAYERS * NT)
            expert_w13(0, 1)
            sp.wait_ge(f2_ps, LAYERS * NT)
            expert_w2(0, 0)
            sp.wait_ge(kv_sb, LAYERS * NT)
            expert_w2(0, 1)
            sp.dma_start(wqkv, a_wqkv.rearrange("c d n -> d c n")).then_inc(in_att, 16)
            sp.dma_start(wo, a_wo).then_inc(in_att, 16)
            for e in range(2, E):
                expert_w13(0, e)
                expert_w2(0, e)
            expert_w13(1, 0)
            expert_w13(1, 1)
            stacks(A)
            stacks(A + 1)
            expert_w2(1, 0)
            expert_w2(1, 1)
            maxima(0)
            for s in range(1, SEQ):
                maxima(s)
                if s + 1 < SEQ:
                    stacks(A + s + 1)
            for e in range(2, E):
                expert_w13(1, e)
                expert_w2(1, e)
            o_t = a_out.rearrange("(t p) d -> p t d", p=P)
            for s in range(SEQ):
                sp.wait_ge(m2_up, 2 * SEQ * E - SEQ + s + 1)
                sp.dma_start(o_t[:, TPS * s:TPS * s + TPS, :], X[:, TPS * s:TPS * s + TPS, :]).then_inc(out_done, 16)
            sp.wait_ge(out_done, 16 * SEQ)

        @block.gpsimd
        def _(pool):
            ones = pm[0:NP3, :, :].rearrange("p b n -> p (b n)").bitcast(BF16)
            nc.gpsimd.memset(ones, 1.0).then_inc(filled, 1)
            pool.wait_ge(filled, 1)
            for b in range(2):
                nc.gpsimd.memset(kst[64:KS, b, :].bitcast(F32), 0.0)
                ins = nc.gpsimd.memset(qst[64:KS, b, :].bitcast(F32), 0.0)
            ins.then_inc(filled, 1)
            pool.wait_ge(filled, 2)
            nc.gpsimd.memset(vp, 0.0).then_inc(filled, 1)

            def part_rests(c):
                wait_front(pool, "k", c)
                qkt = qkt_ret if c < A else qkt_att
                nc.gpsimd.tensor_tensor(qkt, qkf[:, :, :], qkp[:, 0, :, :], ALU.subtract).then_inc(qt_sb, 1)
                pool.wait_ge(q2_sb, c + 1)
                nc.gpsimd.tensor_tensor(qkp[:, 2, :, :], qkt, qkp[:, 1, :, :],
                                        ALU.subtract).then_inc(q3_sb, 1)

            def decay_k(g):
                pool.wait_ge(kv_sb, g + 1)
                if g >= 2:
                    pool.wait_ge(re_ps, g - 1)
                nc.gpsimd.tensor_tensor(kg[:, g % 2, :], kvb[:, g % 2, 0:D], const[:, C_GK:C_GK + P],
                                        ALU.mult).then_inc(kg_sb, 1)

            def low_input(m, s):
                k = m * SEQ + s
                t = turn_no((LNM1, LNM2)[m], s)
                wait_ring(pool, "turn", (LNM1, LNM2)[m], s)
                nc.gpsimd.tensor_tensor(xl[:, s * L:(s + 1) * L], xT[:, t % 2, :],
                                        xh[:, s * L:(s + 1) * L].bitcast(F32), ALU.subtract).then_inc(xl_ready, 1)

            def low_weights(n):
                pool.wait_ge(in_w13[n % 2], 32 * (n // 2 + 1))
                pool.wait_ge(w_hi, n + 1)
                if n >= 2:
                    pool.wait_ge(m1_ps, SEQ * FB * (n - 1))
                nc.gpsimd.tensor_tensor(w13l[:, n % 2, :, :], w13[n % 2],
                                        w13h[:, n % 2, :, :].bitcast(F32), ALU.subtract).then_inc(w_lo, 1)

            pool.wait_ge(in_const, 16)
            part_rests(0)
            for layer in range(LAYERS):
                for s in range(SEQ):
                    decay_k(layer * NT + s * TPS)
                    if s + 1 < SEQ:
                        part_rests(layer * SEQ + s + 1)
                    for k in range(1, TPS):
                        decay_k(layer * NT + s * TPS + k)
                if layer + 1 < LAYERS:
                    part_rests((layer + 1) * SEQ)
            low_weights(0)
            pool.wait_ge(rg_sb, LAYERS * NT)
            pool.wait_ge(re_ps, LAYERS * NT)
            nc.gpsimd.memset(va[:, :, :, :], 0.0).then_inc(va_zero, 1)
            pool.wait_ge(va_zero, 1)
            for j in range(TPS):
                ins = nc.gpsimd.memset(
                    va[:, j, :, 0:HG * 65].rearrange("p a (g r) -> p a g r", g=HG)[:, :, :, HG * HD], 1.0)
            ins.then_inc(va_zero, 1)
            for m in range(2):
                for s in range(SEQ):
                    low_input(m, s)
                for n in range(m * E + 1, min((m + 1) * E + 1, 2 * E)):
                    low_weights(n)
                if m == 0:
                    part_rests(A)
                    part_rests(A + 1)
                    for s in range(2, SEQ):
                        part_rests(A + s)

        @block.vector
        def _(dve):
            chain = [0]

            def link(ins):
                chain[0] += 1
                ins.then_inc(v_chain, 1)
                dve.wait_ge(v_chain, chain[0])

            def bc(ap, shape, axis):
                return ap.unsqueeze(axis).to_broadcast(shape)

            def norm(n, s, src, out):
                for k in range(TPS):
                    ins = nc.vector.bn_stats(st6[:, k, :], src[:, TPS * s + k, :])
                link(ins)
                for k in range(TPS):
                    ins = nc.vector.bn_aggr(mv[:, k, :], st6[:, k, :])
                link(ins)
                v, y, z = rs[:, 0, :], rs[:, 1, :], rs[:, 2, :]
                link(nc.vector.tensor_scalar(v, mv[:, :, 1], EPS, None, ALU.add))
                link(nc.vector.tensor_scalar(y.bitcast(I32), v.bitcast(I32), 1, None, ALU.logical_shift_right))
                link(nc.vector.tensor_scalar(y.bitcast(I32), y.bitcast(I32), -1.0, float(0x5f3759df),
                                             ALU.mult, ALU.add))
                for _ in range(4):
                    link(nc.vector.tensor_tensor(z, y, y, ALU.mult))
                    link(nc.vector.scalar_tensor_tensor(out=z, in0=z, scalar=-0.5, in1=v, op0=ALU.mult,
                                                        op1=ALU.mult))
                    link(nc.vector.scalar_tensor_tensor(out=y, in0=z, scalar=1.5, in1=y, op0=ALU.add,
                                                        op1=ALU.mult))
                for k in range(TPS):
                    t = TPS * s + k
                    ins = nc.vector.tensor_scalar(out[:, t, :], src[:, t, :], mv[:, k, 0:1], y[:, k:k + 1],
                                                  ALU.subtract, ALU.mult)
                if n in TURNED:
                    ins.then_inc(xn_ready, 1)
                else:
                    link(ins)

            def retention(layer):
                def keys_values(t):
                    g = layer * NT + t
                    dve.wait_ge(kv_ps, g + 1)
                    if g >= 2:
                        dve.wait_ge(re_ps, g - 1)
                        dve.wait_ge(kg_sb, g - 1)
                    nc.vector.tensor_tensor(kvb[:, g % 2, :], PC[:, 0, 0:2 * D], kv_b[:, layer, :],
                                            ALU.add).then_inc(kv_sb, 1)
                    dve.wait_ge(kv_sb, g + 1)
                    nc.vector.tensor_copy(
                        vp[:, g % 2, :, :].rearrange("p a (g r) -> p a g r", g=HG)[:, :, :, 0:HD],
                        kvb[:, g % 2, D:2 * D].rearrange("p (a g k) -> p a g k", a=NG, g=HG)).then_inc(vp_sb, 1)

                def decay_q(s):
                    c = layer * SEQ + s
                    wait_front(dve, "q", c)
                    nc.vector.tensor_tensor(
                        qgT[:, c % 2, :].rearrange("p (t n) -> p t n", t=TPS),
                        qkf[:, 0, :].rearrange("p (t n) -> p t n", t=TPS),
                        bc(const[:, C_GQ:C_GQ + P], [P, TPS, P], 1), ALU.mult).then_inc(qg_sb, 1)

                def decay_scores(t, u):
                    g = layer * NT + t
                    dve.wait_ge(sc_ps, 2 * g + u + 1)
                    src = PA if u == 0 else PB
                    nc.vector.tensor_tensor(pm[:, 2 * (g % 2) + u, :],
                                            src[:, :, :].rearrange("p b n -> p (b n)"),
                                            decay[:, 8 * u:8 * u + 8, :].rearrange("p h n -> p (h n)"),
                                            ALU.mult).then_inc(pm_sb, 1)

                def gate(t):
                    g = layer * NT + t
                    c = g // TPS
                    dve.wait_ge(re_ps, g + 1)
                    wait_ring(dve, "xo", layer, t // TPS)
                    if g >= 2:
                        dve.wait_ge(ro_ps, g - 1)
                    nc.vector.tensor_tensor(rgT[:, g % 2, :], PC[:, 1, 0:P],
                                            sxT[:, c % 2, (t % TPS) * P:(t % TPS + 1) * P],
                                            ALU.mult).then_inc(rg_sb, 1)
                    if t % TPS < TPS - 1:
                        link(nc.vector.tensor_tensor(dst[:, :], PC[:, 1, P:2 * P], const[:, C_BLK:C_BLK + P],
                                                     ALU.mult))
                        if t % TPS == 0:
                            ins = nc.vector.tensor_copy(state[:, g % 2, :], dst[:, :])
                        else:
                            ins = nc.vector.scalar_tensor_tensor(
                                out=state[:, g % 2, :], in0=state[:, (g - 1) % 2, :],
                                scalar=const[:, C_G128:C_G128 + 1], in1=dst[:, :], op0=ALU.mult, op1=ALU.add)
                        ins.then_inc(state_sb, 1)
                        dve.wait_ge(state_sb, c * (TPS - 1) + t % TPS + 1)

                def add_out(t):
                    g = layer * NT + t
                    dve.wait_ge(ro_ps, g + 1)
                    nc.vector.tensor_tensor(R[:, t, :], PC[:, 1, 0:D], R[:, t, :], ALU.add).then_inc(ro_up, 1)
                    if t % TPS == TPS - 1:
                        dve.wait_ge(ro_up, g + 1)
                        norm(2 + 2 * layer, t // TPS, R, xn)

                for t in range(NT + 2):
                    if t < NT:
                        keys_values(t)
                        if t % TPS == 0:
                            decay_q(t // TPS)
                        decay_scores(t, 0)
                    if t >= 2:
                        add_out(t - 2)
                    if t < NT:
                        decay_scores(t, 1)
                    if 1 <= t < NT + 1:
                        gate(t - 1)

            def feed_forward(layer):
                for t in range(NT):
                    g = layer * NT + t
                    dve.wait_ge(f2_ps, g + 1)
                    nc.vector.tensor_tensor(R[:, t, :], PC[:, g % 2, 0:D], R[:, t, :], ALU.add).then_inc(f2_up, 1)
                    if t % TPS == TPS - 1:
                        s = t // TPS
                        dve.wait_ge(f2_up, g + 1)
                        if layer + 1 < LAYERS:
                            norm(3 + 2 * layer, s, R, xn)
                        else:
                            leave_blocks(s)

            def leave_blocks(s):
                norm(LNF, s, R, xn)
                r = slice(TPS * s, TPS * s + TPS)
                link(nc.vector.tensor_tensor(xn[:, r, :], xn[:, r, :], bc(lnf[:, 0, :], [P, TPS, D], 1), ALU.mult))
                link(nc.vector.tensor_tensor(xn[:, r, :], xn[:, r, :], bc(lnf[:, 1, :], [P, TPS, D], 1), ALU.add))
                link(nc.vector.tensor_tensor(X[:, r, :], X[:, r, :], xn[:, r, :], ALU.add))
                norm(LNM1, s, X, xn)

            def route(m, s):
                c = m * SEQ + s
                wait_ring(dve, "router", m, s)
                link(nc.vector.tensor_reduce(lgm[:, :], lg[:, :, :], AX_X, ALU.max))
                nc.vector.tensor_tensor(lgd[:, :, :], lg[:, :, :], bc(lgm[:, :], [P, TPS, E], 2),
                                        ALU.subtract).then_inc(lg_d, 1)
                for k in range(TPS):
                    for o, op in ((cgt, ALU.is_gt), (cge, ALU.is_ge)):
                        ins = nc.vector.tensor_tensor(o[:, k, :, :], bc(lg[:, k, :], [P, E, E], 1),
                                                      bc(lg[:, k, :], [P, E, E], 2), op)
                link(ins)
                flat = cge.rearrange("p k a b -> p k (a b)")
                link(nc.vector.tensor_tensor(flat, flat, bc(const[:, C_TRI:C_TRI + E * E], [P, TPS, E * E], 1),
                                             ALU.mult))
                link(nc.vector.tensor_tensor(cgt, cgt, cge, ALU.max))
                nc.vector.tensor_reduce(rank[:, :, :], cgt, AX_X, ALU.add).then_inc(routed, 1)
                dve.wait_ge(routed, c + 1)
                dve.wait_ge(lg_e, c + 1)
                w = wi[:, TPS * s:TPS * s + TPS, :]
                link(nc.vector.scalar_tensor_tensor(out=w, in0=rank[:, :, :], scalar=2.0, in1=lge[:, :, :],
                                                    op0=ALU.is_lt, op1=ALU.mult))
                link(nc.vector.tensor_reduce(wsum[:, :], w, AX_X, ALU.add))
                link(nc.vector.reciprocal(wsum[:, :], wsum[:, :]))
                link(nc.vector.tensor_tensor(w, w, bc(wsum[:, :], [P, TPS, E], 2), ALU.mult))

            def round_weights(n):
                dve.wait_ge(in_w13[n % 2], 32 * (n // 2 + 1))
                if n >= 2:
                    dve.wait_ge(m1_ps, SEQ * FB * (n - 1))
                    dve.wait_ge(w_lo, n - 1)
                nc.vector.tensor_copy(w13h[:, n % 2, :, :], w13[n % 2]).then_inc(w_hi, 1)

            def experts(m):
                def add_expert(e, s):
                    b = (m * E + e) * SEQ + s
                    dve.wait_ge(m2_ps, b + 1)
                    if e >= 1:
                        dve.wait_ge(m2_up, b - SEQ + 1)
                    for k in range(TPS):
                        t = TPS * s + k
                        ins = nc.vector.scalar_tensor_tensor(
                            out=X[:, t, :], in0=PC[:, b % 2, k * D:(k + 1) * D], scalar=wi[:, t, e:e + 1],
                            in1=X[:, t, :], op0=ALU.mult, op1=ALU.add)
                    ins.then_inc(m2_up, 1)
                    if e == E - 1 and m == 0:
                        dve.wait_ge(m2_up, b + 1)
                        norm(LNC, s, X, xn)

                route(m, 0)
                prev = None
                for e in range(E):
                    for s in range(SEQ):
                        b = (m * E + e) * SEQ + s
                        for f in range(FB):
                            g = b * FB + f
                            dve.wait_ge(m1_si, g + 1)
                            if f == 0 and b >= 2:
                                dve.wait_ge(m2_ps, b - 1)
                            nc.vector.tensor_tensor(hT[:, b % 2, f, :], silu_a[:, g % 2, :],
                                                    PB[:, g % 2, :], ALU.mult).then_inc(m1_sb, 1)
                            if f == 1 and prev is not None:
                                add_expert(*prev)
                        prev = (e, s)
                        if e == 0 and s + 1 < SEQ:
                            route(m, s + 1)
                        if s == 1 and m * E + e + 1 < 2 * E:
                            round_weights(m * E + e + 1)
                add_expert(*prev)

            def attention():

                def spread_values(s):
                    wait_front(dve, "v", A + s)
                    dve.wait_ge(va_zero, 2)
                    if s >= 1:
                        dve.wait_ge(av_ps, NV * s)
                    for j in range(TPS):
                        ins = nc.vector.tensor_copy(
                            va[:, j, :, :].rearrange("p a (g r) -> p a g r", g=HG)[:, :, :, 0:HD],
                            vs[:, s % 2, j * D:(j + 1) * D].rearrange("p (a g k) -> p a g k", a=NG, g=HG))
                    ins.then_inc(va_sb, 1)

                def row_max(s, v):
                    i, pair = max_unit(v)
                    dve.wait_ge(pair_ps, PAIR[("max", s, v)] + 1)
                    if v == 0 and s >= 1:
                        dve.wait_ge(mx_sb, s)
                    nc.vector.tensor_reduce(rmax[:, i, 2 * pair:2 * pair + 2], PA[:, :, 0:(i + 1) * P],
                                            AX_X, ALU.max).then_inc(pair_sb, 1)

                def minus_max(s):
                    dve.wait_ge(pair_sb, PAIR[("max", s, NV - 1)] + 1)
                    if s >= 1:
                        dve.wait_ge(pair_sb, PAIR[("mx", s - 1, 0)] + 1)
                    link(nc.vector.tensor_scalar(mxb[:, :, 0, :], rmax[:, :, :], -1.0, None, ALU.mult))
                    link(nc.vector.scalar_tensor_tensor(out=mxr[:, :, :], in0=rmax[:, :, :], scalar=-1.0,
                                                        in1=mxb[:, :, 0, :], op0=ALU.mult, op1=ALU.subtract))
                    link(nc.vector.tensor_copy(mxb[:, :, 1, :], mxr[:, :, :]))
                    link(nc.vector.tensor_tensor(mxb[:, :, 2, :], mxr[:, :, :], mxb[:, :, 1, :], ALU.subtract))
                    nc.vector.tensor_copy(mxf.rearrange("p i (w h) -> p i w h", w=NP3),
                                          mxb[:, :, :, :]).then_inc(mx_sb, 1)

                def weigh(s):
                    dve.wait_ge(pair_ps, PAIR[("tr", s, 0)] + 1)
                    o = PA[:, :, :].rearrange("p b (i c x) -> p (b i c) x", i=TPS, c=2)
                    link(nc.vector.reciprocal(rden[:, :, :], o[:, :, HG * HD:HG * HD + HG]))
                    rd = rden[:, :, :].rearrange("p (b i c) g -> p b i c g", b=2, i=TPS)
                    for b in range(2):
                        for c in range(2):
                            a = 2 * b + c
                            ins = nc.vector.tensor_tensor(
                                xn[:, TPS * s:TPS * s + TPS, HG * HD * a:HG * HD * (a + 1)].rearrange(
                                    "p i (g k) -> p i g k", g=HG),
                                PA[:, b, :].rearrange("p (i c g k) -> p i c g k", i=TPS, c=2, k=HD)[:, :, c, 0:HG, :],
                                bc(rd[:, b, :, c, :], [P, TPS, HG, HD], 3), ALU.mult)
                    ins.then_inc(pair_sb, 1)

                def add_out(s):
                    dve.wait_ge(pair_ps, PAIR[("wo", s, 0)] + 1)
                    r = slice(TPS * s, TPS * s + TPS)
                    nc.vector.tensor_tensor(X[:, r, :], PA[:, 0, :].rearrange("p (i n) -> p i n", i=TPS), X[:, r, :],
                                            ALU.add).then_inc(pair_sb, 1)
                    dve.wait_ge(pair_sb, PAIR[("wo", s, 0)] + 1)
                    norm(LNM2, s, X, xn)

                for v in range(NV):
                    row_max(0, v)
                minus_max(0)
                for s in range(SEQ):
                    spread_values(s)
                    for v in range(NV):
                        for what, s_, v_ in slot_uses(s, v):
                            if what == "max":
                                row_max(s_, v_)
                            if what == "tr":
                                weigh(s_)
                            if what == "wo":
                                add_out(s_)
                        if v == NV // 2 - 1 and s + 1 < SEQ:
                            minus_max(s + 1)
                weigh(SEQ - 1)
                add_out(SEQ - 1)

            dve.wait_ge(in_const, 16)
            for s in range(SEQ):
                dve.wait_ge(in_x[s], 16)
                norm(LN0, s, X, R)
                norm(1, s, R, xn)
            dve.wait_ge(in_ret, in_ret_n)
            dve.wait_ge(in_decay, 16)
            dve.wait_ge(filled, 3)
            dve.wait_ge(k_ones, 32)
            for layer in range(LAYERS):
                retention(layer)
                if layer == LAYERS - 1:
                    round_weights(0)
                if layer == 0:
                    for t_, src in ((idb, C_ID), (mqb, C_MQ), (mkb, C_MK)):
                        ins = nc.vector.tensor_copy(t_[:, :], const[:, src:src + P])
                    ins.then_inc(att_const, 1)
                feed_forward(layer)
            experts(0)
            attention()
            experts(1)


        @block.scalar
        def _(act):
            def ring(*key):
                act.wait_ge(ring_ps, RING[key] + 1)
                return ring_bank[RING[key] % 2][:, :]

            def pair(*key):
                act.wait_ge(pair_ps, PAIR[key] + 1)
                return PA

            def turn(n, s, src):
                dst_ = xT[:, turn_no(n, s) % 2, :]
                if n in (LNM1, LNM2):
                    if s >= 2:
                        act.wait_ge(xl_ready, (n == LNM2) * SEQ + s - 1)
                    nc.scalar.activation(dst_, src, ACT.Copy)
                    return nc.scalar.activation(xh[:, s * L:(s + 1) * L], src, ACT.Copy)
                if n == LNC:
                    act.wait_ge(xl_ready, SEQ)
                    return nc.scalar.activation(dst_, src, ACT.Copy)
                return nc.scalar.activation(dst_, src, ACT.Identity, bias=lnb[:, n - 1:n], scale=lng[:, n - 1:n])

            def first_part(c, which, src):
                if c >= 1 and which == 0:
                    act.wait_ge(parts_out, 32 * c)
                    act.wait_ge(qt_sb, c)
                    act.wait_ge(qg_sb, min(c, A))
                for o in (qkf[:, which, :], qkp[:, 0, which, :]):
                    if c < A:
                        ins = nc.scalar.activation(o, src, ACT.Identity, bias=proj_bc[:, c // SEQ, which:which + 1])
                    else:
                        ins = nc.scalar.activation(o, src, ACT.Copy)
                return ins

            def second_part(c):
                act.wait_ge(qt_sb, c + 1)
                nc.scalar.activation(qkp[:, 1, :, :], qkt_ret if c < A else qkt_att, ACT.Copy).then_inc(q2_sb, 1)

            def front(c):
                key = front_key("turn", c)
                turn(key[1], key[2], ring(*key)).then_inc(ring_sb, 1)
                first_part(c, 0, ring("q", c)).then_inc(ring_sb, 1)
                first_part(c, 1, ring("k", c)).then_inc(ring_sb, 1)
                if c >= A:
                    values(c - A, ring("v", c - A)).then_inc(ring_sb, 1)
                second_part(c)

            def values(s, src):
                if s >= 2:
                    act.wait_ge(va_sb, s - 1)
                return nc.scalar.activation(vs[:, s % 2, :], src, ACT.Copy)

            def plain_turn(n, s):
                turn(n, s, ring("turn", n, s)).then_inc(ring_sb, 1)

            def logits(m, s):
                c = m * SEQ + s
                plain_turn((LNM1, LNM2)[m], s)
                src = ring("router", m, s)
                if c >= 1:
                    act.wait_ge(routed, c)
                nc.scalar.activation(lg[:, :, :].rearrange("p k e -> p (k e)"), src[:, 0:TPS * E],
                                     ACT.Copy).then_inc(ring_sb, 1)

            def exp_logits(m, s):
                act.wait_ge(lg_d, m * SEQ + s + 1)
                nc.scalar.activation(lge[:, :, :], lgd[:, :, :], ACT.Exp).then_inc(lg_e, 1)

            def retention(layer):
                for s in range(SEQ):
                    c = layer * SEQ + s
                    nc.scalar.activation(sxT[:, c % 2, :], ring("xo", layer, s), ACT.Silu,
                                         bias=proj_bc[:, layer, 3:4]).then_inc(ring_sb, 1)
                    if s + 1 < SEQ:
                        front(c + 1)
                    else:
                        plain_turn(2 + 2 * layer, 0)

            def feed_forward(layer):
                for s in range(SEQ):
                    b = layer * SEQ + s
                    for f in range(FB):
                        act.wait_ge(f1_ps, b * FB + f + 1)
                        if f == 0 and b >= 2:
                            act.wait_ge(f2_ps, (b - 1) * TPS)
                        src = (PA, PB)[f // 2][:, f % 2, :]
                        nc.scalar.activation(hT[:, b % 2, f, :], src, ACT.Gelu,
                                             bias=ffn1_b[:, layer, f:f + 1]).then_inc(f1_sb, 1)
                    if s + 1 < SEQ:
                        plain_turn(2 + 2 * layer, s + 1)
                    elif layer + 1 < LAYERS:
                        front((layer + 1) * SEQ)
                    else:
                        logits(0, 0)

            def experts(m):
                exp_logits(m, 0)
                for e in range(E):
                    for s in range(SEQ):
                        for f in range(FB):
                            g = ((m * E + e) * SEQ + s) * FB + f
                            act.wait_ge(m1_ps, g + 1)
                            if g >= 2:
                                act.wait_ge(m1_sb, g - 1)
                            nc.scalar.activation(silu_a[:, g % 2, :], PA[:, g % 2, :], ACT.Silu).then_inc(m1_si, 1)
                            if e == 0 and s + 1 < SEQ and f == 1:
                                logits(m, s + 1)
                        if e == 0 and s + 1 < SEQ:
                            exp_logits(m, s + 1)
                if m == 0:
                    front(A)
                    front(A + 1)

            def attention():
                def turn_max(s):
                    src = pair("mx", s, 0)
                    if s >= 1:
                        act.wait_ge(max_out, 16 * s)
                    nc.scalar.activation(mxT, src[0:NP3 * H, 0, :], ACT.Copy).then_inc(pair_sb, 1)

                def weighted_out(s):
                    act.wait_ge(av_ps, NV * (s + 1))
                    if s >= 1:
                        act.wait_ge(pair_ps, PAIR[("tr", s - 1, 0)] + 1)
                    nc.scalar.activation(aor[:, 0, :], P6[:, :], ACT.Copy)
                    nc.scalar.activation(aor[:, 1, :], P7[:, :], ACT.Copy).then_inc(ao_raw, 1)

                def turn_out(s):
                    nc.scalar.activation(aoT, pair("ao", s, 0)[:, 0, :], ACT.Copy).then_inc(pair_sb, 1)

                def exps(s, v):
                    u = NV * s + v
                    j, _ = exp_unit(v)
                    act.wait_ge(ex_ps, u + 1)
                    if u >= 4:
                        act.wait_ge(av_ps, u - 3)
                    w = (TPS - j) * P
                    nc.scalar.activation(pt[:, u % 4, :, 0:w], (PB, PC)[u % 2][:, :, 0:w], ACT.Exp,
                                         scale=SCALE).then_inc(ex_sb, 1)

                turn_max(0)
                for s in range(SEQ):
                    for v in range(NV):
                        if v == 0 and s >= 1:
                            weighted_out(s - 1)
                        exps(s, v)
                        for what, s_, _ in slot_uses(s, v):
                            c = A + s_
                            if what == "turn":
                                turn(LNC, s_, pair("turn", s_, 0)[:, 0, :]).then_inc(pair_sb, 1)
                            if what == "q":
                                first_part(c, 0, pair("q", s_, 0)[:, 0, :]).then_inc(pair_sb, 1)
                            if what == "k":
                                first_part(c, 1, pair("k", s_, 0)[:, 0, :]).then_inc(pair_sb, 1)
                            if what == "v":
                                values(s_, pair("v", s_, 0)[:, 0, :]).then_inc(pair_sb, 1)
                                second_part(c)
                            if what == "mx":
                                turn_max(s_)
                            if what == "ao":
                                turn_out(s_)
                weighted_out(SEQ - 1)
                turn_out(SEQ - 1)

            act.wait_ge(in_const, 16)
            act.wait_ge(in_ret, in_ret_n)
            act.wait_ge(k_ones, 32)
            front(0)
            for layer in range(LAYERS):
                retention(layer)
                feed_forward(layer)
            experts(0)
            attention()
            logits(1, 0)
            experts(1)

        @block.tensor
        def _(pe):
            mm = nc.tensor.matmul

            def ring(*key):
                k = RING[key]
                if k >= 2:
                    pe.wait_ge(ring_sb, k - 1)
                return ring_bank[k % 2][:, :]

            def pair(*key):
                if PAIR[key] >= 1:
                    pe.wait_ge(pair_sb, PAIR[key])
                return PA

            def turns(n, s, bank):
                pe.wait_ge(xn_ready, turn_no(n, s) + 1)
                for k in range(TPS):
                    ins = nc.tensor.transpose(bank[:, k * P:(k + 1) * P], xn[:, TPS * s + k, :], ident)
                return ins

            def plain_turn(n, s):
                turns(n, s, ring("turn", n, s)).then_inc(ring_ps, 1)

            def channels(c, what, bank):
                wait_front(pe, "turn", c)
                col = "qk".index(what)
                w = proj_w[:, c // SEQ, col * D:(col + 1) * D] if c < A else wqkv[:, col, :]
                return mm(bank, w, xT[:, turn_no(*front_key("turn", c)[1:]) % 2, :], start=True, stop=True)

            def token_values(s, bank):
                wait_front(pe, "turn", A + s)
                x = xT[:, turn_no(LNC, s) % 2, :]
                for k in range(TPS):
                    ins = mm(bank[:, k * P:(k + 1) * P], x[:, k * P:(k + 1) * P], wqkv[:, 2, :], start=True,
                             stop=True)
                return ins

            def front(c):
                key = front_key("turn", c)
                plain_turn(*key[1:])
                channels(c, "q", ring("q", c)).then_inc(ring_ps, 1)
                channels(c, "k", ring("k", c)).then_inc(ring_ps, 1)
                if c >= A:
                    token_values(c - A, ring("v", c - A)).then_inc(ring_ps, 1)

            def route(m, s):
                n = (LNM1, LNM2)[m]
                plain_turn(n, s)
                bank = ring("router", m, s)
                wait_ring(pe, "turn", n, s)
                for k in range(TPS):
                    ins = mm(bank[:, k * E:(k + 1) * E], xT[:, turn_no(n, s) % 2, k * P:(k + 1) * P], gate_w[:, :],
                             start=True, stop=True)
                ins.then_inc(ring_ps, 1)

            def retention(layer):
                def tile_x(t):
                    k = t % TPS
                    return xT[:, turn_no(1 + 2 * layer, t // TPS) % 2, k * P:(k + 1) * P]

                def gate_input(s):
                    x = xT[:, turn_no(1 + 2 * layer, s) % 2, :]
                    mm(ring("xo", layer, s), proj_w[:, layer, 3 * D:4 * D], x, start=True,
                       stop=True).then_inc(ring_ps, 1)

                def keys_values(t):
                    g = layer * NT + t
                    if g >= 1:
                        pe.wait_ge(kv_sb, g)
                    mm(PC[:, 0, 0:2 * D], tile_x(t), proj_w[:, layer, D:3 * D], start=True,
                       stop=True).then_inc(kv_ps, 1)

                def scores(t, u):
                    g = layer * NT + t
                    c = (g // TPS) % 2
                    pe.wait_ge(st_in[c], 7 * 16 * (g // TPS // 2 + 1))
                    if g >= 1:
                        pe.wait_ge(pm_sb, 2 * (g - 1) + u + 1)
                    for h in range(8 * u, 8 * u + 8):
                        k = h % 8
                        o = h * L + (t % TPS) * P
                        ins = mm((PA, PB)[u][:, k // 4, (k % 4) * P:(k % 4 + 1) * P], kst[:, c, o:o + P],
                                 qst[:, c, o:o + P], start=True, stop=True)
                    ins.then_inc(sc_ps, 1)

                def retain(t):
                    g = layer * NT + t
                    pe.wait_ge(pm_sb, 2 * g + 2)
                    pe.wait_ge(vp_sb, g + 1)
                    pe.wait_ge(kg_sb, g + 1)
                    if g >= 1:
                        pe.wait_ge(rg_sb, g)
                    if t >= 1:
                        pe.wait_ge(ro_up, g)
                    first = t % TPS == 0
                    seen = (g // TPS) * (TPS - 1) + t % TPS
                    if seen:
                        pe.wait_ge(state_sb, seen)
                    if not first:
                        pe.wait_ge(qg_sb, g // TPS + 1)
                        mm(PC[:, 1, 0:P], state[:, (g - 1) % 2, :],
                           qgT[:, (g // TPS) % 2, (t % TPS) * P:(t % TPS + 1) * P], start=True, stop=False,
                           skip_group_check=True)
                    for h in range(H):
                        a, k = divmod(h, HG)
                        ins = mm(PC[32 * a:32 * a + 32, 1, 0:P], vp[:, g % 2, a, 32 * k:32 * k + 32],
                                 pm[:, 2 * (g % 2) + h // 8, (h % 8) * P:(h % 8 + 1) * P],
                                 start=first and k == 0, stop=k == HG - 1, skip_group_check=True)
                    if t % TPS < TPS - 1:
                        ins = mm(PC[:, 1, P:2 * P], kg[:, g % 2, :], kvb[:, g % 2, D:2 * D], start=True, stop=True,
                                 skip_group_check=True)
                    ins.then_inc(re_ps, 1)

                def project_out(t):
                    g = layer * NT + t
                    done = t + 1
                    pe.wait_ge(rg_sb, layer * NT + done)
                    states = (layer * SEQ + done // TPS) * (TPS - 1) + done % TPS
                    pe.wait_ge(state_sb, states)
                    if g >= 1:
                        pe.wait_ge(ro_up, g)
                    mm(PC[:, 1, 0:D], rgT[:, g % 2, :], reto_w[:, layer, :], start=True, stop=False)
                    mm(PC[:, 1, 0:D], ones_row, reto_b[:, layer, :], start=False, stop=True).then_inc(ro_ps, 1)

                for t in range(NT + 2):
                    if t < NT:
                        if t % TPS == 0:
                            gate_input(t // TPS)
                        keys_values(t)
                        scores(t, 0)
                    if t >= 2:
                        project_out(t - 2)
                    if t < NT:
                        scores(t, 1)
                    if 1 <= t < NT + 1:
                        retain(t - 1)
                    if t % TPS == 0 and t < NT:
                        if t // TPS + 1 < SEQ:
                            front(layer * SEQ + t // TPS + 1)
                        else:
                            plain_turn(2 + 2 * layer, 0)

            def feed_forward(layer):
                def up(s):
                    wait_ring(pe, "turn", 2 + 2 * layer, s)
                    x = xT[:, turn_no(2 + 2 * layer, s) % 2, :]
                    for f in range(FB):
                        g = (layer * SEQ + s) * FB + f
                        if g >= 4:
                            pe.wait_ge(f1_sb, g - 3)
                        mm((PA, PB)[f // 2][:, f % 2, :], ffn1_w[:, layer, f * P:(f + 1) * P], x, start=True,
                           stop=True).then_inc(f1_ps, 1)

                def down(s):
                    b = layer * SEQ + s
                    pe.wait_ge(f1_sb, (b + 1) * FB)
                    for k in range(TPS):
                        g = b * TPS + k
                        if g >= 2:
                            pe.wait_ge(f2_up, g - 1)
                        bank = PC[:, g % 2, 0:D]
                        for f in range(FB):
                            mm(bank, hT[:, b % 2, f, k * P:(k + 1) * P], ffn2_w[:, layer, f, :], start=f == 0,
                               stop=False)
                        mm(bank, ones_row, ffn2_b[:, layer, :], start=False, stop=True).then_inc(f2_ps, 1)

                pe.wait_ge(pm_sb, 2 * NT * (layer + 1))
                pe.wait_ge(ro_up, NT * (layer + 1))
                up(0)
                for s in range(SEQ):
                    if s + 1 < SEQ:
                        plain_turn(2 + 2 * layer, s + 1)
                        up(s + 1)
                    elif layer + 1 < LAYERS:
                        front((layer + 1) * SEQ)
                    down(s)
                if layer + 1 == LAYERS:
                    route(0, 0)
                pe.wait_ge(f1_sb, SEQ * FB * (layer + 1))
                pe.wait_ge(f2_up, NT * (layer + 1))

            def experts(m):
                def down(e, s):
                    n = m * E + e
                    b = n * SEQ + s
                    pe.wait_ge(in_w2[n % 2], 16 * (n // 2 + 1))
                    pe.wait_ge(m1_sb, (b + 1) * FB)
                    if b >= 2:
                        pe.wait_ge(m2_up, b - 1)
                    for k in range(TPS):
                        for f in range(FB):
                            ins = mm(PC[:, b % 2, k * D:(k + 1) * D], hT[:, b % 2, f, k * P:(k + 1) * P],
                                     w2[n % 2][:, f, :], start=f == 0, stop=f == FB - 1)
                    ins.then_inc(m2_ps, 1)

                prev = None
                for e in range(E):
                    n = m * E + e
                    pe.wait_ge(w_hi, n + 1)
                    pe.wait_ge(w_lo, n + 1)
                    for s in range(SEQ):
                        if e == 0:
                            wait_ring(pe, "turn", (LNM1, LNM2)[m], s)
                            pe.wait_ge(xl_ready, m * SEQ + s + 1)
                        x = slice(s * L, (s + 1) * L)
                        for f in range(FB):
                            g = (n * SEQ + s) * FB + f
                            if g >= 2:
                                pe.wait_ge(m1_sb, g - 1)
                            c = slice(f * P, (f + 1) * P)
                            for k, bank in enumerate((PA, PB)):
                                mm(bank[:, g % 2, :], w13h[:, n % 2, k, c], xh[:, x], start=True, stop=False)
                                mm(bank[:, g % 2, :], w13h[:, n % 2, k, c], xl[:, x], start=False, stop=False)
                                ins = mm(bank[:, g % 2, :], w13l[:, n % 2, k, c], xh[:, x], start=False, stop=True)
                            ins.then_inc(m1_ps, 1)
                            if e == 0 and s + 1 < SEQ and f == 1:
                                route(m, s + 1)
                        if prev is not None:
                            down(*prev)
                        prev = (e, s)
                if m == 0:
                    pe.wait_ge(in_att, in_att_n)
                    front(A)
                down(*prev)
                if m == 0:
                    front(A + 1)
                pe.wait_ge(m1_sb, E * SEQ * FB * (m + 1))
                pe.wait_ge(m2_up, E * SEQ * (m + 1))

            def attention():
                def head(h, c, o, n):
                    return slice(h * L + o, h * L + o + n)

                def max_scores(s, v):
                    i, p = max_unit(v)
                    bank = pair("max", s, v)
                    pe.wait_ge(st_in[s % 2], 7 * 16 * ((A + s) // 2 + 1))
                    w = (i + 1) * P
                    for k in range(2):
                        mm(bank[:, k, i * P:w], idb[:, :], mqb[:, :], start=True, stop=False, skip_group_check=True)
                    for k in range(2):
                        o = (2 * p + k) * L
                        ins = mm(bank[:, k, 0:w], qst[:, s % 2, o + i * P:o + w], kst[:, s % 2, o:o + w],
                                 start=False, stop=True, skip_group_check=True)
                    ins.then_inc(pair_ps, 1)

                def turn_max(s):
                    bank = pair("mx", s, 0)
                    pe.wait_ge(mx_sb, s + 1)
                    for i in range(TPS):
                        ins = nc.tensor.transpose(bank[0:NP3 * H, 0, i * P:(i + 1) * P], mxf[:, i, :], ident)
                    ins.then_inc(pair_ps, 1)

                def exp_scores(s, v):
                    j, p = exp_unit(v)
                    u = NV * s + v
                    if v == 0:
                        pe.wait_ge(max_in, 16 * (s + 1))
                    if u >= 2:
                        pe.wait_ge(ex_sb, u - 1)
                    w = (TPS - j) * P
                    bank = (PB, PC)[u % 2]
                    for k in range(2):
                        mm(bank[:, k, 0:P], idb[:, :], mkb[:, :], start=True, stop=False, skip_group_check=True)
                    for k in range(2):
                        o = (2 * p + k) * L + j * P
                        ins = mm(bank[:, k, 0:w], kst[:, s % 2, o:o + P], qst[:, s % 2, o:o + w],
                                 start=False, stop=True, skip_group_check=True)
                    ins.then_inc(ex_ps, 1)

                def weighted(s, v):
                    j, p = exp_unit(v)
                    u = NV * s + v
                    pe.wait_ge(ex_sb, u + 1)
                    if v == 0:
                        pe.wait_ge(va_sb, s + 1)
                        if s >= 1:
                            pe.wait_ge(ao_raw, s)
                    for k in range(2):
                        h = 2 * p + k
                        a, g = divmod(h, HG)
                        r = 64 * (a % 2)
                        ins = mm((P6, P7)[a // 2][r:r + 64, j * P:L], va[:, j, a, 64 * g:64 * g + 64],
                                 pt[:, u % 4, k, 0:(TPS - j) * P], start=j == 0 and g == 0, stop=True,
                                 skip_group_check=True)
                    ins.then_inc(av_ps, 1)

                def turn_weighted(s):
                    bank = pair("tr", s, 0)
                    pe.wait_ge(ao_raw, s + 1)
                    for b in range(2):
                        for i in range(TPS):
                            ins = nc.tensor.transpose(bank[:, b, i * P:(i + 1) * P], aor[:, b, i * P:(i + 1) * P],
                                                      ident)
                    ins.then_inc(pair_ps, 1)

                def turn_out(s):
                    bank = pair("ao", s, 0)
                    for i in range(TPS):
                        ins = nc.tensor.transpose(bank[:, 0, i * P:(i + 1) * P], xn[:, TPS * s + i, :], ident)
                    ins.then_inc(pair_ps, 1)

                def project(s):
                    bank = pair("wo", s, 0)
                    for i in range(TPS):
                        o = bank[:, 0, i * D:(i + 1) * D]
                        mm(o, aoT[:, i * P:(i + 1) * P], wo, start=True, stop=False)
                        ins = mm(o, ones_row, bo[:, :], start=False, stop=True)
                    ins.then_inc(pair_ps, 1)

                pe.wait_ge(att_const, 1)
                for v in range(NV):
                    max_scores(0, v)
                turn_max(0)
                wait_ring(pe, "v", 1)
                for s in range(SEQ):
                    for v in range(NV):
                        uses = slot_uses(s, v)
                        if uses and uses[0][0] == "max":
                            max_scores(*uses[0][1:])
                        exp_scores(s, v)
                        for what, s_, v_ in uses[1 if uses and uses[0][0] == "max" else 0:]:
                            if what == "max":
                                max_scores(s_, v_)
                            if what == "tr":
                                turn_weighted(s_)
                            if what == "ao":
                                turn_out(s_)
                            if what == "wo":
                                project(s_)
                            if what == "mx":
                                turn_max(s_)
                            if what == "turn":
                                turns(LNC, s_, pair("turn", s_, 0)[:, 0, :]).then_inc(pair_ps, 1)
                            if what in "qk":
                                channels(A + s_, what, pair(what, s_, 0)[:, 0, :]).then_inc(pair_ps, 1)
                            if what == "v":
                                token_values(s_, pair("v", s_, 0)[:, 0, :]).then_inc(pair_ps, 1)
                        if v >= 1:
                            weighted(s, v - 1)
                    weighted(s, NV - 1)
                turn_weighted(SEQ - 1)
                turn_out(SEQ - 1)
                project(SEQ - 1)
                pe.wait_ge(ex_sb, NV * SEQ)
                pe.wait_ge(pair_sb, len(PAIR))

            pe.wait_ge(in_const, 16)
            pe.wait_ge(in_ret, in_ret_n)
            front(0)
            pe.wait_ge(k_ones, 32)
            for layer in range(LAYERS):
                retention(layer)
                feed_forward(layer)
            experts(0)
            attention()
            route(1, 0)
            experts(1)


def kernel(**inputs):
    import concourse.bacc as bacc
    from concourse.bass_utils import run_bass_kernel_spmd

    a = {k: np.asarray(v) for k, v in inputs.items()}
    const, decay = constants()
    ln = lambda s: np.ascontiguousarray(np.stack(
        [a[f"L0_attn_a_ln{1 + j}_{s}"][layer] for layer in range(LAYERS) for j in range(2)], axis=1))
    order = np.arange(D).reshape(H, HD).T.reshape(-1)
    columns = np.concatenate([order, D + order, np.arange(2 * D, 4 * D)])
    proj_w = a["L0_attn_a_proj_w"][:, :, columns]
    proj_b = a["L0_attn_a_proj_b"][:, columns]
    heads = lambda w: w.transpose(1, 0, 2).reshape(D, D)
    turned = lambda w: w.transpose(1, 2, 0).reshape(D, D)
    arrays = {
        "x": a["L0_attn_a_x"].reshape(NT * P, D),
        "const": const,
        "decay": decay,
        "proj_w": proj_w,
        "proj_bc": proj_b.reshape(LAYERS * 4, D).T,
        "kv_b": proj_b[:, D:3 * D],
        "reto_w": a["L0_attn_a_reto_w"],
        "reto_b": a["L0_attn_a_reto_b"],
        "lng": ln("g"),
        "lnb": ln("b"),
        "lnf": np.stack([a["L0_attn_a_lnf_g"], a["L0_attn_a_lnf_b"]]),
        "ffn1_w": a["L0_attn_a_ffn1_w"],
        "ffn1_b": a["L0_attn_a_ffn1_b"].reshape(LAYERS * FB, P).T,
        "ffn2_w": a["L0_attn_a_ffn2_w"],
        "ffn2_b": a["L0_attn_a_ffn2_b"],
        "wqkv": np.stack([turned(a["L0_attn_b_Wq"]), turned(a["L0_attn_b_Wk"]), heads(a["L0_attn_b_Wv"])]),
        "wo": a["L0_attn_b_Wo"].T,
        "bo": a["L0_attn_b_bo"],
        "gate_w": a["L0_ffn_gate_w"],
        "w1": a["L0_ffn_w1"],
        "w3": a["L0_ffn_w3"],
        "w2": a["L0_ffn_w2"],
    }
    nc = bacc.Bacc("TRN2", target_bir_lowering=False, num_devices=1)
    feeds, args = {}, []
    for name, v in arrays.items():
        v = np.ascontiguousarray(v)
        feeds[f"in_{name}"] = v
        args.append(nc.dram_tensor(f"in_{name}", v.shape, mybir.dt.from_np(v.dtype), kind="ExternalInput").ap())
    out = nc.dram_tensor("out", (NT * P, D), F32, kind="ExternalOutput").ap()
    mixer_kernel(nc, *args, out)
    r = run_bass_kernel_spmd(nc, [feeds], core_ids=[0])
    return r.results[0]["out"].reshape(SEQ, L, D)
```

```python
from contextlib import ExitStack

import numpy as np
import concourse.bass as bass
from concourse import mybir

ALU = mybir.AluOpType
ACT = mybir.ActivationFunctionType
F32 = mybir.dt.float32
F32R = mybir.dt.float32r
BF16 = mybir.dt.bfloat16
I32 = mybir.dt.int32
AX_X = mybir.AxisListType.X

P = 128
D = 128
NT = 16
SEQ = 4
TPS = NT // SEQ
L = TPS * P
LAYERS = 2
H = 16
HD = D // H
F = 4 * D
FB = F // P
E = 8
EPS = 1e-5
BIG = 1e30
SCALE = float(HD) ** -0.5
HG = 4
NG = H // HG
NP3 = 3
KQ = NP3 * NP3 * HD
KS = 96
QKM = HD * H


C_ID = 0
C_GQ = C_ID + P
C_GK = C_GQ + P
C_BLK = C_GK + P
C_MQ = C_BLK + P
C_MK = C_MQ + P
C_G128 = C_MK + P
C_ONES = C_G128 + 1
C_TRI = C_ONES + P
C_END = C_TRI + E * E


def constants():
    gamma = (1.0 - 2.0 ** (-5.0 - np.arange(H, dtype=np.float64)))
    gch = np.tile(gamma, HD)
    i = np.arange(P)
    c = np.zeros((P, C_END), np.float32)
    c[:, C_ID:C_ID + P] = np.eye(P)
    c[:, C_GQ:C_GQ + P] = gch[:, None] ** (i[None, :] + 1)
    c[:, C_GK:C_GK + P] = gch[None, :] ** (P - 1 - i[:, None])
    c[:, C_BLK:C_BLK + P] = (i[:, None] % H) == (i[None, :] // HD)
    c[:, C_MQ:C_MQ + P] = np.where(i[None, :] > i[:, None], -BIG, 0.0)
    c[:, C_MK:C_MK + P] = np.where(i[:, None] > i[None, :], -BIG, 0.0)
    c[:, C_G128] = gch ** P
    c[:, C_ONES:C_ONES + P] = 1.0
    e = np.arange(E)
    c[:, C_TRI:C_TRI + E * E] = (e[None, :] < e[:, None]).reshape(1, -1)
    diff = i[None, :] - i[:, None]
    decay = np.where(diff[:, None, :] >= 0, gamma[None, :, None] ** np.maximum(diff, 0)[:, None, :], 0.0)
    return c, decay.astype(np.float32).reshape(P, H * P)


LN0, LNF, LNM1, LNC, LNM2 = 0, 2 * LAYERS + 1, 2 * LAYERS + 2, 2 * LAYERS + 3, 2 * LAYERS + 4
TURNED = [n for n in range(9) if n not in (LN0, LNF)]
BY_ACT = [2 + 2 * layer for layer in range(LAYERS)] + [LNC, LNM2]
BY_DVE = [n for n in TURNED if n not in BY_ACT]
GV = TPS * HG // 2
NV = NG * GV
HV = NV // 2
GM = TPS * HG
LAG = 2
LEAD = 2


def front_key(what, c):
    if what == "turn":
        return ("turn", 1 + 2 * (c // SEQ) if c < LAYERS * SEQ else LNC, c % SEQ)
    return (what, c) if what in "qk" else (what, c % SEQ)


def turn_no(n, s):
    return TURNED.index(n) * SEQ + s


def ring_plan():
    def front(layer, s):
        return [("turn", 1 + 2 * layer, s), ("q", layer * SEQ + s), ("k", layer * SEQ + s)]

    def route(m, s):
        return [("turn", (LNM1, LNM2)[m], s), ("router", m, s)]

    def att(s):
        return [("turn", LNC, s), ("q", LAYERS * SEQ + s), ("k", LAYERS * SEQ + s), ("v", s)]

    plan = front(0, 0)
    for layer in range(LAYERS):
        for s in range(SEQ):
            plan += (front(layer, s + 1) if s + 1 < SEQ else [("turn", 2 + 2 * layer, 0)]) + [("xo", layer, s)]
        for s in range(SEQ):
            if s + 1 < SEQ:
                plan += [("turn", 2 + 2 * layer, s + 1)]
            if s == SEQ - 2 and layer + 1 < LAYERS:
                plan += front(layer + 1, 0)
            if s == SEQ - 1 and layer + 1 == LAYERS:
                plan += route(0, 0)
    for s in range(1, SEQ):
        plan += route(0, s)
    plan += att(0) + att(1)
    for s in range(SEQ):
        plan += route(1, s)
    return {key: k for k, key in enumerate(plan)}


def slot_uses(s, v):
    out = []
    g = NG * s + v // GV
    if g + LEAD < NG * SEQ:
        out += [("max", g + LEAD, 2 * (v % GV)), ("max", g + LEAD, 2 * (v % GV) + 1)]
    if v % GV == 1 and 1 <= g < NG * SEQ - LEAD + 1:
        out += [("mx", g + LEAD - 1)]
    if v == HV + 3:
        out += [("tr", s, 0)]
    if s >= 1:
        out += {3: [("tr", s - 1, 1)], 5: [("ao", s - 1)], 7: [("wo", s - 1)]}.get(v, [])
    if s + 2 < SEQ and 0 <= v - (NV - 6) < 4:
        out += [(("turn", "q", "k", "v")[v - (NV - 6)], s + 2)]
    return out


LATE_MX = 4
LEAD_USES = ([("max", 0, k) for k in range(GM)] + [("max", 1, k) for k in range(LATE_MX)] + [("mx", 0)]
             + [("max", 1, k) for k in range(LATE_MX, GM)] + [("mx", 1)])
LAST_USES = [("tr", SEQ - 1, 1), ("ao", SEQ - 1), ("wo", SEQ - 1)]


def pair_plan():
    plan = LEAD_USES + [use for s in range(SEQ) for v in range(NV) for use in slot_uses(s, v)] + LAST_USES
    return {key: k for k, key in enumerate(plan)}


RING = ring_plan()
PAIR = pair_plan()


def max_unit(g, k):
    return TPS - 1 - k // HG, (g % NG) * HG + k % HG


def exp_unit(v):
    return (v % GV) // 2, 2 * (v // GV) + v % 2


def mixer_kernel(nc, a_x, a_const, a_decay, a_proj_w, a_proj_bc, a_kv_b, a_reto_w, a_reto_b, a_lng, a_lnb,
                 a_lnf, a_ffn1_w, a_ffn1_b, a_ffn2_w, a_ffn2_b, a_wqkv, a_wo, a_bo,
                 a_gate_w, a_w1, a_w3, a_w2, a_out):
    with ExitStack() as ctx:
        def sb(name, shape, dt=F32):
            return ctx.enter_context(nc.sbuf_tensor(name, shape, dt))

        def ps(name, shape):
            return ctx.enter_context(nc.psum_tensor(name, shape, F32))

        def sem(name):
            return ctx.enter_context(nc.semaphore(name))

        const = sb("const", [P, C_END])
        decay = sb("decay", [P, H, P])
        proj_w = sb("proj_w", [P, LAYERS, 4 * D])
        proj_bc = sb("proj_bc", [P, LAYERS, 4])
        kv_b = sb("kv_b", [P, LAYERS, 2 * D])
        reto_w = sb("reto_w", [P, LAYERS, D])
        reto_b = sb("reto_b", [1, LAYERS, D])
        lng = sb("lng", [P, 2 * LAYERS])
        lnb = sb("lnb", [P, 2 * LAYERS])
        lnf = sb("lnf", [P, 2, D])
        ffn_w = sb("ffn_w", [P, LAYERS, 2, F])
        ffn1_w = ffn_w[:, :, 0, :]
        ffn2_w = ffn_w[:, :, 1, :].rearrange("p l (f n) -> p l f n", f=FB)
        ffn1_b = sb("ffn1_b", [P, LAYERS, FB])
        ffn2_b = sb("ffn2_b", [1, LAYERS, D])
        wqkv = ffn_w[:, 1, 0, 0:3 * D].rearrange("p (c n) -> p c n", c=3)
        wo = ffn_w[:, 1, 0, 3 * D:4 * D]
        bo = sb("bo", [1, D])
        gate_w = sb("gate_w", [P, E])
        w13 = (ffn_w[:, 0, :, :], proj_w[:, :, :])
        w2 = tuple(w.rearrange("p (f n) -> p f n", f=FB)
                   for w in (ffn_w[:, 1, 1, :], kv_b[:, :, :].rearrange("p l n -> p (l n)")))
        w13h = sb("w13h", [P, 2, 2, F], F32R)
        w13l = sb("w13l", [P, 2, 2, F], F32R)

        X = sb("X", [P, NT, D])
        R = sb("R", [P, NT, D])
        xn = sb("xn", [P, NT, D])
        xT = sb("xT", [P, 2, L])
        xh = sb("xh", [P, NT * P], F32R)
        xl = sb("xl", [P, NT * P], F32R)
        str_ = sb("str_", [P, TPS, 6])
        mvr = sb("mvr", [P, 2, TPS, 2])
        nrm = sb("nrm", [P, 4, TPS])
        st6 = sb("st6", [P, 2 * TPS, 6])
        mv = sb("mv", [P, 2 * TPS, 2])
        rs = sb("rs", [P, 3, 2 * TPS])
        pm = sb("pm", [P, 4, 8 * P])
        pt = pm[:, :, :].rearrange("p b (k n) -> p b k n", k=2)
        hT = pm[:, :, :].rearrange("p (a g) (f n) -> p a (g f) n", a=2, f=2)
        VA = 9 * HD * HG
        va = sb("va", [P, TPS, NG, VA])
        work = va[:, :, :, :].rearrange("p j a x -> p (j a x)")
        sxT = work[:, 0:2 * L].rearrange("p (a n) -> p a n", a=2)
        qgT = work[:, 2 * L:4 * L].rearrange("p (a n) -> p a n", a=2)
        vp = work[:, 4 * L:4 * L + 2 * NG * 40 * HG].rearrange("p (b a x) -> p b a x", b=2, a=NG)
        qkf = sb("qkf", [P, 2, L])
        qkt_ret = work[:, 7 * L:9 * L].rearrange("p (a n) -> p a n", a=2)
        qkt_att = R[:, 0:2 * TPS, :].rearrange("p (a i) n -> p a (i n)", a=2)
        qkp = sb("qkp", [P, NP3, 2, L], BF16)
        qst = sb("qst", [KS, 2, H * L], BF16)
        kst = sb("kst", [KS, 2, H * L], BF16)
        zeros = pm[0:KS - KQ, 0, 0:L // 2].bitcast(BF16)
        ones = pm[0:KS - KQ, 1, 0:L // 2].bitcast(BF16)
        vs = sb("vs", [P, 2, TPS * D])
        kvb = vs[:, 0, :].rearrange("p (a n) -> p a n", a=2)
        kg = vs[:, 1, 0:2 * D].rearrange("p (a n) -> p a n", a=2)
        rgT = vs[:, 1, 2 * D:4 * D].rearrange("p (a n) -> p a n", a=2)
        dst = sb("dst", [P, D])
        state = sb("state", [P, 2, D])
        late = decay[:, :, :].rearrange("p h n -> p (h n)")
        silu_a = late[:, 2 * L:4 * L].rearrange("p (a n) -> p a n", a=2)
        aor = late[:, 0:2 * L].rearrange("p (b n) -> p b n", b=2)
        aoT = late[:, 2 * L:3 * L]
        mxT = late[0:NP3 * HG, 3 * L:3 * L + L // 2].bitcast(BF16)
        mxf = late[:, 3 * L + L // 2:3 * L + L // 2 + TPS * NP3 * HG].rearrange("p (i w) -> p i w", i=TPS)
        lg = sb("lg", [P, TPS, E])
        lgm = sb("lgm", [P, TPS])
        lgd = sb("lgd", [P, TPS, E])
        lge = sb("lge", [P, TPS, E])
        cgt = late[:, 0:TPS * E * E].rearrange("p (k a b) -> p k a b", k=TPS, a=E)
        cge = late[:, TPS * E * E:2 * TPS * E * E].rearrange("p (k a b) -> p k a b", k=TPS, a=E)
        rank = sb("rank", [P, TPS, E])
        wsum = sb("wsum", [P, TPS])
        wi = sb("wi", [P, NT, E])
        idb = sb("idb", [P, P], BF16)
        mqb = sb("mqb", [P, P], BF16)
        mkb = sb("mkb", [P, P], BF16)
        rmax = sb("rmax", [P, TPS, HG])
        mxr = sb("mxr", [P, TPS, HG])
        mxb = sb("mxb", [P, TPS, NP3, HG], BF16)
        rden = sb("rden", [P, 2, TPS, 2, HG])

        parts_dram = nc.dram_tensor("parts_dram", (2, 5, 2, P, L), BF16, kind="Internal").ap()
        max_dram = nc.dram_tensor("max_dram", (NP3 * HG, L), BF16, kind="Internal").ap()

        PA = ps("PA", [P, 2, 512])
        PB = ps("PB", [P, 2, 512])
        PC = ps("PC", [P, 2, 512])
        P6 = ps("P6", [P, 512])
        P7 = ps("P7", [P, 512])
        ring_bank = (P6, P7)

        ident = const[:, C_ID:C_ID + P]
        ones_row = const[0:1, C_ONES:C_ONES + P]

        in_x = [sem(f"in_x{s}") for s in range(SEQ)]
        in_const = sem("in_const")
        in_decay = sem("in_decay")
        in_ret = sem("in_ret")
        in_ffn = sem("in_ffn")
        in_att = sem("in_att")
        in_w13 = (sem("in_w13a"), sem("in_w13b"))
        in_w2 = (sem("in_w2a"), sem("in_w2b"))
        out_done = sem("out_done")
        filled = sem("filled")
        stack_fill = sem("stack_fill")
        parts_out = sem("parts_out")
        st_in = (sem("st_ina"), sem("st_inb"))
        max_out = sem("max_out")
        max_in = sem("max_in")
        v_chain = sem("v_chain")
        p_chain = sem("p_chain")
        xn_ready = sem("xn_ready")
        stats_sb = sem("stats_sb")
        nrm_sb = sem("nrm_sb")
        xn_act = sem("xn_act")
        ring_ps = sem("ring_ps")
        ring_sb = sem("ring_sb")
        pair_ps = sem("pair_ps")
        pair_sb = (sem("pair_sba"), sem("pair_sbb"))
        xl_ready = sem("xl_ready")
        qt_sb = sem("qt_sb")
        q2_sb = sem("q2_sb")
        q3_sb = sem("q3_sb")
        qg_sb = sem("qg_sb")
        kv_ps = sem("kv_ps")
        kv_sb = sem("kv_sb")
        vp_sb = sem("vp_sb")
        kg_sb = sem("kg_sb")
        sc_ps = sem("sc_ps")
        pm_sb = sem("pm_sb")
        re_ps = sem("re_ps")
        rg_sb = sem("rg_sb")
        dst_sb = sem("dst_sb")
        state_sb = sem("state_sb")
        ro_ps = sem("ro_ps")
        ro_up = sem("ro_up")
        f1_ps = sem("f1_ps")
        f1_sb = sem("f1_sb")
        f2_ps = sem("f2_ps")
        f2_up = sem("f2_up")
        lnf_sb = sem("lnf_sb")
        left_sb = sem("left_sb")
        lg_d = sem("lg_d")
        routed = sem("routed")
        va_zero = sem("va_zero")
        lg_e = sem("lg_e")
        w_hi = sem("w_hi")
        w_lo = sem("w_lo")
        m1a_ps = sem("m1a_ps")
        m1_ps = sem("m1_ps")
        m1_si = sem("m1_si")
        m1_sb = sem("m1_sb")
        m2_ps = sem("m2_ps")
        m2_up = sem("m2_up")
        att_const = sem("att_const")
        va_sb = sem("va_sb")
        mx_sb = sem("mx_sb")
        ex_ps = sem("ex_ps")
        ex_sb = sem("ex_sb")
        av_ps = sem("av_ps")
        ao_raw = sem("ao_raw")

        in_ret_n, in_ffn_n, in_att_n = 5 * 16, 10 * 16, 2 * 16

        block = ctx.enter_context(nc.Block())
        A = LAYERS * SEQ

        def wait_ring(eng, *key):
            eng.wait_ge(ring_sb, RING[key] + 1)

        def wait_pair(eng, *key):
            eng.wait_ge(pair_sb[PAIR[key] % 2], PAIR[key] // 2 + 1)

        def wait_front(eng, what, c):
            if c >= A + 2:
                wait_pair(eng, what, c - A)
            else:
                wait_ring(eng, *front_key(what, c))

        @block.sync
        def _(sp):
            x_t = a_x.rearrange("(t p) d -> p t d", p=P)
            for s in range(SEQ):
                sp.dma_start(X[:, TPS * s:TPS * s + TPS, :], x_t[:, TPS * s:TPS * s + TPS, :]).then_inc(in_x[s], 16)
                if s == 0:
                    sp.dma_start(const[:, :], a_const).then_inc(in_const, 16)
            sp.dma_start(lng[:, :], a_lng).then_inc(in_ret, 16)
            sp.dma_start(lnb[:, :], a_lnb).then_inc(in_ret, 16)
            sp.dma_start(proj_bc[:, :, :], a_proj_bc.rearrange("p (l c) -> p l c", l=LAYERS)).then_inc(in_ret, 16)
            sp.dma_start(proj_w[:, :, :], a_proj_w.rearrange("l d n -> d l n")).then_inc(in_ret, 16)
            sp.dma_start(kv_b[:, :, :], a_kv_b.partition_broadcast(P)).then_inc(in_ret, 16)
            sp.wait_ge(filled, 2)
            for b in range(2):
                for stack, fill in ((qst, zeros), (kst, ones)):
                    sp.dma_start(stack[KQ:KS, b, :].rearrange("r (h n) -> r h n", h=H),
                                 fill.unsqueeze(1).to_broadcast([KS - KQ, H, L])).then_inc(stack_fill, 16)
            sp.dma_start(decay[:, :, :], a_decay.rearrange("p (h n) -> p h n", h=H)).then_inc(in_decay, 16)
            sp.dma_start(reto_w[:, :, :], a_reto_w.rearrange("l d n -> d l n")).then_inc(in_ffn, 16)
            sp.dma_start(reto_b[:, :, :], a_reto_b.rearrange("(a l) n -> a l n", a=1)).then_inc(in_ffn, 16)
            sp.dma_start(lnf[:, :, :], a_lnf.partition_broadcast(P)).then_inc(in_ffn, 16)
            sp.dma_start(ffn1_w, a_ffn1_w.rearrange("l d n -> d l n")).then_inc(in_ffn, 16)
            sp.dma_start(ffn1_b[:, :, :], a_ffn1_b.rearrange("p (l f) -> p l f", l=LAYERS)).then_inc(in_ffn, 16)
            for layer in range(LAYERS):
                sp.dma_start(ffn2_w[:, layer, :, :],
                             a_ffn2_w[layer].rearrange("(f p) n -> p f n", p=P)).then_inc(in_ffn, 16)
            sp.dma_start(ffn2_b[:, :, :], a_ffn2_b.rearrange("(a l) n -> a l n", a=1)).then_inc(in_ffn, 16)
            sp.dma_start(gate_w[:, :], a_gate_w).then_inc(in_ffn, 16)
            sp.dma_start(bo[:, :], a_bo.rearrange("(a n) -> a n", a=1)).then_inc(in_ffn, 16)
            def stacks(c):
                b = c % 2
                sp.wait_ge(q2_sb, c + 1)
                if c >= 2:
                    sp.wait_ge(st_in[b], 7 * 16 * (c // 2))
                sp.dma_start(parts_dram[b, 0:2].rearrange("i q p n -> p (i q) n"),
                             qkp[:, 0:2, :, :].rearrange("p i q n -> p (i q) n")).then_inc(parts_out, 16)
                sp.dma_start(parts_dram[b, NP3:5, 1].rearrange("i p n -> p i n"),
                             qkp[:, 0:2, 1, :]).then_inc(parts_out, 16)
                sp.wait_ge(q3_sb, c + 1)
                sp.dma_start(parts_dram[b, 2].rearrange("q p n -> p q n"), qkp[:, 2, :, :]).then_inc(parts_out, 16)
                sp.wait_ge(parts_out, 3 * 16 * (c + 1))
                if 2 <= c < LAYERS * SEQ + 2:
                    sp.wait_ge(sc_ps, 2 * TPS * (c - 1))
                if c >= LAYERS * SEQ + 2:
                    sp.wait_ge(ex_ps, NV * (c - 1 - LAYERS * SEQ))
                for u in range(NP3):
                    r = slice(NP3 * HD * u, NP3 * HD * (u + 1))
                    q = parts_dram[b, 0:NP3, 0].rearrange("i (k h) n -> i k (h n)", h=H)
                    k = parts_dram[b, u:u + NP3, 1].rearrange("i (k h) n -> i k (h n)", h=H)
                    sp.dma_start(qst[r, b, :], q).then_inc(st_in[b], 16)
                    sp.dma_start(kst[r, b, :], k).then_inc(st_in[b], 16)
                sp.dma_start(qst[KQ:KQ + NP3, b, :], qst[KQ + 8:KQ + 8 + NP3, b, :]).then_inc(st_in[b], 16)

            def expert_w13(m, e):
                n = m * E + e
                if n >= 2:
                    sp.wait_ge(w_lo, n - 1)
                    sp.wait_ge(w_hi, n - 1)
                sp.dma_start(w13[n % 2][:, 0, :], a_w1[e]).then_inc(in_w13[n % 2], 16)
                sp.dma_start(w13[n % 2][:, 1, :], a_w3[e]).then_inc(in_w13[n % 2], 16)

            def expert_w2(m, e):
                n = m * E + e
                if n >= 2:
                    sp.wait_ge(m2_ps, SEQ * (n - 1))
                sp.dma_start(w2[n % 2], a_w2[e].rearrange("(f p) d -> p f d", p=P)).then_inc(in_w2[n % 2], 16)

            def maxima(g):
                b = (g // NG) % 2
                o = (g % NG) * HG * L
                wait_pair(sp, "mx", g)
                if g >= 1:
                    sp.wait_ge(max_in, 16 * g)
                sp.dma_start(max_dram, mxT).then_inc(max_out, 16)
                sp.wait_ge(max_out, 16 * (g + 1))
                sp.dma_start(qst[KQ:KQ + NP3, b, o:o + HG * L], max_dram.rearrange("(i h) n -> i (h n)", h=HG)
                             ).then_inc(max_in, 16)

            for c in range(LAYERS * SEQ):
                stacks(c)
                if c == SEQ:
                    sp.wait_ge(f2_ps, SEQ)
                    expert_w13(0, 0)
            sp.wait_ge(kv_ps, LAYERS * NT)
            expert_w13(0, 1)
            sp.wait_ge(f2_ps, LAYERS * SEQ)
            expert_w2(0, 0)
            sp.wait_ge(kv_sb, LAYERS * NT)
            expert_w2(0, 1)
            sp.dma_start(wqkv, a_wqkv.rearrange("c d n -> d c n")).then_inc(in_att, 16)
            sp.dma_start(wo, a_wo).then_inc(in_att, 16)
            for e in range(2, E):
                expert_w13(0, e)
                expert_w2(0, e)
            expert_w13(1, 0)
            expert_w13(1, 1)
            stacks(A)
            stacks(A + 1)
            expert_w2(1, 0)
            expert_w2(1, 1)
            for g in range(NG * SEQ):
                maxima(g)
                if g % NG == 0 and 1 <= g // NG < SEQ - 1:
                    stacks(A + g // NG + 1)
            for e in range(2, E):
                expert_w13(1, e)
                expert_w2(1, e)
            o_t = a_out.rearrange("(t p) d -> p t d", p=P)
            for s in range(SEQ):
                sp.wait_ge(m2_up, 2 * SEQ * E - SEQ + s + 1)
                sp.dma_start(o_t[:, TPS * s:TPS * s + TPS, :], X[:, TPS * s:TPS * s + TPS, :]).then_inc(out_done, 16)
            sp.wait_ge(out_done, 16 * SEQ)

        @block.gpsimd
        def _(pool):
            nc.gpsimd.memset(pm[0:KS - KQ, 0:2, 0:L // 2], 0.0).then_inc(filled, 1)
            pool.wait_ge(filled, 1)
            nc.gpsimd.memset(ones[0:NP3, :], 1.0).then_inc(filled, 1)
            pool.wait_ge(filled, 2)
            nc.gpsimd.memset(vp, 0.0)

            def first_rest(c):
                wait_front(pool, "k", c)
                nc.gpsimd.tensor_tensor(qkt_ret if c < A else qkt_att, qkf[:, :, :], qkp[:, 0, :, :],
                                        ALU.subtract).then_inc(qt_sb, 1)

            def second_rest(c):
                pool.wait_ge(q2_sb, c + 1)
                nc.gpsimd.tensor_tensor(qkp[:, 2, :, :], qkt_ret if c < A else qkt_att, qkp[:, 1, :, :],
                                        ALU.subtract).then_inc(q3_sb, 1)

            def part_rests(c):
                first_rest(c)
                second_rest(c)

            def link(ins):
                p_chain_n[0] += 1
                ins.then_inc(p_chain, 1)
                pool.wait_ge(p_chain, p_chain_n[0])

            p_chain_n = [0]

            def norm_factors(b):
                pool.wait_ge(stats_sb, b + 1)
                if b >= 1:
                    pool.wait_ge(xn_act, b)
                v, y, z, w = (nrm[:, k, :] for k in range(4))
                link(nc.gpsimd.tensor_scalar(v, mvr[:, b % 2, :, 1], EPS, None, ALU.add))
                link(nc.gpsimd.tensor_scalar(y.bitcast(I32), v.bitcast(I32), -0.5, float(0x5f3759df),
                                             ALU.mult, ALU.add))
                for _ in range(3):
                    link(nc.gpsimd.tensor_tensor(z, y, y, ALU.mult))
                    link(nc.gpsimd.tensor_tensor(z, z, v, ALU.mult))
                    link(nc.gpsimd.tensor_scalar(z, z, -0.5, 1.5, ALU.mult, ALU.add))
                    link(nc.gpsimd.tensor_tensor(y, y, z, ALU.mult))
                link(nc.gpsimd.tensor_tensor(w, y, mvr[:, b % 2, :, 0], ALU.mult))
                nc.gpsimd.tensor_scalar(w, w, -1.0, None, ALU.mult).then_inc(nrm_sb, 1)

            def decay_k(g):
                pool.wait_ge(kv_sb, g + 1)
                if g >= 2:
                    pool.wait_ge(re_ps, g - 1)
                nc.gpsimd.tensor_copy(
                    vp[:, g % 2, :, :].rearrange("p a (g r) -> p a g r", g=HG)[:, :, :, 0:HD],
                    kvb[:, g % 2, D:2 * D].rearrange("p (a g k) -> p a g k", a=NG, g=HG)).then_inc(vp_sb, 1)
                nc.gpsimd.tensor_tensor(kg[:, g % 2, :], kvb[:, g % 2, 0:D], const[:, C_GK:C_GK + P],
                                        ALU.mult).then_inc(kg_sb, 1)

            def leave_blocks(s):
                pool.wait_ge(lnf_sb, s + 1)
                r = slice(TPS * s, TPS * s + TPS)
                gain, shift = (lnf[:, k, :].unsqueeze(1).to_broadcast([P, TPS, D]) for k in range(2))
                link(nc.gpsimd.tensor_tensor(xn[:, r, :], xn[:, r, :], gain, ALU.mult))
                link(nc.gpsimd.tensor_tensor(xn[:, r, :], xn[:, r, :], shift, ALU.add))
                nc.gpsimd.tensor_tensor(X[:, r, :], X[:, r, :], xn[:, r, :], ALU.add).then_inc(left_sb, 1)

            def low_input(m, s):
                k = m * SEQ + s
                t = turn_no((LNM1, LNM2)[m], s)
                wait_ring(pool, "turn", (LNM1, LNM2)[m], s)
                nc.gpsimd.tensor_tensor(xl[:, s * L:(s + 1) * L], xT[:, t % 2, :],
                                        xh[:, s * L:(s + 1) * L].bitcast(F32), ALU.subtract).then_inc(xl_ready, 1)

            def low_weights(n):
                pool.wait_ge(in_w13[n % 2], 32 * (n // 2 + 1))
                pool.wait_ge(w_hi, n + 1)
                if n >= 2:
                    pool.wait_ge(m1_ps, SEQ * FB * (n - 1))
                nc.gpsimd.tensor_tensor(w13l[:, n % 2, :, :], w13[n % 2],
                                        w13h[:, n % 2, :, :].bitcast(F32), ALU.subtract).then_inc(w_lo, 1)

            pool.wait_ge(in_const, 16)
            part_rests(0)
            for layer in range(LAYERS):
                for s in range(SEQ):
                    if s + 1 < SEQ:
                        first_rest(layer * SEQ + s + 1)
                    decay_k(layer * NT + s * TPS)
                    if s + 1 < SEQ:
                        second_rest(layer * SEQ + s + 1)
                    decay_k(layer * NT + s * TPS + 1)
                    decay_k(layer * NT + s * TPS + 2)
                    if s >= 1:
                        norm_factors(layer * SEQ + s - 1)
                    decay_k(layer * NT + s * TPS + 3)
                norm_factors(layer * SEQ + SEQ - 1)
                if layer + 1 < LAYERS:
                    part_rests((layer + 1) * SEQ)
            pool.wait_ge(in_ffn, in_ffn_n)
            low_weights(0)
            pool.wait_ge(rg_sb, LAYERS * NT)
            pool.wait_ge(re_ps, LAYERS * NT)
            nc.gpsimd.memset(va[:, :, :, :], 0.0).then_inc(va_zero, 1)
            pool.wait_ge(va_zero, 1)
            for j in range(TPS):
                ins = nc.gpsimd.memset(
                    va[:, j, :, 0:HG * 65].rearrange("p a (g r) -> p a g r", g=HG)[:, :, :, HG * HD], 1.0)
            ins.then_inc(va_zero, 1)
            for s in range(SEQ - 1):
                leave_blocks(s)
            for m in range(2):
                for s in range(SEQ):
                    low_input(m, s)
                    if m == 1 and s == 0:
                        norm_factors(A + 2 * SEQ - 1)
                    if m == 0 and s == 0:
                        leave_blocks(SEQ - 1)
                for n in range(m * E + 1, (m + 1) * E):
                    low_weights(n)
                if m == 0:
                    norm_factors(A)
                    norm_factors(A + 1)
                    part_rests(A)
                    norm_factors(A + 2)
                    part_rests(A + 1)
                    norm_factors(A + 3)
                    low_weights(E)
                    for s in range(SEQ - 1):
                        if s + 2 < SEQ:
                            part_rests(A + s + 2)
                        norm_factors(A + SEQ + s)

        @block.vector
        def _(dve):
            chain = [0]

            def link(ins):
                chain[0] += 1
                ins.then_inc(v_chain, 1)
                dve.wait_ge(v_chain, chain[0])

            def bc(ap, shape, axis):
                return ap.unsqueeze(axis).to_broadcast(shape)

            def norm(n, s, src, out, count=1):
                tiles = count * TPS
                for k in range(tiles):
                    ins = nc.vector.bn_stats(st6[:, k, :], src[:, TPS * s + k, :])
                link(ins)
                for k in range(tiles):
                    ins = nc.vector.bn_aggr(mv[:, k, :], st6[:, k, :])
                link(ins)
                v, y, z = (rs[:, i, 0:tiles] for i in range(3))
                link(nc.vector.tensor_scalar(v, mv[:, 0:tiles, 1], EPS, None, ALU.add))
                link(nc.vector.tensor_scalar(y.bitcast(I32), v.bitcast(I32), -0.5, float(0x5f3759df),
                                             ALU.mult, ALU.add))
                for _ in range(3):
                    link(nc.vector.tensor_tensor(z, y, y, ALU.mult))
                    link(nc.vector.scalar_tensor_tensor(out=z, in0=z, scalar=-0.5, in1=v, op0=ALU.mult,
                                                        op1=ALU.mult))
                    link(nc.vector.scalar_tensor_tensor(out=y, in0=z, scalar=1.5, in1=y, op0=ALU.add,
                                                        op1=ALU.mult))
                for k in range(tiles):
                    t = TPS * s + k
                    ins = nc.vector.tensor_scalar(out[:, t, :], src[:, t, :], mv[:, k, 0:1], y[:, k:k + 1],
                                                  ALU.subtract, ALU.mult)
                if n in TURNED:
                    ins.then_inc(xn_ready, count)
                elif n == LNF:
                    ins.then_inc(lnf_sb, 1)
                else:
                    link(ins)

            def mean_variance(c):
                if c >= 2:
                    dve.wait_ge(nrm_sb, c - 1)
                for k in range(TPS):
                    ins = nc.vector.bn_aggr(mvr[:, c % 2, k, :], str_[:, k, :])
                ins.then_inc(stats_sb, 1)

            def retention(layer):
                def keys_values(t):
                    g = layer * NT + t
                    dve.wait_ge(kv_ps, g + 1)
                    if g >= 2:
                        dve.wait_ge(re_ps, g - 1)
                        dve.wait_ge(kg_sb, g - 1)
                        dve.wait_ge(vp_sb, g - 1)
                    nc.vector.tensor_tensor(kvb[:, g % 2, :], PC[:, 0, 0:2 * D], kv_b[:, layer, :],
                                            ALU.add).then_inc(kv_sb, 1)

                def decay_q(s):
                    c = layer * SEQ + s
                    wait_front(dve, "q", c)
                    if c >= 2:
                        dve.wait_ge(re_ps, TPS * (c - 1))
                    nc.vector.tensor_tensor(
                        qgT[:, c % 2, :].rearrange("p (t n) -> p t n", t=TPS),
                        qkf[:, 0, :].rearrange("p (t n) -> p t n", t=TPS),
                        bc(const[:, C_GQ:C_GQ + P], [P, TPS, P], 1), ALU.mult).then_inc(qg_sb, 1)

                def decay_scores(t, u):
                    g = layer * NT + t
                    dve.wait_ge(sc_ps, 2 * g + u + 1)
                    src = PA if u == 0 else PB
                    nc.vector.tensor_tensor(pm[:, 2 * (g % 2) + u, :],
                                            src[:, :, :].rearrange("p b n -> p (b n)"),
                                            decay[:, 8 * u:8 * u + 8, :].rearrange("p h n -> p (h n)"),
                                            ALU.mult).then_inc(pm_sb, 1)

                def gate(t):
                    g = layer * NT + t
                    c = g // TPS
                    dve.wait_ge(re_ps, g + 1)
                    wait_ring(dve, "xo", layer, t // TPS)
                    if g >= 2:
                        dve.wait_ge(ro_ps, g - 1)
                    nc.vector.tensor_tensor(rgT[:, g % 2, :], PC[:, 1, 0:P],
                                            sxT[:, c % 2, (t % TPS) * P:(t % TPS + 1) * P],
                                            ALU.mult).then_inc(rg_sb, 1)
                    if t % TPS < TPS - 1:
                        nc.vector.tensor_tensor(dst[:, :], PC[:, 1, P:2 * P], const[:, C_BLK:C_BLK + P],
                                                ALU.mult).then_inc(dst_sb, 1)

                def update_state(t):
                    g = layer * NT + t
                    c = g // TPS
                    if t % TPS < TPS - 1:
                        dve.wait_ge(dst_sb, c * (TPS - 1) + t % TPS + 1)
                        if c * TPS >= 1 or t % TPS >= 1:
                            dve.wait_ge(state_sb, c * (TPS - 1) + t % TPS)
                        if t % TPS == 0:
                            ins = nc.vector.tensor_copy(state[:, g % 2, :], dst[:, :])
                        else:
                            ins = nc.vector.scalar_tensor_tensor(
                                out=state[:, g % 2, :], in0=state[:, (g - 1) % 2, :],
                                scalar=const[:, C_G128:C_G128 + 1], in1=dst[:, :], op0=ALU.mult, op1=ALU.add)
                        ins.then_inc(state_sb, 1)

                def add_out(t):
                    g = layer * NT + t
                    dve.wait_ge(ro_ps, g + 1)
                    nc.vector.tensor_tensor(R[:, t, :], PC[:, 0, 2 * D:3 * D], R[:, t, :], ALU.add).then_inc(ro_up, 1)

                def sums(t):
                    g = layer * NT + t
                    dve.wait_ge(ro_up, g + 1)
                    ins = nc.vector.bn_stats(str_[:, t % TPS, :], R[:, t, :])
                    if t % TPS == TPS - 1:
                        link(ins)
                        mean_variance(g // TPS)

                decay_q(0)
                if layer == 0:
                    dve.wait_ge(in_x[2], 16)
                    dve.wait_ge(in_x[3], 16)
                    norm(LN0, 2, X, R, 2)
                    norm(1, 2, R, xn, 2)
                    dve.wait_ge(in_decay, 16)
                    dve.wait_ge(in_ffn, in_ffn_n)
                    dve.wait_ge(stack_fill, 4 * 16)
                for t in range(NT + 2):
                    if t < NT:
                        keys_values(t)
                    if 2 <= t:
                        update_state(t - 2)
                    if t < NT:
                        if t % TPS == 2 and t // TPS + 1 < SEQ:
                            decay_q(t // TPS + 1)
                        decay_scores(t, 0)
                    if t >= 2:
                        add_out(t - 2)
                    if t < NT:
                        decay_scores(t, 1)
                    if t >= 2:
                        sums(t - 2)
                    if 1 <= t < NT + 1:
                        gate(t - 1)

            def feed_forward(layer):
                for s in range(SEQ):
                    b = layer * SEQ + s
                    r = slice(TPS * s, TPS * s + TPS)
                    dve.wait_ge(f2_ps, b + 1)
                    nc.vector.tensor_tensor(R[:, r, :], PC[:, b % 2, :].rearrange("p (k n) -> p k n", k=TPS),
                                            R[:, r, :], ALU.add).then_inc(f2_up, 1)
                    dve.wait_ge(f2_up, b + 1)
                    if layer + 1 < LAYERS:
                        norm(3 + 2 * layer, s, R, xn)
                    else:
                        norm(LNF, s, R, xn)
                        if s >= 1:
                            enter_experts(s - 1)

            def enter_experts(s):
                dve.wait_ge(left_sb, s + 1)
                norm(LNM1, s, X, xn)

            def route(m, s):
                c = m * SEQ + s
                wait_ring(dve, "router", m, s)
                link(nc.vector.tensor_reduce(lgm[:, :], lg[:, :, :], AX_X, ALU.max))
                nc.vector.tensor_tensor(lgd[:, :, :], lg[:, :, :], bc(lgm[:, :], [P, TPS, E], 2),
                                        ALU.subtract).then_inc(lg_d, 1)
                for k in range(TPS):
                    for o, op in ((cgt, ALU.is_gt), (cge, ALU.is_ge)):
                        ins = nc.vector.tensor_tensor(o[:, k, :, :], bc(lg[:, k, :], [P, E, E], 1),
                                                      bc(lg[:, k, :], [P, E, E], 2), op)
                link(ins)
                flat = cge.rearrange("p k a b -> p k (a b)")
                link(nc.vector.tensor_tensor(flat, flat, bc(const[:, C_TRI:C_TRI + E * E], [P, TPS, E * E], 1),
                                             ALU.mult))
                link(nc.vector.tensor_tensor(cgt, cgt, cge, ALU.max))
                nc.vector.tensor_reduce(rank[:, :, :], cgt, AX_X, ALU.add).then_inc(routed, 1)

            def weigh_experts(m, s):
                c = m * SEQ + s
                dve.wait_ge(routed, c + 1)
                dve.wait_ge(lg_e, c + 1)
                w = wi[:, TPS * s:TPS * s + TPS, :]
                link(nc.vector.scalar_tensor_tensor(out=w, in0=rank[:, :, :], scalar=2.0, in1=lge[:, :, :],
                                                    op0=ALU.is_lt, op1=ALU.mult))
                link(nc.vector.tensor_reduce(wsum[:, :], w, AX_X, ALU.add))
                link(nc.vector.reciprocal(wsum[:, :], wsum[:, :]))
                link(nc.vector.tensor_tensor(w, w, bc(wsum[:, :], [P, TPS, E], 2), ALU.mult))

            def round_weights(n):
                dve.wait_ge(in_w13[n % 2], 32 * (n // 2 + 1))
                if n >= 2:
                    dve.wait_ge(m1_ps, SEQ * FB * (n - 1))
                    dve.wait_ge(w_lo, n - 1)
                nc.vector.tensor_copy(w13h[:, n % 2, :, :], w13[n % 2]).then_inc(w_hi, 1)

            def experts(m):
                def add_expert(e, s):
                    b = (m * E + e) * SEQ + s
                    dve.wait_ge(m2_ps, b + 1)
                    if e >= 1:
                        dve.wait_ge(m2_up, b - SEQ + 1)
                    for k in range(TPS):
                        t = TPS * s + k
                        ins = nc.vector.scalar_tensor_tensor(
                            out=X[:, t, :], in0=PC[:, b % 2, k * D:(k + 1) * D], scalar=wi[:, t, e:e + 1],
                            in1=X[:, t, :], op0=ALU.mult, op1=ALU.add)
                    ins.then_inc(m2_up, 1)
                    if e == E - 1 and m == 0:
                        dve.wait_ge(m2_up, b + 1)
                        for k in range(TPS):
                            ins = nc.vector.bn_stats(str_[:, k, :], X[:, TPS * s + k, :])
                        link(ins)
                        mean_variance(LAYERS * SEQ + s)

                route(m, 0)
                prev = None
                for e in range(E):
                    for s in range(SEQ):
                        b = (m * E + e) * SEQ + s
                        for f in range(FB):
                            g = b * FB + f
                            dve.wait_ge(m1_si, g + 1)
                            dve.wait_ge(m1_ps, g + 1)
                            if f == 0 and b >= 2:
                                dve.wait_ge(m2_ps, b - 1)
                            nc.vector.tensor_tensor(hT[:, b % 2, f, :], silu_a[:, g % 2, :],
                                                    PB[:, g % 2, :], ALU.mult).then_inc(m1_sb, 1)
                            if f == 1 and prev is not None:
                                add_expert(*prev)
                        prev = (e, s)
                        if e == 0:
                            weigh_experts(m, s)
                            if m == 0 and s == 0:
                                enter_experts(SEQ - 1)
                            if s + 1 < SEQ:
                                route(m, s + 1)
                        if s == 1 and m * E + e + 1 < 2 * E:
                            round_weights(m * E + e + 1)
                add_expert(*prev)

            def attention():

                def spread_values(s, b):
                    wait_front(dve, "v", A + s)
                    dve.wait_ge(va_zero, 2)
                    if s >= 1:
                        dve.wait_ge(av_ps, NV * (s - 1) + HV * (b + 1))
                    for j in range(TPS):
                        ins = nc.vector.tensor_copy(
                            va[:, j, 2 * b:2 * b + 2, :].rearrange("p a (g r) -> p a g r", g=HG)[:, :, :, 0:HD],
                            vs[:, s % 2, j * D + b * D // 2:j * D + (b + 1) * D // 2].rearrange(
                                "p (a g k) -> p a g k", a=2, g=HG))
                    ins.then_inc(va_sb, 1)

                def row_max(g, k):
                    n = PAIR[("max", g, k)]
                    i, h = max_unit(g, k)
                    dve.wait_ge(pair_ps, n + 1)
                    nc.vector.tensor_reduce(rmax[:, i, h % HG:h % HG + 1], PA[:, n % 2, 0:(i + 1) * P],
                                            AX_X, ALU.max).then_inc(pair_sb[n % 2], 1)

                def minus_max(g):
                    wait_pair(dve, "max", g, GM - 2)
                    wait_pair(dve, "max", g, GM - 1)
                    if g >= 1:
                        dve.wait_ge(pair_ps, PAIR[("mx", g - 1)] + 1)
                    link(nc.vector.tensor_scalar(mxb[:, :, 0, :], rmax[:, :, :], -1.0, None, ALU.mult))
                    link(nc.vector.scalar_tensor_tensor(out=mxr[:, :, :], in0=rmax[:, :, :], scalar=-1.0,
                                                        in1=mxb[:, :, 0, :], op0=ALU.mult, op1=ALU.subtract))
                    link(nc.vector.tensor_copy(mxb[:, :, 1, :], mxr[:, :, :]))
                    link(nc.vector.tensor_tensor(mxb[:, :, 2, :], mxr[:, :, :], mxb[:, :, 1, :], ALU.subtract))
                    nc.vector.tensor_copy(mxf.rearrange("p i (w h) -> p i w h", w=NP3),
                                          mxb[:, :, :, :]).then_inc(mx_sb, 1)
                    dve.wait_ge(mx_sb, g + 1)

                def weigh(s, b):
                    n = PAIR[("tr", s, b)]
                    dve.wait_ge(pair_ps, n + 1)
                    o = PA[:, n % 2, :].rearrange("p (i c x) -> p i c x", i=TPS, c=2)
                    link(nc.vector.reciprocal(rden[:, b, :, :, :], o[:, :, :, HG * HD:HG * HD + HG]))
                    for c in range(2):
                        a = 2 * b + c
                        ins = nc.vector.tensor_tensor(
                            xn[:, TPS * s:TPS * s + TPS, HG * HD * a:HG * HD * (a + 1)].rearrange(
                                "p i (g k) -> p i g k", g=HG),
                            PA[:, n % 2, :].rearrange("p (i c g k) -> p i c g k", i=TPS, c=2, k=HD)[:, :, c, 0:HG, :],
                            bc(rden[:, b, :, c, :], [P, TPS, HG, HD], 3), ALU.mult)
                    ins.then_inc(pair_sb[n % 2], 1)

                def add_out(s):
                    n = PAIR[("wo", s)]
                    dve.wait_ge(pair_ps, n + 1)
                    r = slice(TPS * s, TPS * s + TPS)
                    nc.vector.tensor_tensor(X[:, r, :], PA[:, n % 2, :].rearrange("p (i n) -> p i n", i=TPS),
                                            X[:, r, :], ALU.add).then_inc(pair_sb[n % 2], 1)
                    wait_pair(dve, "wo", s)
                    for k in range(TPS):
                        ins = nc.vector.bn_stats(str_[:, k, :], X[:, TPS * s + k, :])
                    link(ins)
                    mean_variance((LAYERS + 1) * SEQ + s)

                def run(uses):
                    for use in uses:
                        if use[0] == "max":
                            row_max(*use[1:])
                            if use[2] == GM - 1:
                                minus_max(use[1])
                        if use[0] == "tr":
                            weigh(*use[1:])
                        if use[0] == "wo":
                            add_out(use[1])

                run(LEAD_USES)
                spread_values(0, 0)
                spread_values(0, 1)
                for s in range(SEQ):
                    for v in range(NV):
                        run(slot_uses(s, v))
                        if v == 1 and s >= 1:
                            spread_values(s, 1)
                        if v == HV + 1 and s + 1 < SEQ:
                            spread_values(s + 1, 0)
                run(LAST_USES)

            dve.wait_ge(in_const, 16)
            for s in range(2):
                dve.wait_ge(in_x[s], 16)
                norm(LN0, s, X, R)
                norm(1, s, R, xn)
            dve.wait_ge(in_ret, in_ret_n)
            for layer in range(LAYERS):
                retention(layer)
                if layer == LAYERS - 1:
                    round_weights(0)
                if layer == 0:
                    for t_, src in ((idb, C_ID), (mqb, C_MQ), (mkb, C_MK)):
                        ins = nc.vector.tensor_copy(t_[:, :], const[:, src:src + P])
                    ins.then_inc(att_const, 1)
                feed_forward(layer)
            experts(0)
            attention()
            experts(1)


        @block.scalar
        def _(act):
            def ring(*key):
                act.wait_ge(ring_ps, RING[key] + 1)
                return ring_bank[RING[key] % 2][:, :]

            def turn(n, s, src):
                dst_ = xT[:, turn_no(n, s) % 2, :]
                if n in (LNM1, LNM2):
                    if s >= 2:
                        act.wait_ge(xl_ready, (n == LNM2) * SEQ + s - 1)
                    nc.scalar.activation(dst_, src, ACT.Copy)
                    return nc.scalar.activation(xh[:, s * L:(s + 1) * L], src, ACT.Copy)
                if n == LNC:
                    act.wait_ge(xl_ready, SEQ)
                    return nc.scalar.activation(dst_, src, ACT.Copy)
                return nc.scalar.activation(dst_, src, ACT.Identity, bias=lnb[:, n - 1:n], scale=lng[:, n - 1:n])

            def first_part(c, which, src):
                if c >= 1 and which == 0:
                    act.wait_ge(parts_out, 3 * 16 * c)
                    act.wait_ge(qt_sb, c)
                    act.wait_ge(qg_sb, min(c, A))
                for o in (qkf[:, which, :], qkp[:, 0, which, :]):
                    if c < A:
                        ins = nc.scalar.activation(o, src, ACT.Identity, bias=proj_bc[:, c // SEQ, which:which + 1])
                    else:
                        ins = nc.scalar.activation(o, src, ACT.Copy)
                return ins

            def second_part(c):
                act.wait_ge(qt_sb, c + 1)
                nc.scalar.activation(qkp[:, 1, :, :], qkt_ret if c < A else qkt_att, ACT.Copy).then_inc(q2_sb, 1)

            def turn_queries_keys(c):
                key = front_key("turn", c)
                turn(key[1], key[2], ring(*key)).then_inc(ring_sb, 1)
                first_part(c, 0, ring("q", c)).then_inc(ring_sb, 1)
                first_part(c, 1, ring("k", c)).then_inc(ring_sb, 1)

            def front(c):
                turn_queries_keys(c)
                if c >= A:
                    values(c - A, ring("v", c - A)).then_inc(ring_sb, 1)
                else:
                    second_part(c)

            def values(s, src):
                if s >= 2:
                    act.wait_ge(va_sb, s - 1)
                return nc.scalar.activation(vs[:, s % 2, :], src, ACT.Copy)

            def plain_turn(n, s):
                turn(n, s, ring("turn", n, s)).then_inc(ring_sb, 1)

            def logits(m, s):
                plain_turn((LNM1, LNM2)[m], s)
                keep_logits(m, s)

            def keep_logits(m, s):
                c = m * SEQ + s
                src = ring("router", m, s)
                if c >= 1:
                    act.wait_ge(routed, c)
                nc.scalar.activation(lg[:, :, :].rearrange("p k e -> p (k e)"), src[:, 0:TPS * E],
                                     ACT.Copy).then_inc(ring_sb, 1)

            def exp_logits(m, s):
                act.wait_ge(lg_d, m * SEQ + s + 1)
                nc.scalar.activation(lge[:, :, :], lgd[:, :, :], ACT.Exp).then_inc(lg_e, 1)

            def normalize(n, s):
                act.wait_ge(nrm_sb, BY_ACT.index(n) * SEQ + s + 1)
                src = X if n in (LNC, LNM2) else R
                for k in range(TPS):
                    t = TPS * s + k
                    ins = nc.scalar.activation(xn[:, t, :], src[:, t, :], ACT.Identity, bias=nrm[:, 3, k:k + 1],
                                               scale=nrm[:, 1, k:k + 1])
                ins.then_inc(xn_act, 1)

            def retention(layer):
                for s in range(SEQ):
                    c = layer * SEQ + s
                    if s + 1 < SEQ:
                        front(c + 1)
                    else:
                        plain_turn(2 + 2 * layer, 0)
                    nc.scalar.activation(sxT[:, c % 2, :], ring("xo", layer, s), ACT.Silu,
                                         bias=proj_bc[:, layer, 3:4]).then_inc(ring_sb, 1)
                    if s >= 1:
                        normalize(2 + 2 * layer, s - 1)

            def feed_forward(layer):
                for s in range(SEQ):
                    b = layer * SEQ + s
                    for f in range(FB):
                        act.wait_ge(f1_ps, b * FB + f + 1)
                        if f == 0 and b >= 2:
                            act.wait_ge(f2_ps, b - 1)
                        src = (PA, PB)[f // 2][:, f % 2, :]
                        nc.scalar.activation(hT[:, b % 2, f, :], src, ACT.Gelu,
                                             bias=ffn1_b[:, layer, f:f + 1]).then_inc(f1_sb, 1)
                    if s + 1 < SEQ:
                        plain_turn(2 + 2 * layer, s + 1)
                        if s == 0:
                            normalize(2 + 2 * layer, SEQ - 1)
                    if s == SEQ - 2 and layer + 1 < LAYERS:
                        turn_queries_keys((layer + 1) * SEQ)
                    if s == SEQ - 1 and layer + 1 < LAYERS:
                        second_part((layer + 1) * SEQ)
                    if s == SEQ - 1 and layer + 1 == LAYERS:
                        logits(0, 0)

            def experts(m):
                for e in range(E):
                    for s in range(SEQ):
                        for f in range(FB):
                            g = ((m * E + e) * SEQ + s) * FB + f
                            act.wait_ge(m1a_ps, g + 1)
                            if g >= 2:
                                act.wait_ge(m1_sb, g - 1)
                            nc.scalar.activation(silu_a[:, g % 2, :], PA[:, g % 2, :], ACT.Silu).then_inc(m1_si, 1)
                            if e == 0 and s + 1 < SEQ and f == 1:
                                plain_turn((LNM1, LNM2)[m], s + 1)
                            if e == 0 and s + 1 < SEQ and f == 2:
                                keep_logits(m, s + 1)
                            if (m, e, s, f) == (1, 0, 0, FB - 1):
                                normalize(LNM2, SEQ - 1)
                            if (m, e) == (0, E - 1) and s >= 2:
                                if f == 0 and s == 3:
                                    second_part(A)
                                if f == 2:
                                    normalize(LNC, s - 2)
                                if f == 3:
                                    front(A + s - 2)
                        if e == 0:
                            exp_logits(m, s)
                if m == 0:
                    second_part(A + 1)
                    normalize(LNC, SEQ - 2)
                    normalize(LNC, SEQ - 1)

            def attention():
                def run(uses):
                    for use in uses:
                        what, s = use[:2]
                        if what in ("max", "tr", "wo"):
                            continue
                        n = PAIR[use]
                        act.wait_ge(pair_ps, n + 1)
                        src = PA[:, n % 2, :]
                        if what == "mx":
                            if s >= 1:
                                act.wait_ge(max_out, 16 * s)
                            ins = nc.scalar.activation(mxT, src[0:NP3 * HG, :], ACT.Copy)
                        if what == "turn":
                            ins = turn(LNC, s, src)
                        if what == "q":
                            ins = first_part(A + s, 0, src)
                        if what == "k":
                            ins = first_part(A + s, 1, src)
                        if what == "v":
                            ins = values(s, src)
                        if what == "ao":
                            ins = nc.scalar.activation(aoT, src, ACT.Copy)
                        ins.then_inc(pair_sb[n % 2], 1)
                        if what == "v":
                            second_part(A + s)

                def weighted_out(s, b):
                    act.wait_ge(av_ps, NV * s + HV * (b + 1))
                    if s >= 1:
                        act.wait_ge(pair_ps, PAIR[("tr", s - 1, b)] + 1)
                    nc.scalar.activation(aor[:, b, :], (P6, P7)[b][:, :], ACT.Copy).then_inc(ao_raw, 1)

                def exps(s, v):
                    u = NV * s + v
                    j, _ = exp_unit(v)
                    act.wait_ge(ex_ps, u + 1)
                    if u >= 4:
                        act.wait_ge(av_ps, u - 3)
                    w = (TPS - j) * P
                    nc.scalar.activation(pt[:, u % 4, :, 0:w], (PB, PC)[u % 2][:, :, 0:w], ACT.Exp,
                                         scale=SCALE).then_inc(ex_sb, 1)

                run(LEAD_USES)
                for s in range(SEQ):
                    for v in range(NV):
                        exps(s, v)
                        run(slot_uses(s, v))
                        if v == LAG - 1 and s >= 1:
                            weighted_out(s - 1, 1)
                        if v == HV + LAG - 1:
                            weighted_out(s, 0)
                        if v == HV - 4 and s >= 1:
                            normalize(LNM2, s - 1)
                weighted_out(SEQ - 1, 1)
                plain_turn(LNM2, 0)
                run(LAST_USES)
                keep_logits(1, 0)

            act.wait_ge(in_const, 16)
            act.wait_ge(in_ret, in_ret_n)
            front(0)
            for layer in range(LAYERS):
                retention(layer)
                feed_forward(layer)
            experts(0)
            attention()
            experts(1)

        @block.tensor
        def _(pe):
            mm = nc.tensor.matmul

            def ring(*key):
                k = RING[key]
                if k >= 2:
                    pe.wait_ge(ring_sb, k - 1)
                return ring_bank[k % 2][:, :]

            def pair(*key):
                n = PAIR[key]
                if n >= 2:
                    pe.wait_ge(pair_sb[n % 2], n // 2)
                return PA[:, n % 2, :]

            def turns(n, s, bank):
                if n in BY_ACT:
                    pe.wait_ge(xn_act, BY_ACT.index(n) * SEQ + s + 1)
                else:
                    pe.wait_ge(xn_ready, BY_DVE.index(n) * SEQ + s + 1)
                for k in range(TPS):
                    ins = nc.tensor.transpose(bank[:, k * P:(k + 1) * P], xn[:, TPS * s + k, :], ident)
                return ins

            def plain_turn(n, s):
                turns(n, s, ring("turn", n, s)).then_inc(ring_ps, 1)

            def channels(c, what, bank):
                wait_front(pe, "turn", c)
                col = "qk".index(what)
                w = proj_w[:, c // SEQ, col * D:(col + 1) * D] if c < A else wqkv[:, col, :]
                return mm(bank, w, xT[:, turn_no(*front_key("turn", c)[1:]) % 2, :], start=True, stop=True)

            def token_values(s, bank):
                wait_front(pe, "turn", A + s)
                x = xT[:, turn_no(LNC, s) % 2, :]
                for k in range(TPS):
                    ins = mm(bank[:, k * P:(k + 1) * P], x[:, k * P:(k + 1) * P], wqkv[:, 2, :], start=True,
                             stop=True)
                return ins

            def front(c):
                plain_turn(*front_key("turn", c)[1:])
                queries_keys(c)

            def queries_keys(c):
                channels(c, "q", ring("q", c)).then_inc(ring_ps, 1)
                channels(c, "k", ring("k", c)).then_inc(ring_ps, 1)
                if c >= A:
                    token_values(c - A, ring("v", c - A)).then_inc(ring_ps, 1)

            def route(m, s):
                plain_turn((LNM1, LNM2)[m], s)
                router(m, s)

            def router(m, s):
                n = (LNM1, LNM2)[m]
                bank = ring("router", m, s)
                wait_ring(pe, "turn", n, s)
                for k in range(TPS):
                    ins = mm(bank[:, k * E:(k + 1) * E], xT[:, turn_no(n, s) % 2, k * P:(k + 1) * P], gate_w[:, :],
                             start=True, stop=True)
                ins.then_inc(ring_ps, 1)

            def retention(layer):
                def tile_x(t):
                    k = t % TPS
                    return xT[:, turn_no(1 + 2 * layer, t // TPS) % 2, k * P:(k + 1) * P]

                def gate_input(s):
                    x = xT[:, turn_no(1 + 2 * layer, s) % 2, :]
                    mm(ring("xo", layer, s), proj_w[:, layer, 3 * D:4 * D], x, start=True,
                       stop=True).then_inc(ring_ps, 1)

                def keys_values(t):
                    g = layer * NT + t
                    if g >= 1:
                        pe.wait_ge(kv_sb, g)
                    if t >= 3:
                        pe.wait_ge(ro_up, g - 2)
                    mm(PC[:, 0, 0:2 * D], tile_x(t), proj_w[:, layer, D:3 * D], start=True,
                       stop=True).then_inc(kv_ps, 1)

                def scores(t, u):
                    g = layer * NT + t
                    c = (g // TPS) % 2
                    pe.wait_ge(st_in[c], 7 * 16 * (g // TPS // 2 + 1))
                    if g >= 1:
                        pe.wait_ge(pm_sb, 2 * (g - 1) + u + 1)
                    for h in range(8 * u, 8 * u + 8):
                        k = h % 8
                        o = h * L + (t % TPS) * P
                        ins = mm((PA, PB)[u][:, k // 4, (k % 4) * P:(k % 4 + 1) * P], kst[:, c, o:o + P],
                                 qst[:, c, o:o + P], start=True, stop=True)
                    ins.then_inc(sc_ps, 1)

                def retain(t):
                    g = layer * NT + t
                    pe.wait_ge(pm_sb, 2 * g + 2)
                    pe.wait_ge(vp_sb, g + 1)
                    pe.wait_ge(kg_sb, g + 1)
                    if g >= 1:
                        pe.wait_ge(rg_sb, g)
                    first = t % TPS == 0
                    seen = (g // TPS) * (TPS - 1) + t % TPS
                    if seen:
                        pe.wait_ge(state_sb, seen)
                    if not first:
                        pe.wait_ge(qg_sb, g // TPS + 1)
                        mm(PC[:, 1, 0:P], state[:, (g - 1) % 2, :],
                           qgT[:, (g // TPS) % 2, (t % TPS) * P:(t % TPS + 1) * P], start=True, stop=False,
                           skip_group_check=True)
                    for h in range(H):
                        a, k = divmod(h, HG)
                        ins = mm(PC[32 * a:32 * a + 32, 1, 0:P], vp[:, g % 2, a, 32 * k:32 * k + 32],
                                 pm[:, 2 * (g % 2) + h // 8, (h % 8) * P:(h % 8 + 1) * P],
                                 start=first and k == 0, stop=k == HG - 1, skip_group_check=True)
                    if t % TPS < TPS - 1:
                        ins = mm(PC[:, 1, P:2 * P], kg[:, g % 2, :], kvb[:, g % 2, D:2 * D], start=True, stop=True,
                                 skip_group_check=True)
                    ins.then_inc(re_ps, 1)

                def project_out(t):
                    g = layer * NT + t
                    pe.wait_ge(rg_sb, g + 1)
                    pe.wait_ge(kv_sb, layer * NT + min(t + 3, NT))
                    if g >= 1:
                        pe.wait_ge(ro_up, g)
                    o = PC[:, 0, 2 * D:3 * D]
                    mm(o, rgT[:, g % 2, :], reto_w[:, layer, :], start=True, stop=False)
                    mm(o, ones_row, reto_b[:, layer, :], start=False, stop=True).then_inc(ro_ps, 1)

                def ahead_turn(s):
                    if s + 1 < SEQ:
                        plain_turn(1 + 2 * layer, s + 1)
                    else:
                        plain_turn(2 + 2 * layer, 0)

                def ahead(s):
                    if s + 1 < SEQ:
                        queries_keys(layer * SEQ + s + 1)

                ahead_turn(0)
                ahead(0)
                for t in range(NT + 2):
                    if t < NT:
                        keys_values(t)
                        scores(t, 0)
                        if t % TPS == 0:
                            gate_input(t // TPS)
                    if t >= 2:
                        project_out(t - 2)
                    if t < NT:
                        scores(t, 1)
                    last = t % TPS == TPS - 1 and t + 1 < NT
                    if last:
                        ahead_turn(t // TPS + 1)
                    if 1 <= t < NT + 1:
                        retain(t - 1)
                    if last:
                        ahead(t // TPS + 1)

            def feed_forward(layer):
                def up(s):
                    wait_ring(pe, "turn", 2 + 2 * layer, s)
                    x = xT[:, turn_no(2 + 2 * layer, s) % 2, :]
                    for f in range(FB):
                        g = (layer * SEQ + s) * FB + f
                        if g >= 4:
                            pe.wait_ge(f1_sb, g - 3)
                        mm((PA, PB)[f // 2][:, f % 2, :], ffn1_w[:, layer, f * P:(f + 1) * P], x, start=True,
                           stop=True).then_inc(f1_ps, 1)

                def down(s):
                    b = layer * SEQ + s
                    pe.wait_ge(f1_sb, (b + 1) * FB)
                    if b >= 2:
                        pe.wait_ge(f2_up, b - 1)
                    for k in range(TPS):
                        bank = PC[:, b % 2, k * D:(k + 1) * D]
                        for f in range(FB):
                            mm(bank, hT[:, b % 2, f, k * P:(k + 1) * P], ffn2_w[:, layer, f, :], start=f == 0,
                               stop=False)
                        ins = mm(bank, ones_row, ffn2_b[:, layer, :], start=False, stop=True)
                    ins.then_inc(f2_ps, 1)

                pe.wait_ge(pm_sb, 2 * NT * (layer + 1))
                pe.wait_ge(ro_up, NT * (layer + 1))
                up(0)
                for s in range(SEQ):
                    if s + 1 < SEQ:
                        plain_turn(2 + 2 * layer, s + 1)
                        up(s + 1)
                    if s == SEQ - 2 and layer + 1 < LAYERS:
                        front((layer + 1) * SEQ)
                    down(s)
                if layer + 1 == LAYERS:
                    route(0, 0)
                pe.wait_ge(f1_sb, SEQ * FB * (layer + 1))
                if layer + 1 < LAYERS:
                    pe.wait_ge(f2_up, SEQ * (layer + 1))

            def experts(m):
                def down(e, s):
                    n = m * E + e
                    b = n * SEQ + s
                    pe.wait_ge(in_w2[n % 2], 16 * (n // 2 + 1))
                    pe.wait_ge(m1_sb, (b + 1) * FB)
                    if b == 0:
                        pe.wait_ge(f2_up, LAYERS * SEQ)
                    if b >= 2:
                        pe.wait_ge(m2_up, b - 1)
                    for k in range(TPS):
                        for f in range(FB):
                            ins = mm(PC[:, b % 2, k * D:(k + 1) * D], hT[:, b % 2, f, k * P:(k + 1) * P],
                                     w2[n % 2][:, f, :], start=f == 0, stop=f == FB - 1)
                    ins.then_inc(m2_ps, 1)

                prev = None
                for e in range(E):
                    n = m * E + e
                    pe.wait_ge(w_hi, n + 1)
                    pe.wait_ge(w_lo, n + 1)
                    for s in range(SEQ):
                        if e == 0:
                            wait_ring(pe, "turn", (LNM1, LNM2)[m], s)
                            pe.wait_ge(xl_ready, m * SEQ + s + 1)
                        x = slice(s * L, (s + 1) * L)
                        for f in range(FB):
                            g = (n * SEQ + s) * FB + f
                            c = slice(f * P, (f + 1) * P)
                            for k, (bank, read, done) in enumerate(((PA, m1_si, m1a_ps), (PB, m1_sb, m1_ps))):
                                if g >= 2:
                                    pe.wait_ge(read, g - 1)
                                mm(bank[:, g % 2, :], w13h[:, n % 2, k, c], xh[:, x], start=True, stop=False)
                                mm(bank[:, g % 2, :], w13h[:, n % 2, k, c], xl[:, x], start=False, stop=False)
                                ins = mm(bank[:, g % 2, :], w13l[:, n % 2, k, c], xh[:, x], start=False, stop=True)
                                ins.then_inc(done, 1)
                            if e == 0 and s + 1 < SEQ and f == 1:
                                plain_turn((LNM1, LNM2)[m], s + 1)
                            if e == 0 and s + 1 < SEQ and f == 2:
                                router(m, s + 1)
                            if f == 1 and prev is not None:
                                down(*prev)
                            if (m, e, f) == (0, E - 1, FB - 1) and s >= 2:
                                if s == 2:
                                    pe.wait_ge(in_att, in_att_n)
                                front(A + s - 2)
                        prev = (e, s)
                down(*prev)
                pe.wait_ge(m1_sb, E * SEQ * FB * (m + 1))
                pe.wait_ge(m2_up, E * SEQ * (m + 1))

            def attention():
                def head(h, c, o, n):
                    return slice(h * L + o, h * L + o + n)

                def max_scores(g, n):
                    i, h = max_unit(g, n)
                    s = g // NG
                    bank = pair("max", g, n)
                    pe.wait_ge(st_in[s % 2], 7 * 16 * ((A + s) // 2 + 1))
                    w = (i + 1) * P
                    mm(bank[:, i * P:w], idb[:, :], mqb[:, :], start=True, stop=False, skip_group_check=True)
                    o = h * L
                    mm(bank[:, 0:w], qst[:, s % 2, o + i * P:o + w], kst[:, s % 2, o:o + w],
                       start=False, stop=True, skip_group_check=True).then_inc(pair_ps, 1)

                def turn_max(g):
                    bank = pair("mx", g)
                    pe.wait_ge(mx_sb, g + 1)
                    for i in range(TPS):
                        ins = nc.tensor.transpose(bank[0:NP3 * HG, i * P:(i + 1) * P], mxf[:, i, :], ident)
                    ins.then_inc(pair_ps, 1)

                def exp_scores(s, v):
                    j, p = exp_unit(v)
                    u = NV * s + v
                    if v % GV == 0:
                        pe.wait_ge(max_in, 16 * (u // GV + 1))
                    if u >= 2:
                        pe.wait_ge(ex_sb, u - 1)
                    w = (TPS - j) * P
                    bank = (PB, PC)[u % 2]
                    for k in range(2):
                        mm(bank[:, k, 0:P], idb[:, :], mkb[:, :], start=True, stop=False, skip_group_check=True)
                    for k in range(2):
                        o = (2 * p + k) * L + j * P
                        ins = mm(bank[:, k, 0:w], kst[:, s % 2, o:o + P], qst[:, s % 2, o:o + w],
                                 start=False, stop=True, skip_group_check=True)
                    ins.then_inc(ex_ps, 1)

                def weighted(u):
                    s, v = divmod(u, NV)
                    j, p = exp_unit(v)
                    pe.wait_ge(ex_sb, u + 1)
                    if v % HV == 0:
                        b = v // HV
                        pe.wait_ge(va_sb, 2 * s + b + 1)
                        if s >= 1:
                            pe.wait_ge(ao_raw, 2 * (s - 1) + b + 1)
                    for k in range(2):
                        h = 2 * p + k
                        a, g = divmod(h, HG)
                        r = 64 * (a % 2)
                        ins = mm((P6, P7)[a // 2][r:r + 64, j * P:L], va[:, j, a, 64 * g:64 * g + 64],
                                 pt[:, u % 4, k, 0:(TPS - j) * P], start=j == 0 and g == 0, stop=True,
                                 skip_group_check=True)
                    ins.then_inc(av_ps, 1)

                def turn_weighted(s, b):
                    bank = pair("tr", s, b)
                    pe.wait_ge(ao_raw, 2 * s + b + 1)
                    for i in range(TPS):
                        ins = nc.tensor.transpose(bank[:, i * P:(i + 1) * P], aor[:, b, i * P:(i + 1) * P], ident)
                    ins.then_inc(pair_ps, 1)

                def turn_out(s):
                    bank = pair("ao", s)
                    wait_pair(pe, "tr", s, 0)
                    wait_pair(pe, "tr", s, 1)
                    for i in range(TPS):
                        ins = nc.tensor.transpose(bank[:, i * P:(i + 1) * P], xn[:, TPS * s + i, :], ident)
                    ins.then_inc(pair_ps, 1)

                def project(s):
                    bank = pair("wo", s)
                    wait_pair(pe, "ao", s)
                    for i in range(TPS):
                        o = bank[:, i * D:(i + 1) * D]
                        mm(o, aoT[:, i * P:(i + 1) * P], wo, start=True, stop=False)
                        ins = mm(o, ones_row, bo[:, :], start=False, stop=True)
                    ins.then_inc(pair_ps, 1)

                def run(uses):
                    for what, *key in uses:
                        if what == "max":
                            max_scores(*key)
                        if what == "mx":
                            turn_max(*key)
                        if what == "tr":
                            turn_weighted(*key)
                        if what == "ao":
                            turn_out(*key)
                        if what == "wo":
                            project(*key)
                        if what == "turn":
                            turns(LNC, key[0], pair("turn", *key)).then_inc(pair_ps, 1)
                        if what in "qk":
                            channels(A + key[0], what, pair(what, *key)).then_inc(pair_ps, 1)
                        if what == "v":
                            token_values(key[0], pair("v", *key)).then_inc(pair_ps, 1)

                pe.wait_ge(att_const, 1)
                run(LEAD_USES)
                wait_ring(pe, "v", 1)
                for s in range(SEQ):
                    for v in range(NV):
                        uses = slot_uses(s, v)
                        run(uses[0:1])
                        exp_scores(s, v)
                        run(uses[1:])
                        if NV * s + v >= LAG:
                            weighted(NV * s + v - LAG)
                for u in range(NV * SEQ - LAG, NV * SEQ):
                    weighted(u)
                run(LAST_USES[0:1])
                plain_turn(LNM2, 0)
                run(LAST_USES[1:2])
                router(1, 0)
                run(LAST_USES[2:])
                pe.wait_ge(ex_sb, NV * SEQ)
                for n in (len(PAIR) - 2, len(PAIR) - 1):
                    pe.wait_ge(pair_sb[n % 2], n // 2 + 1)

            pe.wait_ge(in_const, 16)
            pe.wait_ge(in_ret, in_ret_n)
            front(0)
            pe.wait_ge(in_ffn, in_ffn_n)
            pe.wait_ge(stack_fill, 4 * 16)
            for layer in range(LAYERS):
                retention(layer)
                feed_forward(layer)
            experts(0)
            attention()
            experts(1)


def kernel(**inputs):
    import concourse.bacc as bacc
    from concourse.bass_utils import run_bass_kernel_spmd

    a = {k: np.asarray(v) for k, v in inputs.items()}
    const, decay = constants()
    ln = lambda s: np.ascontiguousarray(np.stack(
        [a[f"L0_attn_a_ln{1 + j}_{s}"][layer] for layer in range(LAYERS) for j in range(2)], axis=1))
    order = np.arange(D).reshape(H, HD).T.reshape(-1)
    columns = np.concatenate([order, D + order, np.arange(2 * D, 4 * D)])
    proj_w = a["L0_attn_a_proj_w"][:, :, columns]
    proj_b = a["L0_attn_a_proj_b"][:, columns]
    heads = lambda w: w.transpose(1, 0, 2).reshape(D, D)
    turned = lambda w: w.transpose(1, 2, 0).reshape(D, D)
    arrays = {
        "x": a["L0_attn_a_x"].reshape(NT * P, D),
        "const": const,
        "decay": decay,
        "proj_w": proj_w,
        "proj_bc": proj_b.reshape(LAYERS * 4, D).T,
        "kv_b": proj_b[:, D:3 * D],
        "reto_w": a["L0_attn_a_reto_w"],
        "reto_b": a["L0_attn_a_reto_b"],
        "lng": ln("g"),
        "lnb": ln("b"),
        "lnf": np.stack([a["L0_attn_a_lnf_g"], a["L0_attn_a_lnf_b"]]),
        "ffn1_w": a["L0_attn_a_ffn1_w"],
        "ffn1_b": a["L0_attn_a_ffn1_b"].reshape(LAYERS * FB, P).T,
        "ffn2_w": a["L0_attn_a_ffn2_w"],
        "ffn2_b": a["L0_attn_a_ffn2_b"],
        "wqkv": np.stack([turned(a["L0_attn_b_Wq"]), turned(a["L0_attn_b_Wk"]), heads(a["L0_attn_b_Wv"])]),
        "wo": a["L0_attn_b_Wo"].T,
        "bo": a["L0_attn_b_bo"],
        "gate_w": a["L0_ffn_gate_w"],
        "w1": a["L0_ffn_w1"],
        "w3": a["L0_ffn_w3"],
        "w2": a["L0_ffn_w2"],
    }
    nc = bacc.Bacc("TRN2", target_bir_lowering=False, num_devices=1)
    feeds, args = {}, []
    for name, v in arrays.items():
        v = np.ascontiguousarray(v)
        feeds[f"in_{name}"] = v
        args.append(nc.dram_tensor(f"in_{name}", v.shape, mybir.dt.from_np(v.dtype), kind="ExternalInput").ap())
    out = nc.dram_tensor("out", (NT * P, D), F32, kind="ExternalOutput").ap()
    mixer_kernel(nc, *args, out)
    r = run_bass_kernel_spmd(nc, [feeds], core_ids=[0])
    return r.results[0]["out"].reshape(SEQ, L, D)
```
